# Optimizing a Trainium2 kernel written in Bass

```python
import numpy as np
import jax
import jax.numpy as jnp

def _softmax(x, axis=-1):
    return jax.nn.softmax(x, axis=axis)

def _gelu(x):
    return jax.nn.gelu(x, approximate=True)

def _silu(x):
    return jax.nn.silu(x)

def _sigmoid(x):
    return jax.nn.sigmoid(x)

def _layernorm(x, axis=-1, eps=1e-05):
    m = jnp.mean(x, axis=axis, keepdims=True)
    v = jnp.var(x, axis=axis, keepdims=True)
    return (x - m) / jnp.sqrt(v + eps)

def _scatter_add(tgt, idx, src, axis=0):
    return tgt.at[idx].add(src)

def _segment_sum(src, seg, n):
    return jax.ops.segment_sum(src, seg, n)
kernel_name = 'mk_decoder_preln_d1_seqx_r8_2ffd64'

def setup_inputs(seed: int=0):
    np.random.seed(seed)
    _w = jnp.asarray

    def _rec_inputs():
        import jax
        import jax.numpy as jnp
        _rk = jax.random.key(seed)
        x = 0.002226 + 0.9996 * jax.random.normal(jax.random.fold_in(_rk, 1), (8, 256, 128), jnp.float32)
        _lenS = 256 - jax.random.randint(jax.random.fold_in(_rk, 7), (8,), 0, max(1, 256 // 4) + 1, jnp.int32)
        _lenS2 = 512 - jax.random.randint(jax.random.fold_in(_rk, 8), (8,), 0, max(1, 512 // 4) + 1, jnp.int32)
        _ctx_1024P = jax.random.normal(jax.random.fold_in(_rk, 11), (8, 16, 128), jnp.float32)
        _ctx_1024c = jax.random.dirichlet(jax.random.fold_in(_rk, 511), 0.3 * jnp.ones((16,), jnp.float32), (8, 512))
        _ctx_1024t = jnp.einsum('bsk,bkd->bsd', _ctx_1024c, _ctx_1024P)
        _ctx_1024t = _ctx_1024t * jax.lax.rsqrt(jnp.mean(jnp.square(_ctx_1024t)) + 1e-12) * 0.953939
        ctx_1024 = -0.000125008 + 0.999885 * (_ctx_1024t + 0.3 * jax.random.normal(jax.random.fold_in(_rk, 611), (8, 512, 128), jnp.float32))
        return (x, ctx_1024)
    x, ctx_1024 = _rec_inputs()

    def _L0_attn_setup():
        import jax, jax.numpy as jnp
        import numpy as np
        LN_EPS = 1e-05
        key = jax.random.key(seed)
        ks = jax.random.split(key, 5)
        B, S, E, H = (4, 128, 128, 16)
        sd = E ** (-0.5)
        return {'x': jax.random.normal(ks[0], (B, S, E), jnp.float32), 'Wq': jax.random.normal(ks[1], (E, E), jnp.float32) * sd, 'Wk': jax.random.normal(ks[2], (E, E), jnp.float32) * sd, 'Wv': jax.random.normal(ks[3], (E, E), jnp.float32) * sd, 'bias_table': jax.random.normal(ks[4], (2 * S - 1, H), jnp.float32) * 0.02, 'ln_gamma': jnp.ones((E,), jnp.float32), 'ln_beta': jnp.zeros((E,), jnp.float32)}
    _L0_attn_all = _L0_attn_setup()
    _L0_attn_in = {k: v for k, v in _L0_attn_all.items() if k in ('Wq', 'Wk', 'Wv', 'bias_table', 'ln_gamma', 'ln_beta')}
    del _L0_attn_all

    def _L0_xattn_setup():
        import jax, jax.numpy as jnp
        import numpy as np
        EPS = 1e-05

        def layer_norm(x, g, b):
            mu = jnp.mean(x, axis=-1, keepdims=True)
            var = jnp.var(x, axis=-1, keepdims=True)
            return (x - mu) * jax.lax.rsqrt(var + EPS) * g + b
        key = jax.random.key(seed)
        ks = jax.random.split(key, 8)
        dim, heads, dim_head = (128, 16, 64)
        inner = heads * dim_head
        b, n, m = (8, 512, 64)
        s = dim ** (-0.5)
        return {'x': jax.random.normal(ks[0], (b, n, dim), jnp.float32), 'latents': jax.random.normal(ks[1], (b, m, dim), jnp.float32), 'ln_m_g': jnp.ones((dim,), jnp.float32), 'ln_m_b': jnp.zeros((dim,), jnp.float32), 'ln_l_g': jnp.ones((dim,), jnp.float32), 'ln_l_b': jnp.zeros((dim,), jnp.float32), 'Wq': jax.random.normal(ks[2], (dim, inner), jnp.float32) * s, 'Wkv': jax.random.normal(ks[3], (dim, 2 * inner), jnp.float32) * s, 'Wout': jax.random.normal(ks[4], (inner, dim), jnp.float32) * s}
    _L0_xattn_all = _L0_xattn_setup()
    _L0_xattn_in = {k: v for k, v in _L0_xattn_all.items() if k in ('ln_m_g', 'ln_m_b', 'ln_l_g', 'ln_l_b', 'Wq', 'Wkv', 'Wout')}
    del _L0_xattn_all

    def _L0_ffn_setup():
        import jax, jax.numpy as jnp
        import numpy as np
        B, C, D = (2, 256, 128)
        I = 256
        E, K = (8, 2)
        CF = 1.25
        key = jax.random.key(seed)
        k1, k2, k3, k4 = jax.random.split(key, 4)
        scale = 0.02
        return {'hidden_states': jax.random.normal(k1, (B, C, D), jnp.float32), 'Wg': jax.random.normal(k2, (E, D), jnp.float32) * scale, 'W1': jax.random.normal(k3, (E, D, 2 * I), jnp.float32) * scale, 'W2': jax.random.normal(k4, (E, I, D), jnp.float32) * scale}
    _L0_ffn_all = _L0_ffn_setup()
    _L0_ffn_in = {k: v for k, v in _L0_ffn_all.items() if k in ('Wg', 'W1', 'W2')}
    del _L0_ffn_all
    return {'x': x, 'ctx_1024': ctx_1024, 'L0_attn_Wq': _L0_attn_in['Wq'], 'L0_attn_Wk': _L0_attn_in['Wk'], 'L0_attn_Wv': _L0_attn_in['Wv'], 'L0_attn_bias_table': _L0_attn_in['bias_table'], 'L0_attn_ln_gamma': _L0_attn_in['ln_gamma'], 'L0_attn_ln_beta': _L0_attn_in['ln_beta'], 'L0_xattn_ln_m_g': _L0_xattn_in['ln_m_g'], 'L0_xattn_ln_m_b': _L0_xattn_in['ln_m_b'], 'L0_xattn_ln_l_g': _L0_xattn_in['ln_l_g'], 'L0_xattn_ln_l_b': _L0_xattn_in['ln_l_b'], 'L0_xattn_Wq': _L0_xattn_in['Wq'], 'L0_xattn_Wkv': _L0_xattn_in['Wkv'], 'L0_xattn_Wout': _L0_xattn_in['Wout'], 'L0_ffn_Wg': _L0_ffn_in['Wg'], 'L0_ffn_W1': _L0_ffn_in['W1'], 'L0_ffn_W2': _L0_ffn_in['W2']}

def reference(x, ctx_1024, L0_attn_Wq, L0_attn_Wk, L0_attn_Wv, L0_attn_bias_table, L0_attn_ln_gamma, L0_attn_ln_beta, L0_xattn_ln_m_g, L0_xattn_ln_m_b, L0_xattn_ln_l_g, L0_xattn_ln_l_b, L0_xattn_Wq, L0_xattn_Wkv, L0_xattn_Wout, L0_ffn_Wg, L0_ffn_W1, L0_ffn_W2):
    import jax
    import jax.numpy as jnp

    def _L0_attn_ref(x, Wq, Wk, Wv, bias_table, ln_gamma, ln_beta):
        import jax, jax.numpy as jnp
        import numpy as np
        LN_EPS = 1e-05
        B, S, E = x.shape
        H = bias_table.shape[1]
        d = E // H
        scale = E ** (-0.5)
        q = (x @ Wq.T).reshape(B, S, H, d).transpose(0, 2, 1, 3)
        k = (x @ Wk.T).reshape(B, S, H, d).transpose(0, 2, 1, 3)
        v = (x @ Wv.T).reshape(B, S, H, d).transpose(0, 2, 1, 3)
        attn = jax.nn.softmax(jnp.einsum('bhsd,bhtd->bhst', q, k) * scale, axis=-1)
        rel_idx = jnp.arange(S)[:, None] - jnp.arange(S)[None, :] + (S - 1)
        rel_bias = bias_table[rel_idx].transpose(2, 0, 1)
        attn = attn + rel_bias[None]
        out = jnp.einsum('bhst,bhtd->bhsd', attn, v)
        out = out.transpose(0, 2, 1, 3).reshape(B, S, E)
        mu = out.mean(-1, keepdims=True)
        var = out.var(-1, keepdims=True)
        out = (out - mu) * jax.lax.rsqrt(var + LN_EPS) * ln_gamma + ln_beta
        return out

    def _L0_xattn_ref(x, latents, ln_m_g, ln_m_b, ln_l_g, ln_l_b, Wq, Wkv, Wout):
        import jax, jax.numpy as jnp
        import numpy as np
        EPS = 1e-05

        def layer_norm(x, g, b):
            mu = jnp.mean(x, axis=-1, keepdims=True)
            var = jnp.var(x, axis=-1, keepdims=True)
            return (x - mu) * jax.lax.rsqrt(var + EPS) * g + b
        heads, dim_head = (16, 64)
        scale = dim_head ** (-0.5)
        x = layer_norm(x, ln_m_g, ln_m_b)
        lat = layer_norm(latents, ln_l_g, ln_l_b)
        b, m, _ = lat.shape
        q = lat @ Wq
        kv_input = jnp.concatenate([x, lat], axis=1)
        kv = kv_input @ Wkv
        k, v = jnp.split(kv, 2, axis=-1)

        def split_heads(t):
            return t.reshape(t.shape[0], t.shape[1], heads, dim_head).transpose(0, 2, 1, 3)
        q, k, v = (split_heads(q), split_heads(k), split_heads(v))
        dots = jnp.einsum('bhid,bhjd->bhij', q, k) * scale
        attn = jax.nn.softmax(dots, axis=-1)
        out = jnp.einsum('bhij,bhjd->bhid', attn, v)
        out = out.transpose(0, 2, 1, 3).reshape(b, m, heads * dim_head)
        return out @ Wout

    def _L0_ffn_ref(hidden_states, Wg, W1, W2):
        import jax, jax.numpy as jnp
        import numpy as np
        B, C, D = (2, 256, 128)
        I = 256
        E, K = (8, 2)
        CF = 1.25
        Bx, Cx, d = hidden_states.shape
        N = Bx * Cx
        cap = int(N * K * CF / E)
        x = hidden_states.reshape(N, d)
        logits = x @ Wg.T
        top_v, top_i = jax.lax.top_k(logits, K)
        gates = jax.nn.softmax(top_v, axis=-1)
        flat_e = top_i.reshape(N * K)
        gates_f = gates.reshape(N * K)
        tok = jnp.repeat(jnp.arange(N), K)
        onehot = jax.nn.one_hot(flat_e, E, dtype=jnp.int32)
        pos = jnp.cumsum(onehot, axis=0) - 1
        pos_f = jnp.take_along_axis(pos, flat_e[:, None], axis=1)[:, 0]
        keep = pos_f < cap
        pos_safe = jnp.where(keep, pos_f, cap)
        exp_batches = jnp.zeros((E, cap, d), x.dtype).at[flat_e, pos_safe].set(x[tok], mode='drop')
        h = jnp.einsum('ecd,edf->ecf', exp_batches, W1)
        inp, gate = jnp.split(h, 2, axis=-1)
        h = jax.nn.gelu(inp, approximate=False) * gate
        exp_out = jnp.einsum('eci,eid->ecd', h, W2)
        gathered = exp_out[flat_e, jnp.minimum(pos_safe, cap - 1)]
        contrib = jnp.where(keep, gates_f, 0.0)[:, None] * gathered
        out = jax.ops.segment_sum(contrib, tok, num_segments=N)
        return out.reshape(Bx, Cx, d)
    x = x + _L0_attn_ref(_layernorm(x, axis=-1), L0_attn_Wq, L0_attn_Wk, L0_attn_Wv, L0_attn_bias_table, L0_attn_ln_gamma, L0_attn_ln_beta)
    x = x + _L0_xattn_ref(ctx_1024, _layernorm(x, axis=-1), L0_xattn_ln_m_g, L0_xattn_ln_m_b, L0_xattn_ln_l_g, L0_xattn_ln_l_b, L0_xattn_Wq, L0_xattn_Wkv, L0_xattn_Wout)
    x = x + _L0_ffn_ref(_layernorm(x, axis=-1), L0_ffn_Wg, L0_ffn_W1, L0_ffn_W2)
    return x

_drawn_inputs = setup_inputs


def setup_inputs(seed=0):
    import zlib

    import numpy as np

    out = dict(_drawn_inputs(seed))
    spreads = {'L0_attn_ln_gamma': (1.0, 0.2),
     'L0_attn_ln_beta': (0.0, 0.1),
     'L0_xattn_ln_m_g': (1.0, 0.2),
     'L0_xattn_ln_m_b': (0.0, 0.1),
     'L0_xattn_ln_l_g': (1.0, 0.2),
     'L0_xattn_ln_l_b': (0.0, 0.1)}
    factors = {'L0_ffn_Wg': 8.0, 'L0_ffn_W1': 8.0, 'L0_ffn_W2': 8.0}
    for name, (base, spread) in spreads.items():
        noise = np.random.default_rng([zlib.crc32(name.encode()), seed]).standard_normal(out[name].shape)
        drawn = base * np.exp(spread * noise) if base else spread * noise
        out[name] = jnp.asarray(drawn.astype(out[name].dtype))
    for name, factor in factors.items():
        out[name] = (out[name] * factor).astype(out[name].dtype)
    return out
```

```python
from contextlib import ExitStack

import concourse.bass as bass
import concourse.mybir as mybir
from concourse.alu_op_type import AluOpType as ALU

F32 = mybir.dt.float32
U32 = mybir.dt.uint32
ACT = mybir.ActivationFunctionType
AX = mybir.AxisListType

P = 128
B, S, E = 8, 256, 128
C = 512
H = 16
D_SELF = E // H
D_CROSS = 64
EPS = 1e-5
QT = S // P
NT = B * QT
KC = C // P
L = C + S
KT = L // P
HALF = L // 2
PAIRS = H // 2
G = H // 4
N_EXP, TOP, I_FF = 8, 2, 256
N_TOK = B * S
CAP = int(N_TOK * TOP * 1.25 / N_EXP)


def wait(engine, sem, value):
    if isinstance(value, int) and value <= 0:
        return
    engine.wait_ge(sem, value)


def build(nc, x_in, ctx_in, wq_s, wk_s, wv_s, line_in, ln_rows, ln_cols, wq_c, wk_c, wv_c, wo_c, wg, w1, w2, out):
    es = ExitStack()
    with es:
        def sb(name, shape, dt=F32):
            return es.enter_context(nc.sbuf_tensor(name, shape, dt))

        def sem(name):
            return es.enter_context(nc.semaphore(name))

        x_all = sb("x_all", [P, NT, E])
        kvT = sb("kvT", [P, B, L])
        o_all = sb("o_all", [P, NT, E])
        xnT_all = sb("xnT_all", [P, N_TOK])
        bias = sb("bias", [P, QT, H, S])
        mt_all = sb("mt_all", [P, H, E])
        wv_all = sb("wv_all", [P, H * D_CROSS])
        wo_all = sb("wo_all", [P, PAIRS, E])
        wq_sb = sb("wq_sb", [P, E])
        wk_sb = sb("wk_sb", [P, E])
        wv_sb = sb("wv_sb", [P, 4 * P])
        ident = sb("ident", [P, P])
        head_mask = sb("head_mask", [P, H])
        gb_rows = sb("gb_rows", [P, 2, E])
        gb_cols = sb("gb_cols", [P, 4])
        stats = sb("stats", [P, B * KC, 6])
        mv = sb("mv", [P, B * KC, 2])
        rstd = sb("rstd", [P, B * KC, 1])
        half_neg = sb("half_neg", [P, B * KC, 1])
        nmax = sb("nmax", [P, 4, 4])
        rsum = sb("rsum", [P, 4, 4])
        rinv = sb("rinv", [P, 4, 4])
        probs = sb("probs", [P, 4, 4 * S])
        probsT = sb("probsT", [P, 2, 2 * KT * S])
        avT = sb("avT", [P, 2, S])

        score = es.enter_context(nc.psum_tensor("score", [P, 2, 1024], F32))
        tr_a = es.enter_context(nc.psum_tensor("tr_a", [P, 512], F32))
        tr_b = es.enter_context(nc.psum_tensor("tr_b", [P, 512], F32))
        av = es.enter_context(nc.psum_tensor("av", [P, 512], F32))
        misc = es.enter_context(nc.psum_tensor("misc", [P, 512], F32))

        prepare(nc, es, sb, sem, locals())
        self_attention(nc, sb, sem, locals())
        latents(nc, sb, sem, locals())
        cross_attention(nc, sb, sem, locals())
        experts(nc, sb, sem, locals())


def prepare(nc, es, sb, sem, v):
    x_all, kvT, bias, mt_all, ident, misc, score = (v[k] for k in ("x_all", "kvT", "bias", "mt_all", "ident", "misc", "score"))
    stats, mv, rstd, half_neg, xnT_all = (v[k] for k in ("stats", "mv", "rstd", "half_neg", "xnT_all"))
    head_mask, gb_cols, gb_rows = v["head_mask"], v["gb_cols"], v["gb_rows"]
    with ExitStack() as own:
        def tmp(name, shape):
            return own.enter_context(nc.sbuf_tensor(name, shape, F32))
        ctx_sb = tmp("ctx_sb", [P, B * KC, E])
        xn = tmp("xn", [P, NT, E])
        wq_c_sb = tmp("wq_c_sb", [P, PAIRS, E])
        wk_c_sb = tmp("wk_c_sb", [P, PAIRS, E])
        line = tmp("line", [H, 2 * S])
        line_dram = nc.dram_tensor("line_dram", (H, P, 2 * S), F32)
        x_loaded, ctx_loaded, wc_loaded, w_loaded = sem("x_loaded"), sem("ctx_loaded"), sem("wc_loaded"), sem("w_loaded")
        line_loaded, line_made, line_stored, bias_loaded = sem("line_loaded"), sem("line_made"), sem("line_stored"), sem("bias_loaded")
        consts, vec, var_ready, rstd_ready = sem("consts"), sem("p_vec"), sem("p_var_ready"), sem("p_rstd_ready")
        x_normed, xt_done, xt_free, wv_cleared = sem("x_normed"), sem("xt_done"), sem("xt_free"), sem("wv_cleared")
        ctx_normed, mt_done, tr_done, tr_free = sem("ctx_normed"), sem("mt_done"), sem("p_tr_done"), sem("p_tr_free")
        block = own.enter_context(nc.Block())

        @block.sync
        def _(sp):
            sp.dma_start(x_all[:], v["x_in"].rearrange("(t p) e -> p t e", p=P)).then_inc(x_loaded, 16)
            sp.dma_start(line[:, S:2 * S - 1], v["line_in"]).then_inc(line_loaded, 16)
            sp.dma_start(ctx_sb[:], v["ctx_in"].rearrange("(t p) e -> p t e", p=P)).then_inc(ctx_loaded, 16)
            sp.wait_ge(line_made, 2)
            sp.dma_start(line_dram.ap(), line[:].rearrange("h (o k) -> h o k", o=1).to_broadcast([H, P, 2 * S])).then_inc(line_stored, 16)
            sp.wait_ge(line_stored, 16)
            for qt in range(QT):
                window = bass.AP(line_dram, S - 1 - qt * P, [[2 * S - 1, P], [2 * S * P, H], [1, S]])
                sp.dma_start(bias[:, qt], window).then_inc(bias_loaded, 16)
            sp.wait_ge(bias_loaded, 16 * QT)
            sp.wait_ge(w_loaded, 16 * 7)

        @block.gpsimd
        def _(pool):
            pool.memset(ident[:], 0.0).then_inc(consts, 1)
            pool.memset(head_mask[:], 1.0).then_inc(consts, 1)
            pool.memset(half_neg[:], -0.5).then_inc(consts, 1)
            pool.wait_ge(consts, 3)
            pool.affine_select(out=ident[:], in_=ident[:], compare_op=ALU.not_equal, fill=1.0,
                               base=0, pattern=[[-1, P]], channel_multiplier=1).then_inc(consts, 1)
            pool.affine_select(out=head_mask[:], in_=head_mask[:], compare_op=ALU.is_ge, fill=0.0,
                               base=0, pattern=[[-D_SELF, H]], channel_multiplier=1).then_inc(consts, 1)
            pool.wait_ge(consts, 5)
            pool.affine_select(out=head_mask[:], in_=head_mask[:], compare_op=ALU.is_ge, fill=0.0,
                               base=D_SELF - 1, pattern=[[D_SELF, H]], channel_multiplier=-1).then_inc(consts, 1)
            for k, n in enumerate((NT, B * KC)):
                pool.wait_ge(var_ready, k + 1)
                pool.tensor_scalar(rstd[:, 0:n, :], mv[:, 0:n, 1:2], EPS, 1.0, ALU.add, ALU.mult).then_inc(rstd_ready, 1)
                pool.wait_ge(rstd_ready, 2 * k + 1)
                pool.tensor_tensor(rstd[:, 0:n, :], rstd[:, 0:n, :], half_neg[:, 0:n, :], ALU.pow).then_inc(rstd_ready, 1)

        @block.vector
        def _(dve):
            count = [0]

            def link(ins, hold):
                count[0] += 1
                ins.then_inc(vec, 1)
                if hold:
                    dve.wait_ge(vec, count[0])
                return ins

            dve.memset(v["wv_sb"][:], 0.0).then_inc(wv_cleared, 1)
            dve.wait_ge(line_loaded, 16)
            dve.tensor_copy(line[:, 0:S], line[:, S:S + 1].to_broadcast([H, S])).then_inc(line_made, 1)
            dve.memset(line[:, 2 * S - 1:2 * S], 0.0).then_inc(line_made, 1)
            dve.wait_ge(x_loaded, 16)
            for t in range(NT):
                link(dve.bn_stats(stats[:, t, :], x_all[:, t, :]), t == NT - 1)
            for t in range(NT):
                last = dve.bn_aggr(mv[:, t, :], stats[:, t, :])
                if t < NT - 1:
                    link(last, False)
            last.then_inc(var_ready, 1)
            dve.wait_ge(rstd_ready, 2)
            for t in range(NT):
                dve.tensor_scalar(xn[:, t, :], x_all[:, t, :], mv[:, t, 0:1], rstd[:, t, :],
                                  ALU.subtract, ALU.mult).then_inc(x_normed, 1)
            dve.wait_ge(ctx_loaded, 16)
            for t in range(B * KC):
                link(dve.bn_stats(stats[:, t, :], ctx_sb[:, t, :]), t == B * KC - 1)
            for t in range(B * KC):
                last = dve.bn_aggr(mv[:, t, :], stats[:, t, :])
                if t < B * KC - 1:
                    link(last, False)
            last.then_inc(var_ready, 1)
            dve.wait_ge(rstd_ready, 4)
            for t in range(B * KC):
                dve.tensor_scalar(ctx_sb[:, t, :], ctx_sb[:, t, :], mv[:, t, 0:1], rstd[:, t, :],
                                  ALU.subtract, ALU.mult).then_inc(ctx_normed, 1)

        @block.tensor
        def _(pe):
            pe.wait_ge(wc_loaded, 32)
            for h in range(H):
                r = slice(64 * (h % 2), 64 * (h % 2) + 64)
                at = (h % 2) * 512 + (h // 2) % 4 * P
                m = pe.matmul(score[:, h // 8, at:at + P], wq_c_sb[r, h // 2, :], wk_c_sb[r, h // 2, :], start=True, stop=True)
                if h % 8 == 7:
                    m.then_inc(mt_done, 1)
            pe.wait_ge(consts, 4)
            for k in range(NT // 4):
                if k >= 2:
                    pe.wait_ge(xt_free, k - 1)
                pe.wait_ge(x_normed, 4 * k + 4)
                for j in range(4):
                    m = pe.transpose((v["tr_a"], v["tr_b"])[k % 2][:, j * P:(j + 1) * P], xn[:, 4 * k + j, :], ident[:])
                m.then_inc(xt_done, 1)
            for b in range(B):
                bank = (misc, v["av"])[b % 2]
                if b >= 2:
                    pe.wait_ge(tr_free, b - 1)
                pe.wait_ge(ctx_normed, KC * (b + 1))
                for k in range(KC):
                    m = pe.transpose(bank[:, k * P:(k + 1) * P], ctx_sb[:, b * KC + k, :], ident[:])
                m.then_inc(tr_done, 1)

        @block.scalar
        def _(act):
            act.dma_start(wq_c_sb[:], v["wq_c"]).then_inc(wc_loaded, 16)
            act.dma_start(wk_c_sb[:], v["wk_c"]).then_inc(wc_loaded, 16)
            act.dma_start(gb_cols[:], v["ln_cols"]).then_inc(w_loaded, 16)
            act.dma_start(gb_rows[:], v["ln_rows"].rearrange("(o k) e -> o k e", o=1).to_broadcast([P, 2, E])).then_inc(w_loaded, 16)
            act.dma_start(v["wq_sb"][:], v["wq_s"]).then_inc(w_loaded, 16)
            act.dma_start(v["wk_sb"][:], v["wk_s"]).then_inc(w_loaded, 16)
            act.wait_ge(wv_cleared, 1)
            act.dma_start(v["wv_sb"].rearrange("p (h c) -> p h c", c=32)[:, :, 0:D_SELF],
                          v["wv_s"].rearrange("p (h c) -> p h c", c=D_SELF)).then_inc(w_loaded, 16)
            act.dma_start(v["wv_all"][:], v["wv_c"]).then_inc(w_loaded, 16)
            act.dma_start(v["wo_all"][:], v["wo_c"]).then_inc(w_loaded, 16)
            for k in range(2):
                act.wait_ge(mt_done, k + 1)
                act.activation(mt_all[:, 8 * k:8 * k + 8, :].rearrange("p (h o) e -> p o h e", o=2),
                               score[:, k, :].rearrange("p (o h e) -> p o h e", o=2, e=E), ACT.Copy, scale=D_CROSS ** -0.5)
            for k in range(NT // 4):
                act.wait_ge(xt_done, k + 1)
                act.activation(xnT_all[:, 512 * k:512 * k + 512], (v["tr_a"], v["tr_b"])[k % 2][:], ACT.Copy).then_inc(xt_free, 1)
            act.wait_ge(w_loaded, 16 * 7)
            for b in range(B):
                bank = (misc, v["av"])[b % 2]
                act.wait_ge(tr_done, b + 1)
                act.activation(kvT[:, b, 0:C], bank[:], ACT.Identity, scale=gb_cols[:, 0:1],
                               bias=gb_cols[:, 1:2]).then_inc(tr_free, 1)


def self_attention(nc, sb, sem, v):
    xnT_all, o_all, bias, ident, head_mask = (v[k] for k in ("xnT_all", "o_all", "bias", "ident", "head_mask"))
    wq_sb, wk_sb, wv_sb = v["wq_sb"], v["wk_sb"], v["wv_sb"]
    score, tr_a, tr_b, av, misc = (v[k] for k in ("score", "tr_a", "tr_b", "av", "misc"))
    nmax, rsum, rinv, probs, probsT, avT = (v[k] for k in ("nmax", "rsum", "rinv", "probs", "probsT", "avT"))
    U = G * QT
    with ExitStack() as own:
        def tmp(name, shape):
            return own.enter_context(nc.sbuf_tensor(name, shape, F32))
        xnT = tmp("xnT", [P, S])
        q_next = tmp("q_next", [P, S])
        qT = tmp("qT", [P, S])
        kT = tmp("kT", [P, S])
        q_scale = tmp("q_scale", [P, 1])
        k_diag = tmp("k_diag", [P, H, S])
        v_pad = tmp("v_pad", [P, QT, 4 * P])
        qk_done, max_done, exp_done, inv_done, p_ready = (sem("s_" + n) for n in ("qk_done", "max_done", "exp_done", "inv_done", "p_ready"))
        tr_done, ta_free, tb_free, av_done, avT_ready = (sem("s_" + n) for n in ("tr_done", "ta_free", "tb_free", "av_done", "avT_ready"))
        scale_ready, misc_full, misc_free, q_ready, kd_ready, x_staged = (sem("s_" + n) for n in ("scale_ready", "misc_full", "misc_free", "q_ready", "kd_ready", "x_staged"))
        block = own.enter_context(nc.Block())

        OUT2, V0, OUT3, V1, OUT0, PROJECT, OUT1 = range(7)
        R = 7

        def use(b, k):
            if isinstance(b, int) and b == -1:
                return 0
            if isinstance(b, int) and b == 0 and k == V0:
                return 1
            if isinstance(b, int) and b == B - 1 and k == OUT1:
                return R * b + k - 2
            if isinstance(b, int) and b == B:
                return R * (B - 1) + (5 if k == OUT2 else 6)
            return R * b + k - 1

        @block.tensor
        def _(pe):
            def scores(b, u):
                g, qt, n = u // QT, u % QT, U * b + u
                if u == 0:
                    pe.wait_ge(q_ready, b + 1)
                if qt == 0:
                    pe.wait_ge(kd_ready, G * b + g + 1)
                wait(pe, exp_done, n - 1)
                for j in range(2):
                    m = pe.matmul(score[:, u % 2, j * 512:(j + 1) * 512], qT[:, qt * P:(qt + 1) * P],
                                  k_diag[:, 4 * g + 2 * j:4 * g + 2 * j + 2, :], start=True, stop=True)
                m.then_inc(qk_done, 1)

            def transposes(b, u):
                n = U * b + u
                pe.wait_ge(p_ready, n + 1)
                for half, bank, free in ((0, tr_a, ta_free), (1, tr_b, tb_free)):
                    wait(pe, free, n)
                    for k in range(4):
                        at = half * 512 + k * P
                        m = pe.transpose(bank[:, k * P:(k + 1) * P], probs[:, u % 4, at:at + P], ident[:])
                    m.then_inc(tr_done, 1)

            def attend(b, g):
                n = G * b + g
                pe.wait_ge(ta_free, QT * n + QT)
                pe.wait_ge(tb_free, QT * n + QT)
                wait(pe, avT_ready, n)
                if g == 0:
                    pe.wait_ge(misc_free, use(b, V1) + 1)
                for kt in range(QT):
                    for j in range(4):
                        m = pe.matmul(av[32 * j:32 * j + 32, 0:S], v_pad[:, kt, (4 * g + j) * 32:(4 * g + j + 1) * 32],
                                      probsT[:, g % 2, (2 * j + kt) * S:(2 * j + kt + 1) * S],
                                      start=kt == 0, stop=kt == QT - 1, tile_position=(0, 32 * j))
                m.then_inc(av_done, 1)

            def natural(b, g, at):
                wait(pe, misc_free, at)
                pe.wait_ge(avT_ready, G * b + g + 1)
                for qt in range(QT):
                    m = pe.transpose(misc[:, qt * P:(qt + 1) * P], avT[:, g % 2, qt * P:(qt + 1) * P], ident[:])
                m.then_inc(misc_full, 1)

            def project_qk(b):
                wait(pe, misc_free, use(b, PROJECT))
                pe.wait_ge(x_staged, b + 2)
                pe.matmul(misc[:, 0:S], wq_sb[:], xnT[:], start=True, stop=True)
                pe.matmul(misc[:, S:2 * S], wk_sb[:], xnT[:], start=True, stop=True).then_inc(misc_full, 1)

            def project_v(b, kt):
                wait(pe, misc_free, use(b, (V0, V1)[kt]))
                pe.matmul(misc[:], xnT[:, kt * P:(kt + 1) * P], wv_sb[:], start=True, stop=True).then_inc(misc_full, 1)

            def batch(b, first=False, last=False):
                scores(b, 0)
                if not first:
                    attend(b - 1, 2)
                    transposes(b - 1, 6)
                scores(b, 1)
                if not first:
                    transposes(b - 1, 7)
                    natural(b - 1, 2, use(b, OUT2))
                scores(b, 2)
                if not first:
                    attend(b - 1, 3)
                transposes(b, 0)
                project_v(b, 0)
                scores(b, 3)
                transposes(b, 1)
                if not first:
                    natural(b - 1, 3, use(b, OUT3))
                project_v(b, 1)
                scores(b, 4)
                attend(b, 0)
                transposes(b, 2)
                scores(b, 5)
                transposes(b, 3)
                natural(b, 0, use(b, OUT0))
                scores(b, 6)
                attend(b, 1)
                transposes(b, 4)
                if not last:
                    project_qk(b)
                scores(b, 7)
                transposes(b, 5)
                natural(b, 1, use(b, OUT1))

            project_qk(-1)
            batch(0, first=True)
            with pe.Fori(1, B - 1) as b:
                batch(b)
            batch(B - 1, last=True)
            attend(B - 1, 2)
            transposes(B - 1, 6)
            transposes(B - 1, 7)
            natural(B - 1, 2, use(B, OUT2))
            attend(B - 1, 3)
            natural(B - 1, 3, use(B, OUT3))

        @block.scalar
        def _(act):
            def exponentials(b, u):
                n = U * b + u
                act.wait_ge(max_done, n + 1)
                if not isinstance(n, int) or n >= 4:
                    act.wait_ge(tr_done, 2 * n - 6)
                for j in range(4):
                    m = act.activation(probs[:, u % 4, j * S:(j + 1) * S], score[:, u % 2, j * S:(j + 1) * S], ACT.Exp,
                                       bias=nmax[:, u % 4, j:j + 1], accum_out=rsum[:, u % 4, j:j + 1])
                m.then_inc(exp_done, 1)

            def evacuate_a(b, u):
                n, g, qt = U * b + u, u // QT, u % QT
                act.wait_ge(tr_done, 2 * n + 1)
                wait(act, av_done, G * b + g - 1)
                act.activation(probsT[:, g % 2, 0:4 * S].rearrange("p (k q) -> p k q", k=4)[:, :, qt * P:(qt + 1) * P],
                               tr_a[:].rearrange("p (k q) -> p k q", k=4), ACT.Copy).then_inc(ta_free, 1)

            def evacuate_av(b, g):
                act.wait_ge(av_done, G * b + g + 1)
                act.activation(avT[:, g % 2, :], av[:, 0:S], ACT.Copy).then_inc(avT_ready, 1)

            def evacuate_qk(b):
                act.wait_ge(misc_full, use(b, PROJECT) + 1)
                wait(act, q_ready, b + 1)
                wait(act, kd_ready, G * b + G)
                act.activation(q_next[:], misc[:, 0:S], ACT.Copy)
                act.activation(kT[:], misc[:, S:2 * S], ACT.Copy).then_inc(misc_free, 1)

            def evacuate_v(b, kt):
                act.wait_ge(misc_full, use(b, (V0, V1)[kt]) + 1)
                wait(act, av_done, G * b)
                act.activation(v_pad[:, kt, :], misc[:], ACT.Copy).then_inc(misc_free, 1)

            def evacuate_natural(b, g, at):
                act.wait_ge(misc_full, at + 1)
                act.activation(o_all[:, bass.ds(QT * b, QT), g * 32:(g + 1) * 32].rearrange("p t (j c) -> p t j c", c=D_SELF),
                               misc[:, 0:S].rearrange("p (t j c) -> p t j c", t=QT, j=4)[:, :, :, 0:D_SELF],
                               ACT.Copy).then_inc(misc_free, 1)

            def batch(b, first=False, last=False):
                if not first:
                    evacuate_av(b - 1, 2)
                    evacuate_a(b - 1, 6)
                exponentials(b, 0)
                if not first:
                    evacuate_a(b - 1, 7)
                    evacuate_natural(b - 1, 2, use(b, OUT2))
                exponentials(b, 1)
                if not first:
                    evacuate_av(b - 1, 3)
                evacuate_a(b, 0)
                evacuate_v(b, 0)
                exponentials(b, 2)
                evacuate_a(b, 1)
                if not first:
                    evacuate_natural(b - 1, 3, use(b, OUT3))
                evacuate_v(b, 1)
                exponentials(b, 3)
                evacuate_av(b, 0)
                evacuate_a(b, 2)
                exponentials(b, 4)
                evacuate_a(b, 3)
                evacuate_natural(b, 0, use(b, OUT0))
                exponentials(b, 5)
                evacuate_av(b, 1)
                evacuate_a(b, 4)
                if not last:
                    evacuate_qk(b)
                exponentials(b, 6)
                evacuate_a(b, 5)
                evacuate_natural(b, 1, use(b, OUT1))
                exponentials(b, 7)

            evacuate_qk(-1)
            batch(0, first=True)
            with act.Fori(1, B - 1) as b:
                batch(b)
            batch(B - 1, last=True)
            evacuate_av(B - 1, 2)
            evacuate_a(B - 1, 6)
            evacuate_a(B - 1, 7)
            evacuate_natural(B - 1, 2, use(B, OUT2))
            evacuate_av(B - 1, 3)
            evacuate_natural(B - 1, 3, use(B, OUT3))

        @block.vector
        def _(dve):
            def maxima(b, u):
                dve.wait_ge(qk_done, U * b + u + 1)
                dve.tensor_reduce(nmax[:, u % 4, :], score[:, u % 2, :].rearrange("p (j k) -> p j k", j=4),
                                  axis=AX.X, op=ALU.max, negate=True).then_inc(max_done, 1)

            def evacuate_b(b, u):
                n, g, qt = U * b + u, u // QT, u % QT
                dve.wait_ge(tr_done, 2 * n + 2)
                wait(dve, av_done, G * b + g - 1)
                dve.tensor_copy(probsT[:, g % 2, 4 * S:8 * S].rearrange("p (k q) -> p k q", k=4)[:, :, qt * P:(qt + 1) * P],
                                tr_b[:].rearrange("p (k q) -> p k q", k=4)).then_inc(tb_free, 1)

            def normalize(b, u):
                n, g, qt = U * b + u, u // QT, u % QT
                dve.wait_ge(exp_done, n + 1)
                dve.reciprocal(rinv[:, u % 4, :], rsum[:, u % 4, :]).then_inc(inv_done, 1)
                dve.wait_ge(inv_done, n + 1)
                for j in range(4):
                    m = dve.scalar_tensor_tensor(out=probs[:, u % 4, j * S:(j + 1) * S], in0=probs[:, u % 4, j * S:(j + 1) * S],
                                                 scalar=rinv[:, u % 4, j:j + 1], in1=bias[:, qt, 4 * g + j, :],
                                                 op0=ALU.mult, op1=ALU.add)
                m.then_inc(p_ready, 1)

            def batch(b, first=False):
                for u in range(U):
                    maxima(b, u)
                    if u >= 2:
                        evacuate_b(b, u - 2)
                    elif not first:
                        evacuate_b(b - 1, U + u - 2)
                    if u >= 1:
                        normalize(b, u - 1)
                    elif not first:
                        normalize(b - 1, U - 1)

            batch(0, first=True)
            with dve.Fori(1, B) as b:
                batch(b)
            evacuate_b(B - 1, U - 2)
            normalize(B - 1, U - 1)
            evacuate_b(B - 1, U - 1)

        @block.gpsimd
        def _(pool):
            def stage_x(b):
                if not (isinstance(b, int) and b == -1):
                    pool.wait_ge(misc_full, use(b, V1) + 1)
                pool.tensor_copy(xnT[:], xnT_all[:, bass.ds(S * (b + 1), S)]).then_inc(x_staged, 1)

            def spread_keys(b, g):
                if not (isinstance(b, int) and b == -1):
                    pool.wait_ge(qk_done, U * b + QT * (g + 1))
                pool.tensor_tensor(k_diag[:, 4 * g:4 * g + 4, :],
                                   kT[:].rearrange("p (o k) -> p o k", o=1).to_broadcast([P, 4, S]),
                                   head_mask[:, 4 * g:4 * g + 4].rearrange("p (h o) -> p h o", o=1).to_broadcast([P, 4, S]),
                                   ALU.mult).then_inc(kd_ready, 1)

            def next_batch(b):
                stage_x(b)
                pool.wait_ge(misc_free, use(b, PROJECT) + 1)
                for g in range(G - 1):
                    spread_keys(b, g)
                if not (isinstance(b, int) and b == -1):
                    pool.wait_ge(qk_done, U * b + U)
                pool.tensor_tensor(qT[:], q_next[:], q_scale[:].to_broadcast([P, S]), ALU.mult).then_inc(q_ready, 1)
                spread_keys(b, G - 1)

            pool.memset(q_scale[:], E ** -0.5).then_inc(scale_ready, 1)
            pool.wait_ge(scale_ready, 1)
            next_batch(-1)
            with pool.Fori(0, B - 1) as b:
                next_batch(b)


def norm_stats(dve, step, x, n, stats, mv, ready):
    for t in range(n):
        m = dve.bn_stats(stats[:, t, :], x[:, t, :])
    step(m)
    for t in range(n):
        m = dve.bn_aggr(mv[:, t, :], stats[:, t, :])
    m.then_inc(ready, 1)


def latents(nc, sb, sem, v):
    x_all, o_all, kvT, ident, gb_rows, gb_cols = (v[k] for k in ("x_all", "o_all", "kvT", "ident", "gb_rows", "gb_cols"))
    stats, mv, rstd, half_neg = (v[k] for k in ("stats", "mv", "rstd", "half_neg"))
    banks = (v["misc"], v["av"])
    with ExitStack() as own:
        step_done, var_ready, rstd_ready, latent_ready, tr_done, tr_free = (
            sem("l_" + n) for n in ("step_done", "var_ready", "rstd_ready", "latent_ready", "tr_done", "tr_free"))
        block = own.enter_context(nc.Block())

        @block.vector
        def _(dve):
            steps = [0]

            def step(m):
                steps[0] += 1
                m.then_inc(step_done, 1)
                dve.wait_ge(step_done, steps[0])

            def normalized(dst, src, k, last=None):
                dve.wait_ge(rstd_ready, 2 * k + 2)
                for t in range(NT):
                    m = dve.tensor_scalar(dst[:, t, :], src[:, t, :], mv[:, t, 0:1], rstd[:, t, :], ALU.subtract, ALU.mult)
                    if last is not None:
                        m.then_inc(last, 1)
                if last is None:
                    step(m)

            def row(k):
                return gb_rows[:, k:k + 1, :].to_broadcast([P, NT, E])

            norm_stats(dve, step, o_all, NT, stats, mv, var_ready)
            normalized(o_all, o_all, 0)
            step(dve.tensor_tensor(o_all[:], o_all[:], row(0), ALU.mult))
            step(dve.tensor_tensor(o_all[:], o_all[:], row(1), ALU.add))
            step(dve.tensor_tensor(x_all[:], x_all[:], o_all[:], ALU.add))
            norm_stats(dve, step, x_all, NT, stats, mv, var_ready)
            normalized(o_all, x_all, 1)
            norm_stats(dve, step, o_all, NT, stats, mv, var_ready)
            normalized(o_all, o_all, 2, latent_ready)

        @block.gpsimd
        def _(pool):
            for k in range(3):
                inverse_roots(pool, v, NT, k, var_ready, rstd_ready)

        @block.tensor
        def _(pe):
            for k in range(NT // 4):
                pe.wait_ge(latent_ready, 4 * k + 4)
                if k >= 2:
                    pe.wait_ge(tr_free, k - 1)
                for j in range(4):
                    m = pe.transpose(banks[k % 2][:, j * P:(j + 1) * P], o_all[:, 4 * k + j, :], ident[:])
                m.then_inc(tr_done, 1)

        @block.scalar
        def _(act):
            for k in range(NT // 4):
                act.wait_ge(tr_done, k + 1)
                act.activation(kvT[:, 2 * k:2 * k + 2, C:L], banks[k % 2][:].rearrange("p (b q) -> p b q", b=2), ACT.Identity,
                               scale=gb_cols[:, 2:3], bias=gb_cols[:, 3:4]).then_inc(tr_free, 1)


def inverse_roots(pool, v, n, k, var_ready, rstd_ready):
    mv, rstd, half_neg = v["mv"], v["rstd"], v["half_neg"]
    pool.wait_ge(var_ready, k + 1)
    pool.tensor_scalar(rstd[:, 0:n, :], mv[:, 0:n, 1:2], EPS, 1.0, ALU.add, ALU.mult).then_inc(rstd_ready, 1)
    pool.wait_ge(rstd_ready, 2 * k + 1)
    pool.tensor_tensor(rstd[:, 0:n, :], rstd[:, 0:n, :], half_neg[:, 0:n, :], ALU.pow).then_inc(rstd_ready, 1)


def cross_attention(nc, sb, sem, v):
    x_all, kvT, ident, mt_all, wv_all, wo_all = (v[k] for k in ("x_all", "kvT", "ident", "mt_all", "wv_all", "wo_all"))
    score, tr_a, tr_b, av, misc = (v[k] for k in ("score", "tr_a", "tr_b", "av", "misc"))
    nmax, rsum, rinv, probs, probsT, avT = (v[k] for k in ("nmax", "rsum", "rinv", "probs", "probsT", "avT"))
    IT = B * PAIRS // 2
    ITB = PAIRS // 2
    U = 4
    V_FIRST = 4
    with ExitStack() as own:
        def tmp(name, shape):
            return own.enter_context(nc.sbuf_tensor(name, shape, F32))
        mt = tmp("mt", [P, 2, 2, E])
        kv = tmp("kv", [P, L])
        aT = tmp("aT", [P, 2, 2, S])
        val = tmp("val", [P, 2, KT, P])
        qk_done, max_done, exp_done, inv_done, p_ready = (sem("c_" + n) for n in ("qk_done", "max_done", "exp_done", "inv_done", "p_ready"))
        tr_done, ta_free, tb_free, av_done, avT_ready = (sem("c_" + n) for n in ("tr_done", "ta_free", "tb_free", "av_done", "avT_ready"))
        misc_full, misc_free, out_added, staged = (sem("c_" + n) for n in ("misc_full", "misc_free", "out_added", "staged"))
        block = own.enter_context(nc.Block())

        def use_v_out(p):
            return 3 * p + 2

        def use_q(p):
            return 3 * p

        def use_v(p):
            return 3 * p + 1

        @block.tensor
        def _(pe):
            def scores(i, j, u):
                p, h, qt = 2 * i + j, u // 2, u % 2
                n = U * p + u
                if u == 0:
                    pe.wait_ge(misc_free, use_q(p) + 1)
                wait(pe, exp_done, n - 1)
                for half in range(2):
                    m = pe.matmul(score[:, u % 2, half * 512:half * 512 + HALF], aT[:, j, h, qt * P:(qt + 1) * P],
                                  kvT[:, i // ITB, half * HALF:(half + 1) * HALF] if isinstance(i, int) else
                                  kvT[:, bass.ds(i // ITB, 1), half * HALF:(half + 1) * HALF], start=True, stop=True)
                m.then_inc(qk_done, 1)

            def transposes(p, u):
                n = U * p + u
                pe.wait_ge(p_ready, n + 1)
                for half, bank, free in ((0, tr_a, ta_free), (1, tr_b, tb_free)):
                    wait(pe, free, n)
                    for k in range(KT // 2):
                        at = half * HALF + k * P
                        m = pe.transpose(bank[:, k * P:(k + 1) * P], probs[:, u % 4, at:at + P], ident[:])
                    m.then_inc(tr_done, 1)

            def attend(p, par):
                pe.wait_ge(ta_free, U * p + U)
                pe.wait_ge(tb_free, U * p + U)
                pe.wait_ge(misc_free, use_v_out(p) + 1)
                wait(pe, avT_ready, p)
                for kt in range(KT):
                    for h in range(2):
                        m = pe.matmul(av[64 * h:64 * h + 64, 0:S], val[:, par, kt, 64 * h:64 * h + 64],
                                      probsT[:, par, (KT * h + kt) * S:(KT * h + kt + 1) * S],
                                      start=kt == 0, stop=kt == KT - 1, tile_position=(0, 64 * h))
                m.then_inc(av_done, 1)

            def queries(i, j):
                p = 2 * i + j
                wait(pe, misc_free, use_q(p))
                wait(pe, out_added, p - 2)
                pe.wait_ge(staged, 3 * i + 1 + 2 * j)
                for h in range(2):
                    rhs = kvT[:, i // ITB, C:L] if isinstance(i, int) else kvT[:, bass.ds(i // ITB, 1), C:L]
                    m = pe.matmul(misc[:, h * S:(h + 1) * S], mt[:, j, h, :], rhs, start=True, stop=True)
                m.then_inc(misc_full, 1)

            def value_columns(i, j):
                return bass.ds((i % ITB) * (2 * P) + j * P, P)

            def values_first(i, j):
                p = 2 * i + j
                wait(pe, misc_free, use_v(p))
                if j == 0:
                    pe.wait_ge(staged, 3 * i + 2)
                for kt in range(V_FIRST):
                    m = pe.matmul(misc[:, kt * P:(kt + 1) * P], kv[:, kt * P:(kt + 1) * P], wv_all[:, value_columns(i, j)],
                                  start=True, stop=True)
                m.then_inc(misc_full, 1)

            def project_out(i, j):
                pe.wait_ge(avT_ready, 2 * i + j + 1)
                for qt in range(QT):
                    m = pe.matmul(misc[:, 256 + qt * P:256 + (qt + 1) * P], avT[:, j, qt * P:(qt + 1) * P],
                                  wo_all[:, (i % ITB) * 2 + j, :] if isinstance(i, int) else
                                  wo_all[:, bass.ds((i % ITB) * 2 + j, 1), :], start=True, stop=True)
                return m

            def values_rest(i, j):
                for kt in range(V_FIRST, KT):
                    m = pe.matmul(misc[:, (kt - V_FIRST) * P:(kt - V_FIRST + 1) * P], kv[:, kt * P:(kt + 1) * P],
                                  wv_all[:, value_columns(i, j)], start=True, stop=True)
                return m

            def pair(i, j, first=False, last=False):
                p = 2 * i + j
                before = (i, 0) if j else (i - 1, 1)
                after = (i, 1) if j == 0 else (i + 1, 0)
                none_before = first and j == 0
                scores(i, j, 0)
                if not none_before:
                    transposes(p - 1, 2)
                wait(pe, misc_free, use_v_out(p))
                m = values_rest(i, j)
                if not first:
                    m = project_out(i - 1, j)
                m.then_inc(misc_full, 1)
                scores(i, j, 1)
                if not none_before:
                    transposes(p - 1, 3)
                if not (last and j):
                    queries(*after)
                scores(i, j, 2)
                if not none_before:
                    attend(p - 1, 1 - j)
                transposes(p, 0)
                scores(i, j, 3)
                transposes(p, 1)
                if not (last and j):
                    values_first(*after)

            queries(0, 0)
            values_first(0, 0)
            for j in range(2):
                pair(0, j, first=True)
            with pe.Fori(1, IT - 1) as i:
                for j in range(2):
                    pair(i, j)
            for j in range(2):
                pair(IT - 1, j, last=True)
            p = 2 * IT - 1
            transposes(p, 2)
            transposes(p, 3)
            pe.wait_ge(misc_free, use_v_out(p) + 1)
            wait(pe, out_added, p - 1)
            project_out(IT - 1, 0).then_inc(misc_full, 1)
            attend(p, 1)
            pe.wait_ge(out_added, p)
            project_out(IT - 1, 1).then_inc(misc_full, 1)

        @block.scalar
        def _(act):
            def exponentials(p, u):
                n = U * p + u
                act.wait_ge(max_done, n + 1)
                if not isinstance(n, int) or n >= 4:
                    act.wait_ge(tr_done, 2 * n - 6)
                act.activation(probs[:, u, 0:L].rearrange("p (a k) -> p a k", a=2),
                               score[:, u % 2, :].rearrange("p (a k) -> p a k", a=2)[:, :, 0:HALF], ACT.Exp,
                               bias=nmax[:, u, 0:1], accum_out=rsum[:, u, 0:1]).then_inc(exp_done, 1)

            def evacuate_a(p, par, u):
                n, h, qt = U * p + u, u // 2, u % 2
                act.wait_ge(tr_done, 2 * n + 1)
                wait(act, av_done, p - 1)
                act.activation(probsT[:, par, KT * h * S:(KT * h + 3) * S].rearrange("p (k q) -> p k q", k=3)[:, :, qt * P:(qt + 1) * P],
                               tr_a[:, 0:HALF].rearrange("p (k q) -> p k q", k=3), ACT.Copy).then_inc(ta_free, 1)

            def evacuate_av(p, par):
                act.wait_ge(av_done, p + 1)
                wait(act, misc_full, use_v_out(p) + 1 if not isinstance(p, int) or p >= 2 else 0)
                act.activation(avT[:, par, :], av[:, 0:S], ACT.Copy).then_inc(avT_ready, 1)

            def evacuate_values(p, par, use, kt, n):
                act.wait_ge(misc_full, use + 1)
                wait(act, av_done, p - 1)
                act.activation(val[:, par, kt:kt + n, :], misc[:, 0:n * P].rearrange("p (k c) -> p k c", k=n),
                               ACT.Copy).then_inc(misc_free, 1)

            def evacuate_queries(p, par):
                act.wait_ge(misc_full, use_q(p) + 1)
                wait(act, qk_done, U * (p - 1))
                act.activation(aT[:, par, :, :], misc[:].rearrange("p (h q) -> p h q", h=2), ACT.Copy).then_inc(misc_free, 1)

            def pair(i, j, first=False, last=False):
                p = 2 * i + j
                none_before = first and j == 0
                if not none_before:
                    evacuate_a(p - 1, 1 - j, 2)
                evacuate_values(p, j, use_v_out(p), V_FIRST, KT - V_FIRST)
                exponentials(p, 0)
                if not none_before:
                    evacuate_a(p - 1, 1 - j, 3)
                if not (last and j):
                    evacuate_queries(p + 1, 1 - j)
                exponentials(p, 1)
                if not none_before:
                    evacuate_av(p - 1, 1 - j)
                evacuate_a(p, j, 0)
                exponentials(p, 2)
                evacuate_a(p, j, 1)
                if not (last and j):
                    evacuate_values(p + 1, 1 - j, use_v(p + 1), 0, V_FIRST)
                exponentials(p, 3)

            evacuate_queries(0, 0)
            evacuate_values(0, 0, use_v(0), 0, V_FIRST)
            for j in range(2):
                pair(0, j, first=True)
            with act.Fori(1, IT - 1) as i:
                for j in range(2):
                    pair(i, j)
            for j in range(2):
                pair(IT - 1, j, last=True)
            p = 2 * IT - 1
            evacuate_a(p, 1, 2)
            evacuate_a(p, 1, 3)
            act.wait_ge(av_done, p + 1)
            act.activation(avT[:, 1, :], av[:, 0:S], ACT.Copy).then_inc(avT_ready, 1)

        @block.vector
        def _(dve):
            def maxima(p, u):
                dve.wait_ge(qk_done, U * p + u + 1)
                dve.tensor_reduce(nmax[:, u, 0:1], score[:, u % 2, :].rearrange("p (a k) -> p a k", a=2)[:, :, 0:HALF],
                                  axis=AX.XY, op=ALU.max, negate=True).then_inc(max_done, 1)

            def evacuate_b(p, par, u):
                n, h, qt = U * p + u, u // 2, u % 2
                dve.wait_ge(tr_done, 2 * n + 2)
                wait(dve, av_done, p - 1)
                dve.tensor_copy(probsT[:, par, (KT * h + 3) * S:(KT * h + 6) * S].rearrange("p (k q) -> p k q", k=3)[:, :, qt * P:(qt + 1) * P],
                                tr_b[:, 0:HALF].rearrange("p (k q) -> p k q", k=3)).then_inc(tb_free, 1)

            def normalize(p, u):
                n = U * p + u
                dve.wait_ge(exp_done, n + 1)
                dve.reciprocal(rinv[:, u, 0:1], rsum[:, u, 0:1]).then_inc(inv_done, 1)
                dve.wait_ge(inv_done, n + 1)
                dve.tensor_scalar(probs[:, u, 0:L], probs[:, u, 0:L], rinv[:, u, 0:1], None, ALU.mult).then_inc(p_ready, 1)

            def add_output(i, n, use):
                dve.wait_ge(misc_full, use + 1)
                wait(dve, out_added, n)
                x = x_all[:, bass.ds((i // ITB) * QT, QT), :]
                dve.tensor_tensor(x, misc[:, 256:512].rearrange("p (t e) -> p t e", t=QT), x, ALU.add).then_inc(out_added, 1)

            def pair(i, j, first=False):
                p = 2 * i + j
                none_before = first and j == 0
                for u in range(U):
                    maxima(p, u)
                    if u >= 2:
                        evacuate_b(p, j, u - 2)
                    elif not none_before:
                        evacuate_b(p - 1, 1 - j, U + u - 2)
                    if u == 0 and not first:
                        dve.wait_ge(misc_free, use_v_out(p) + 1)
                        add_output(i - 1, p - 2, use_v_out(p))
                    if u >= 1:
                        normalize(p, u - 1)
                    elif not none_before:
                        normalize(p - 1, U - 1)

            for j in range(2):
                pair(0, j, first=True)
            with dve.Fori(1, IT) as i:
                for j in range(2):
                    pair(i, j)
            p = 2 * IT - 1
            evacuate_b(p, 1, 2)
            normalize(p, 3)
            evacuate_b(p, 1, 3)
            add_output(IT - 1, p - 1, use_v_out(p) + 1)
            add_output(IT - 1, p, use_v_out(p) + 2)

        @block.gpsimd
        def _(pool):
            def stage_weights(i, j):
                p = 2 * i + j
                wait(pool, misc_full, use_q(p - 2) + 1 if not isinstance(p, int) or p >= 2 else 0)
                pool.tensor_copy(mt[:, j, :, :], mt_all[:, bass.ds((i % ITB) * 4 + 2 * j, 2), :]).then_inc(staged, 1)

            def stage_tokens(i):
                wait(pool, misc_full, use_v_out(2 * i - 1) + 1 if not isinstance(i, int) or i >= 1 else 0)
                pool.tensor_copy(kv[:], kvT[:, bass.ds(i // ITB, 1), :].rearrange("p o l -> p (o l)")).then_inc(staged, 1)

            stage_weights(0, 0)
            stage_tokens(0)
            stage_weights(0, 1)
            with pool.Fori(1, IT) as i:
                stage_weights(i, 0)
                stage_tokens(i)
                stage_weights(i, 1)


def experts(nc, sb, sem, v):
    x_all, o_all, xnT_all, ident = (v[k] for k in ("x_all", "o_all", "xnT_all", "ident"))
    stats, mv, rstd, half_neg = (v[k] for k in ("stats", "mv", "rstd", "half_neg"))
    misc, av, tr_a, tr_b, score = (v[k] for k in ("misc", "av", "tr_a", "tr_b", "score"))
    TT = N_TOK // 512
    with ExitStack() as own:
        def tmp(name, shape, dt=F32):
            return own.enter_context(nc.sbuf_tensor(name, shape, dt))
        wg_sb = tmp("wg_sb", [P, N_EXP])
        w1_sb = tmp("w1_sb", [P, 2, 2 * I_FF])
        w2_sb = tmp("w2_sb", [P, 2, 2, E])
        hid = tmp("hid", [P, 2, 2, 512])
        before = tmp("before", [P, P])
        ones = tmp("ones", [P, P])
        iota_e = tmp("iota_e", [P, NT, N_EXP])
        carry_on = tmp("carry_on", [P, N_EXP, NT])
        logits = tmp("logits", [P, NT, N_EXP])
        top_v = tmp("top_v", [P, NT, 8])
        top_i = tmp("top_i", [P, NT, 8], U32)
        top_f = tmp("top_f", [P, NT, 8])
        pick = tmp("pick", [P, 2, NT, N_EXP])
        chosen = tmp("chosen", [P, NT, N_EXP])
        gate_w = tmp("gate_w", [P, 4, NT, 1])
        totals = tmp("totals", [P, N_EXP, NT])
        running = tmp("running", [P, N_EXP, NT])
        place = tmp("place", [P, NT, N_EXP])
        gates = tmp("gates", [P, NT, N_EXP])
        step_done, var_ready, rstd_ready, normed, tr_done, tr_free = (
            sem("e_" + n) for n in ("step_done", "var_ready", "rstd_ready", "normed", "tr_done", "tr_free"))
        consts, logits_done, chosen_ready, places_done, gap_ready, gate_exp, wg_loaded, w_loaded = (
            sem("e_" + n) for n in ("consts", "logits_done", "chosen_ready", "places_done", "gap_ready", "gate_exp", "wg_loaded", "w_loaded"))
        up_done, gelu_done, hid_ready, down_done, added, stored = (
            sem("e_" + n) for n in ("up_done", "gelu_done", "hid_ready", "down_done", "added", "stored"))
        block = own.enter_context(nc.Block())
        N = N_EXP * TT

        @block.sync
        def _(sp):
            sp.dma_start(wg_sb[:], v["wg"]).then_inc(wg_loaded, 16)

            def load(e, par):
                sp.dma_start(w1_sb[:, par, :], v["w1"][e]).then_inc(w_loaded, 16)
                sp.dma_start(w2_sb[:, par], v["w2"][e].rearrange("(k p) e -> p k e", p=P)).then_inc(w_loaded, 16)
                sp.wait_ge(w_loaded, 32 * e + 32)

            for e in range(N_EXP):
                wait(sp, down_done, TT * (e - 1))
                load(e, e % 2)
            for t in range(0, NT, 4):
                sp.wait_ge(added, N - TT + t // 4 + 1)
                sp.dma_start(v["out"].rearrange("(t p) e -> p t e", p=P)[:, t:t + 4, :], x_all[:, t:t + 4, :]).then_inc(stored, 16)
            sp.wait_ge(stored, 16 * NT // 4)

        @block.gpsimd
        def _(pool):
            pool.memset(ones[:], 1.0).then_inc(consts, 1)
            pool.memset(before[:], 1.0).then_inc(consts, 1)
            pool.memset(carry_on[:], 1.0).then_inc(consts, 1)
            pool.iota(iota_e[:], pattern=[[0, NT], [1, N_EXP]], base=0, channel_multiplier=0,
                      allow_small_or_imprecise_dtypes=True).then_inc(consts, 1)
            pool.wait_ge(consts, 4)
            pool.affine_select(out=before[:], in_=before[:], compare_op=ALU.is_ge, fill=0.0, base=-1,
                               pattern=[[1, P]], channel_multiplier=-1).then_inc(consts, 1)
            pool.memset(carry_on[:, :, 0:1], 0.0).then_inc(consts, 1)
            inverse_roots(pool, v, NT, 0, var_ready, rstd_ready)

        @block.vector
        def _(dve):
            steps = [0]

            def step(m):
                steps[0] += 1
                m.then_inc(step_done, 1)
                dve.wait_ge(step_done, steps[0])

            norm_stats(dve, step, x_all, NT, stats, mv, var_ready)
            dve.wait_ge(rstd_ready, 2)
            for t in range(NT):
                dve.tensor_scalar(o_all[:, t, :], x_all[:, t, :], mv[:, t, 0:1], rstd[:, t, :],
                                  ALU.subtract, ALU.mult).then_inc(normed, 1)
            dve.wait_ge(logits_done, 1)
            step(dve.tensor_copy(logits[:], misc[:, 0:NT * N_EXP].rearrange("p (t e) -> p t e", e=N_EXP)))
            for t in range(NT):
                m = dve.max(top_v[:, t, :], logits[:, t, :])
            step(m)
            for t in range(NT):
                m = dve.max_index(top_i[:, t, :], top_v[:, t, :], logits[:, t, :])
            step(m)
            step(dve.tensor_copy(top_f[:], top_i[:]))
            dve.wait_ge(consts, 6)
            for k in range(TOP):
                m = dve.tensor_tensor(pick[:, k], iota_e[:], top_f[:, :, k:k + 1].to_broadcast([P, NT, N_EXP]), ALU.is_equal)
            step(m)
            dve.tensor_tensor(chosen[:], pick[:, 0], pick[:, 1], ALU.add).then_inc(chosen_ready, 1)
            dve.tensor_tensor(gate_w[:, 0], top_v[:, :, 1:2], top_v[:, :, 0:1], ALU.subtract).then_inc(gap_ready, 1)
            dve.wait_ge(gate_exp, 1)
            step(dve.tensor_scalar(gate_w[:, 2], gate_w[:, 1], 1.0, None, ALU.add))
            step(dve.reciprocal(gate_w[:, 3], gate_w[:, 2]))
            step(dve.tensor_tensor(gate_w[:, 1], gate_w[:, 1], gate_w[:, 3], ALU.mult))
            m = dve.tensor_tensor(pick[:, 0], pick[:, 0], gate_w[:, 3].to_broadcast([P, NT, N_EXP]), ALU.mult)
            m = dve.tensor_tensor(pick[:, 1], pick[:, 1], gate_w[:, 1].to_broadcast([P, NT, N_EXP]), ALU.mult)
            step(m)
            step(dve.tensor_tensor(gates[:], pick[:, 0], pick[:, 1], ALU.add))
            dve.wait_ge(places_done, 1)
            step(dve.tensor_copy(totals[:], av[:, 0:P].rearrange("p (t e) -> p e t", e=N_EXP)))
            step(dve.tensor_tensor_scan(running[:].rearrange("p e t -> p (e t)"), carry_on[:].rearrange("p e t -> p (e t)"),
                                        totals[:].rearrange("p e t -> p (e t)"), 0.0, ALU.mult, ALU.add))
            step(dve.tensor_tensor(running[:], running[:], totals[:], ALU.subtract))
            step(dve.tensor_tensor(place[:], misc[:, 0:P].rearrange("p (t e) -> p t e", e=N_EXP),
                                   running[:].rearrange("p e t -> p t e"), ALU.add))
            step(dve.tensor_scalar(place[:], place[:], float(CAP), None, ALU.is_lt))
            step(dve.tensor_tensor(gates[:], gates[:], place[:], ALU.mult))

            def multiply(n, tt):
                for f in range(2):
                    dve.wait_ge(gelu_done, 2 * n + f + 1)
                    dve.tensor_tensor(hid[:, tt % 2, f, :], hid[:, tt % 2, f, :], score[:, f, 512:1024],
                                      ALU.mult).then_inc(hid_ready, 1)

            def accumulate(n, e, tt):
                dve.wait_ge(down_done, n + 1)
                wait(dve, added, n - TT + 1)
                for k in range(4):
                    t = 4 * tt + k
                    m = dve.scalar_tensor_tensor(out=x_all[:, t, :], in0=(tr_a, tr_b)[tt % 2][:, k * P:(k + 1) * P],
                                                 scalar=gates[:, t, bass.ds(e, 1)], in1=x_all[:, t, :],
                                                 op0=ALU.mult, op1=ALU.add)
                m.then_inc(added, 1)

            def two_experts(i, first=False):
                for par in range(2):
                    e = 2 * i + par
                    for tt in range(TT):
                        multiply(TT * e + tt, tt)
                        if tt:
                            accumulate(TT * e + tt - 1, e, tt - 1)
                        elif not (first and par == 0):
                            accumulate(TT * e - 1, e - 1, TT - 1)

            two_experts(0, first=True)
            with dve.Fori(1, N_EXP // 2) as i:
                two_experts(i)
            accumulate(N - 1, N_EXP - 1, TT - 1)

        @block.tensor
        def _(pe):
            for k in range(NT // 4):
                if k >= 2:
                    pe.wait_ge(tr_free, k - 1)
                pe.wait_ge(normed, 4 * k + 4)
                for j in range(4):
                    m = pe.transpose((tr_a, tr_b)[k % 2][:, j * P:(j + 1) * P], o_all[:, 4 * k + j, :], ident[:])
                m.then_inc(tr_done, 1)
            pe.wait_ge(wg_loaded, 16)
            for t in range(NT):
                if t % 4 == 0:
                    pe.wait_ge(tr_free, t // 4 + 1)
                m = pe.matmul(misc[:, t * N_EXP:(t + 1) * N_EXP], xnT_all[:, t * P:(t + 1) * P], wg_sb[:], start=True, stop=True)
            m.then_inc(logits_done, 1)
            pe.wait_ge(chosen_ready, 1)
            pe.wait_ge(consts, 6)
            flat = chosen[:].rearrange("p t e -> p (t e)")
            pe.matmul(misc[:, 0:P], before[:], flat, start=True, stop=True)
            pe.matmul(av[:, 0:P], ones[:], flat, start=True, stop=True).then_inc(places_done, 1)

            def up(n, par, tt):
                for f in range(2):
                    wait(pe, hid_ready, 2 * n + f - 1)
                    for half in range(2):
                        at = half * I_FF + f * P
                        m = pe.matmul(score[:, f, half * 512:(half + 1) * 512], w1_sb[:, par, at:at + P],
                                      xnT_all[:, tt * 512:(tt + 1) * 512], start=True, stop=True)
                    m.then_inc(up_done, 1)

            def down(n, par, tt):
                pe.wait_ge(hid_ready, 2 * n + 2)
                wait(pe, added, n - 1)
                for k in range(4):
                    for f in range(2):
                        m = pe.matmul((tr_a, tr_b)[tt % 2][:, k * P:(k + 1) * P], hid[:, tt % 2, f, k * P:(k + 1) * P],
                                      w2_sb[:, par, f, :], start=f == 0, stop=f == 1)
                m.then_inc(down_done, 1)

            def two_experts(i, first=False):
                for par in range(2):
                    e = 2 * i + par
                    pe.wait_ge(w_loaded, 32 * e + 32)
                    for tt in range(TT):
                        up(TT * e + tt, par, tt)
                        if tt:
                            down(TT * e + tt - 1, par, tt - 1)
                        elif not (first and par == 0):
                            down(TT * e - 1, 1 - par, TT - 1)

            two_experts(0, first=True)
            with pe.Fori(1, N_EXP // 2) as i:
                two_experts(i)
            down(N - 1, 1, TT - 1)

        @block.scalar
        def _(act):
            for k in range(NT // 4):
                act.wait_ge(tr_done, k + 1)
                act.activation(xnT_all[:, 512 * k:512 * k + 512], (tr_a, tr_b)[k % 2][:], ACT.Copy).then_inc(tr_free, 1)
            act.wait_ge(gap_ready, 1)
            act.activation(gate_w[:, 1], gate_w[:, 0], ACT.Exp).then_inc(gate_exp, 1)

            def gelu(n, tt):
                for f in range(2):
                    act.wait_ge(up_done, 2 * n + f + 1)
                    wait(act, down_done, n - 1)
                    act.activation(hid[:, tt % 2, f, :], score[:, f, 0:512], ACT.Gelu).then_inc(gelu_done, 1)

            for tt in range(TT):
                gelu(tt, tt)
            with act.Fori(1, N_EXP) as e:
                for tt in range(TT):
                    gelu(TT * e + tt, tt)


_INS = {
    "x_in": lambda a: a["x"].reshape(B * S, E),
    "ctx_in": lambda a: a["ctx_1024"].reshape(B * C, E),
    "wq_s": lambda a: a["L0_attn_Wq"].T,
    "wk_s": lambda a: a["L0_attn_Wk"].T,
    "wv_s": lambda a: a["L0_attn_Wv"].T,
    "line_in": lambda a: a["L0_attn_bias_table"][::-1].T,
    "wq_c": lambda a: a["L0_xattn_Wq"].T.reshape(PAIRS, P, E).transpose(1, 0, 2),
    "wk_c": lambda a: a["L0_xattn_Wkv"][:, :H * D_CROSS].T.reshape(PAIRS, P, E).transpose(1, 0, 2),
    "wv_c": lambda a: a["L0_xattn_Wkv"][:, H * D_CROSS:],
    "wo_c": lambda a: a["L0_xattn_Wout"].reshape(PAIRS, P, E).transpose(1, 0, 2),
    "wg": lambda a: a["L0_ffn_Wg"].T,
    "w1": lambda a: a["L0_ffn_W1"],
    "w2": lambda a: a["L0_ffn_W2"],
}


def kernel(**inputs):
    import numpy as np
    import concourse.bacc as bacc
    from concourse.bass_utils import run_bass_kernel_spmd

    a = {k: np.asarray(x) for k, x in inputs.items()}
    arrays = {k: np.ascontiguousarray(lay(a)) for k, lay in _INS.items()}
    arrays["ln_rows"] = np.stack([a["L0_attn_ln_gamma"], a["L0_attn_ln_beta"]])
    arrays["ln_cols"] = np.stack([a["L0_xattn_ln_m_g"], a["L0_xattn_ln_m_b"], a["L0_xattn_ln_l_g"], a["L0_xattn_ln_l_b"]], axis=1)
    nc = bacc.Bacc("TRN2", target_bir_lowering=False, num_devices=1)
    aps = {k: nc.dram_tensor(k, x.shape, mybir.dt.from_np(x.dtype), kind="ExternalInput").ap() for k, x in arrays.items()}
    out = nc.dram_tensor("out", (B * S, E), F32, kind="ExternalOutput").ap()
    build(nc, out=out, **aps)
    r = run_bass_kernel_spmd(nc, [arrays], core_ids=[0])
    return r.results[0]["out"].reshape(B, S, E)
```

```python
from contextlib import ExitStack

import concourse.bass as bass
import concourse.mybir as mybir
from concourse.alu_op_type import AluOpType as ALU

F32 = mybir.dt.float32
F32R = mybir.dt.float32r
U32 = mybir.dt.uint32
ACT = mybir.ActivationFunctionType
AX = mybir.AxisListType

P = 128
B, S, E = 8, 256, 128
C = 512
H = 16
D_SELF = E // H
D_CROSS = 64
EPS = 1e-5
QT = S // P
NT = B * QT
KC = C // P
L = C + S
KT = L // P
HALF = L // 2
PAIRS = H // 2
G = H // 4
N_EXP, TOP, I_FF = 8, 2, 256
N_TOK = B * S
CAP = int(N_TOK * TOP * 1.25 / N_EXP)


def wait(engine, sem, value):
    if isinstance(value, int) and value <= 0:
        return
    engine.wait_ge(sem, value)


def build(nc, x_in, ctx_in, wq_s, wk_s, wv_s, line_in, row_masks, ln_rows, ln_cols, wq_c, wk_c, wv_c, wo_c, wg, w1, w2, out):
    es = ExitStack()
    with es:
        def sb(name, shape, dt=F32):
            return es.enter_context(nc.sbuf_tensor(name, shape, dt))

        def sem(name):
            return es.enter_context(nc.semaphore(name))

        x_all = sb("x_all", [P, NT, E])
        o_all = sb("o_all", [P, NT, E])
        xnT_all = sb("xnT_all", [P, N_TOK])
        ident = sb("ident", [P, P])
        stats = sb("stats", [P, B * KC, 6])
        mv = sb("mv", [P, B * KC, 2])
        rstd = sb("rstd", [P, B * KC, 1])
        half_neg = sb("half_neg", [P, B * KC, 1])

        score = es.enter_context(nc.psum_tensor("score", [P, 2, 1024], F32))
        tr_a = es.enter_context(nc.psum_tensor("tr_a", [P, 512], F32))
        tr_b = es.enter_context(nc.psum_tensor("tr_b", [P, 512], F32))
        av = es.enter_context(nc.psum_tensor("av", [P, 512], F32))
        misc = es.enter_context(nc.psum_tensor("misc", [P, 512], F32))

        with ExitStack() as attentions:
            def at(name, shape, dt=F32):
                return attentions.enter_context(nc.sbuf_tensor(name, shape, dt))
            kvT = at("kvT", [P, 2, B, L], F32R)
            mt_all = at("mt_all", [P, 2, H, E], F32R)
            wv_all = at("wv_all", [P, 2, H * D_CROSS], F32R)
            wo_all = at("wo_all", [P, PAIRS, E])
            wq_stack = at("wq_stack", [P, G, P])
            wk_stack = at("wk_stack", [P, G, P])
            v_all = at("v_all", [P, NT, E])
            masks = at("masks", [P, 8])
            gb_rows = at("gb_rows", [P, 2, E])
            gb_cols = at("gb_cols", [P, 4])
            nmax = at("nmax", [P, 4, 4])
            rsum = at("rsum", [P, 4, 4])
            rinv = at("rinv", [P, 4, 4])
            probs = at("probs", [P, 4, 4 * S])
            probsT = at("probsT", [P, 2, 2 * KT * S])
            avT = at("avT", [P, 2, S])
            prepare(nc, es, sb, sem, locals())
            self_attention(nc, sb, sem, locals())
            latents(nc, sb, sem, locals())
            cross_attention(nc, sb, sem, locals())
        experts(nc, sb, sem, locals())


def prepare(nc, es, sb, sem, v):
    x_all, kvT, mt_all, ident, misc, score = (v[k] for k in ("x_all", "kvT", "mt_all", "ident", "misc", "score"))
    stats, mv, rstd, half_neg, xnT_all = (v[k] for k in ("stats", "mv", "rstd", "half_neg", "xnT_all"))
    gb_cols, gb_rows = v["gb_cols"], v["gb_rows"]
    with ExitStack() as own:
        def tmp(name, shape):
            return own.enter_context(nc.sbuf_tensor(name, shape, F32))
        ctx_sb = v["probs"][:].rearrange("p u (t e) -> p (u t) e", e=E)
        xn = v["o_all"]
        kv_full = tmp("kv_full", [P, 2, C])
        wv_full = tmp("wv_full", [P, H * D_CROSS])
        wq_c_sb = tmp("wq_c_sb", [P, PAIRS, E])
        wk_c_sb = tmp("wk_c_sb", [P, PAIRS, E])
        wq_sb = tmp("wq_sb", [P, E])
        wk_sb = tmp("wk_sb", [P, E])
        wv_sb = tmp("wv_sb", [P, E])
        mirror = tmp("mirror", [P, P])
        v_rev = tmp("v_rev", [P, NT, E])
        line = tmp("line", [H, 2 * S])
        bias = v["probsT"][:].rearrange("p a (h k) -> p (a h) k", k=S + P)
        line_dram = nc.dram_tensor("line_dram", (H, 2 * S), F32)
        x_loaded, ctx_loaded, wc_loaded, w_loaded = sem("x_loaded"), sem("ctx_loaded"), sem("wc_loaded"), sem("w_loaded")
        line_loaded, line_made, line_stored, bias_loaded = sem("line_loaded"), sem("line_made"), sem("line_stored"), (sem("bias_a_loaded"), sem("bias_b_loaded"))
        consts, vec, var_ready, rstd_ready = sem("consts"), sem("p_vec"), sem("p_var_ready"), sem("p_rstd_ready")
        mt_hi, mt_lo, wv_hi, kv_hi, kv_lo = sem("mt_hi"), sem("mt_lo"), sem("wv_hi"), sem("kv_hi"), sem("kv_lo")
        x_normed, xt_done, xt_free, stacked = sem("x_normed"), sem("xt_done"), sem("xt_free"), sem("stacked")
        v_done, v_free, rev_done, rev_free, shift_done = sem("v_done"), sem("v_free"), sem("rev_done"), sem("rev_free"), sem("shift_done")
        ctx_normed, mt_done, tr_done, tr_free = sem("ctx_normed"), sem("mt_done"), sem("p_tr_done"), sem("p_tr_free")
        block = own.enter_context(nc.Block())

        @block.sync
        def _(sp):
            sp.dma_start(x_all[:], v["x_in"].rearrange("(t p) e -> p t e", p=P)).then_inc(x_loaded, 16)
            sp.dma_start(line[:, 0:S - 1], v["line_in"]).then_inc(line_loaded, 16)
            sp.dma_start(ctx_sb[:], v["ctx_in"].rearrange("(t p) e -> p t e", p=P)).then_inc(ctx_loaded, 16)
            sp.wait_ge(line_made, 1)
            sp.dma_start(line_dram.ap(), line[:]).then_inc(line_stored, 16)
            sp.wait_ge(line_stored, 16)
            for half in range(2):
                window = bass.AP(line_dram, half * (H // 2) * 2 * S, [[1, P], [2 * S, H // 2], [1, S + P]])
                sp.dma_start(bias[:, half * (H // 2):(half + 1) * (H // 2), :], window).then_inc(bias_loaded[half], 16)
            for half in range(2):
                sp.wait_ge(bias_loaded[half], 16)
            sp.wait_ge(w_loaded, 16 * 8)

        @block.gpsimd
        def _(pool):
            pool.memset(ident[:], 0.0).then_inc(consts, 1)
            pool.memset(mirror[:], 0.0).then_inc(consts, 1)
            pool.memset(half_neg[:], -0.5).then_inc(consts, 1)
            pool.wait_ge(consts, 3)
            pool.affine_select(out=ident[:], in_=ident[:], compare_op=ALU.not_equal, fill=1.0,
                               base=0, pattern=[[-1, P]], channel_multiplier=1).then_inc(consts, 1)
            pool.affine_select(out=mirror[:], in_=mirror[:], compare_op=ALU.not_equal, fill=1.0,
                               base=1 - P, pattern=[[1, P]], channel_multiplier=1).then_inc(consts, 1)
            for k, n in enumerate((NT, B * KC)):
                pool.wait_ge(var_ready, k + 1)
                pool.tensor_scalar(rstd[:, 0:n, :], mv[:, 0:n, 1:2], EPS, 1.0, ALU.add, ALU.mult).then_inc(rstd_ready, 1)
                pool.wait_ge(rstd_ready, 2 * k + 1)
                pool.tensor_tensor(rstd[:, 0:n, :], rstd[:, 0:n, :], half_neg[:, 0:n, :], ALU.pow).then_inc(rstd_ready, 1)

        @block.vector
        def _(dve):
            count = [0]

            def link(ins, hold):
                count[0] += 1
                ins.then_inc(vec, 1)
                if hold:
                    dve.wait_ge(vec, count[0])
                return ins

            dve.wait_ge(line_loaded, 16)
            dve.tensor_copy(line[:, S - 1:2 * S], line[:, S - 2:S - 1].to_broadcast([H, S + 1])).then_inc(line_made, 1)
            dve.wait_ge(x_loaded, 16)
            for t in range(NT):
                link(dve.bn_stats(stats[:, t, :], x_all[:, t, :]), t == NT - 1)
            for t in range(NT):
                last = dve.bn_aggr(mv[:, t, :], stats[:, t, :])
                if t < NT - 1:
                    link(last, False)
            last.then_inc(var_ready, 1)
            dve.wait_ge(rstd_ready, 2)
            for t in range(NT):
                dve.tensor_scalar(xn[:, t, :], x_all[:, t, :], mv[:, t, 0:1], rstd[:, t, :],
                                  ALU.subtract, ALU.mult).then_inc(x_normed, 1)
            dve.wait_ge(w_loaded, 16 * 8)
            for dst, src, by in ((v["wq_stack"], wq_sb, E ** -0.5), (v["wk_stack"], wk_sb, 1.0)):
                dve.tensor_scalar(dst[:].rearrange("p g (j c d) -> p (g j) c d", j=4, c=4),
                                  src[:].rearrange("p (h o d) -> p h o d", o=1, d=D_SELF).to_broadcast([P, H, 4, D_SELF]),
                                  by, None, ALU.mult).then_inc(stacked, 1)
            for k in range(NT // 4):
                dve.wait_ge(rev_done, k + 1)
                dve.tensor_copy(v_rev[:, 4 * k:4 * k + 4, :], (v["tr_a"], v["tr_b"])[k % 2][:].rearrange("p (t e) -> p t e", t=4)).then_inc(rev_free, 1)
            dve.wait_ge(ctx_loaded, 16)
            for t in range(B * KC):
                link(dve.bn_stats(stats[:, t, :], ctx_sb[:, t, :]), t == B * KC - 1)
            for t in range(B * KC):
                last = dve.bn_aggr(mv[:, t, :], stats[:, t, :])
                if t < B * KC - 1:
                    link(last, False)
            last.then_inc(var_ready, 1)
            dve.wait_ge(rstd_ready, 4)
            for t in range(B * KC):
                dve.tensor_scalar(ctx_sb[:, t, :], ctx_sb[:, t, :], mv[:, t, 0:1], rstd[:, t, :],
                                  ALU.subtract, ALU.mult).then_inc(ctx_normed, 1)
            for k in range(2):
                dve.wait_ge(mt_hi, k + 1)
                for o in range(2):
                    m = dve.scalar_tensor_tensor(out=mt_all[:, 1, 8 * k + o:8 * k + 8:2, :],
                                             in0=score[:, k, 512 * o:512 * o + 512].rearrange("p (h e) -> p h e", e=E), scalar=D_CROSS ** -0.5,
                                             in1=mt_all[:, 0, 8 * k + o:8 * k + 8:2, :].bitcast(F32), op0=ALU.mult, op1=ALU.subtract)
                m.then_inc(mt_lo, 1)
            dve.wait_ge(wv_hi, 1)
            dve.tensor_tensor(v["wv_all"][:, 1, :], wv_full[:], v["wv_all"][:, 0, :].bitcast(F32), ALU.subtract)
            for k in range(2 * QT):
                dve.wait_ge(shift_done, k + 1)
                dve.tensor_copy(v["o_all"][:].rearrange("p (b t) (h d) -> p t h b d", t=QT, d=D_SELF)[:, k % 2, (k // 2) * 8:(k // 2) * 8 + 8],
                                score[:, k // 2, (k % 2) * 512:(k % 2) * 512 + 512].rearrange("p (h b d) -> p h b d", h=8, b=B))
            for b in range(B):
                dve.wait_ge(kv_hi, b + 1)
                dve.tensor_tensor(kvT[:, 1, b, 0:C], kv_full[:, b % 2, :], kvT[:, 0, b, 0:C].bitcast(F32), ALU.subtract).then_inc(kv_lo, 1)

        @block.tensor
        def _(pe):
            pe.wait_ge(wc_loaded, 32)
            for h in range(H):
                r = slice(64 * (h % 2), 64 * (h % 2) + 64)
                at = (h % 2) * 512 + (h // 2) % 4 * P
                m = pe.matmul(score[:, h // 8, at:at + P], wq_c_sb[r, h // 2, :], wk_c_sb[r, h // 2, :], start=True, stop=True)
                if h % 8 == 7:
                    m.then_inc(mt_done, 1)
            pe.wait_ge(consts, 4)
            for k in range(NT // 4):
                if k >= 2:
                    pe.wait_ge(xt_free, k - 1)
                pe.wait_ge(x_normed, 4 * k + 4)
                for j in range(4):
                    m = pe.transpose((v["tr_a"], v["tr_b"])[k % 2][:, j * P:(j + 1) * P], xn[:, 4 * k + j, :], ident[:])
                m.then_inc(xt_done, 1)
            pe.wait_ge(w_loaded, 16 * 8)
            for k in range(NT // 4):
                pe.wait_ge(xt_free, NT // 4)
                if k >= 2:
                    pe.wait_ge(v_free, k - 1)
                for j in range(4):
                    t = 4 * k + j
                    m = pe.matmul((v["tr_a"], v["tr_b"])[k % 2][:, j * P:(j + 1) * P], xnT_all[:, t * P:(t + 1) * P], wv_sb[:], start=True, stop=True)
                m.then_inc(v_done, 1)
            pe.wait_ge(consts, 5)
            for k in range(NT // 4):
                pe.wait_ge(v_free, NT // 4)
                if k >= 2:
                    pe.wait_ge(rev_free, k - 1)
                pe.matmul((v["tr_a"], v["tr_b"])[k % 2][:], mirror[:], v["v_all"][:, 4 * k:4 * k + 4, :].rearrange("p t e -> p (t e)"),
                          start=True, stop=True).then_inc(rev_done, 1)
            pe.wait_ge(rev_free, NT // 4)
            pe.wait_ge(mt_lo, 2)
            for half in range(2):
                pe.wait_ge(bias_loaded[half], 16)
                for qt in range(QT):
                    for h in range(8 * half, 8 * half + 8):
                        for kt in range(QT):
                            at = P * (1 - kt) + P * qt
                            m = pe.matmul(score[:, half, qt * 512 + (h % 8) * 64:qt * 512 + (h % 8) * 64 + 64], bias[:, h, at:at + P],
                                          v_rev[:].rearrange("p (b t) e -> p t b e", t=QT)[:, kt, :, h * D_SELF:(h + 1) * D_SELF],
                                          start=kt == 0, stop=kt == 1)
                    m.then_inc(shift_done, 1)
            for b in range(B):
                bank = (misc, v["av"])[b % 2]
                if b >= 2:
                    pe.wait_ge(tr_free, b - 1)
                pe.wait_ge(ctx_normed, KC * (b + 1))
                for k in range(KC):
                    m = pe.transpose(bank[:, k * P:(k + 1) * P], ctx_sb[:, b * KC + k, :], ident[:])
                m.then_inc(tr_done, 1)

        @block.scalar
        def _(act):
            act.dma_start(wq_c_sb[:], v["wq_c"]).then_inc(wc_loaded, 16)
            act.dma_start(wk_c_sb[:], v["wk_c"]).then_inc(wc_loaded, 16)
            act.dma_start(gb_cols[:], v["ln_cols"]).then_inc(w_loaded, 16)
            act.dma_start(gb_rows[:], v["ln_rows"].rearrange("(o k) e -> o k e", o=1).to_broadcast([P, 2, E])).then_inc(w_loaded, 16)
            act.dma_start(wq_sb[:], v["wq_s"]).then_inc(w_loaded, 16)
            act.dma_start(wk_sb[:], v["wk_s"]).then_inc(w_loaded, 16)
            act.dma_start(wv_sb[:], v["wv_s"]).then_inc(w_loaded, 16)
            act.dma_start(v["masks"][:], v["row_masks"]).then_inc(w_loaded, 16)
            act.dma_start(wv_full[:], v["wv_c"]).then_inc(w_loaded, 16)
            act.dma_start(v["wo_all"][:], v["wo_c"]).then_inc(w_loaded, 16)
            for k in range(2):
                act.wait_ge(mt_done, k + 1)
                act.activation(mt_all[:, 0, 8 * k:8 * k + 8, :].rearrange("p (h o) e -> p o h e", o=2),
                               score[:, k, :].rearrange("p (o h e) -> p o h e", o=2, e=E), ACT.Copy,
                               scale=D_CROSS ** -0.5).then_inc(mt_hi, 1)
            for k in range(NT // 4):
                act.wait_ge(xt_done, k + 1)
                act.activation(xnT_all[:, 512 * k:512 * k + 512], (v["tr_a"], v["tr_b"])[k % 2][:], ACT.Copy).then_inc(xt_free, 1)
            for k in range(NT // 4):
                act.wait_ge(v_done, k + 1)
                act.activation(v["v_all"][:, 4 * k:4 * k + 4, :], (v["tr_a"], v["tr_b"])[k % 2][:].rearrange("p (t e) -> p t e", t=4),
                               ACT.Copy).then_inc(v_free, 1)
            act.wait_ge(w_loaded, 16 * 8)
            act.activation(v["wv_all"][:, 0, :], wv_full[:], ACT.Copy).then_inc(wv_hi, 1)
            for b in range(B):
                bank = (misc, v["av"])[b % 2]
                act.wait_ge(tr_done, b + 1)
                if b >= 2:
                    act.wait_ge(kv_lo, b - 1)
                act.activation(kv_full[:, b % 2, :], bank[:], ACT.Identity, scale=gb_cols[:, 0:1],
                               bias=gb_cols[:, 1:2]).then_inc(tr_free, 1)
                act.wait_ge(tr_free, b + 1)
                act.activation(kvT[:, 0, b, 0:C], kv_full[:, b % 2, :], ACT.Copy).then_inc(kv_hi, 1)


def self_attention(nc, sb, sem, v):
    xnT_all, o_all, v_all, ident, masks = (v[k] for k in ("xnT_all", "o_all", "v_all", "ident", "masks"))
    wq_stack, wk_stack = v["wq_stack"], v["wk_stack"]
    score, tr_a, tr_b, av, misc = (v[k] for k in ("score", "tr_a", "tr_b", "av", "misc"))
    nmax, probs, probsT, avT = (v[k] for k in ("nmax", "probs", "probsT", "avT"))
    U = G * QT
    with ExitStack() as own:
        def tmp(name, shape, dt=F32):
            return own.enter_context(nc.sbuf_tensor(name, shape, dt))
        high = tmp("high", [P, 2, S], F32R)
        q_parts = tmp("q_parts", [P, G, S], F32R)
        k_parts = tmp("k_parts", [P, 2, S])
        k_diag = tmp("k_diag", [P, G, 4, S], F32R)
        v_pad = tmp("v_pad", [P, QT, G, 4, 32])
        sum_inv = tmp("sum_inv", [P, QT, 4, 1])
        share = tmp("share", [P, QT, 4, D_SELF])
        qk_done, max_done, exp_done, high_ready, k_ready, kd_ready = (sem("s_" + n) for n in ("qk_done", "max_done", "exp_done", "high_ready", "k_ready", "kd_ready"))
        tr_done, ta_free, tb_free, av_done, avT_ready, v_ready = (sem("s_" + n) for n in ("tr_done", "ta_free", "tb_free", "av_done", "avT_ready", "v_ready"))
        proj_done, out_full, out_free, divided, cleared = (sem("s_" + n) for n in ("proj_done", "out_full", "out_free", "divided", "cleared"))
        block = own.enter_context(nc.Block())

        def known(x):
            return isinstance(x, int)

        @block.tensor
        def _(pe):
            def scores(b, u):
                g, qt, n = u // QT, u % QT, U * b + u
                if qt == 0:
                    pe.wait_ge(kd_ready, G * b + g + 1)
                wait(pe, exp_done, n - 1)
                for j in range(2):
                    m = pe.matmul(score[:, u % 2, j * 512:(j + 1) * 512], q_parts[:, g, qt * P:(qt + 1) * P],
                                  k_diag[:, g, 2 * j:2 * j + 2, :], start=True, stop=True)
                m.then_inc(qk_done, 1)

            def transposes(b, u):
                n = U * b + u
                pe.wait_ge(exp_done, n + 1)
                for half, bank, free in ((0, tr_a, ta_free), (1, tr_b, tb_free)):
                    wait(pe, free, n)
                    for k in range(4):
                        at = half * 512 + k * P
                        m = pe.transpose(bank[:, k * P:(k + 1) * P], probs[:, u % 4, at:at + P], ident[:])
                    m.then_inc(tr_done, 1)

            def attend(b, g):
                n = G * b + g
                pe.wait_ge(ta_free, QT * n + QT)
                pe.wait_ge(tb_free, QT * n + QT)
                wait(pe, avT_ready, n)
                pe.wait_ge(v_ready, n + 1)
                for kt in range(QT):
                    for j in range(4):
                        m = pe.matmul(av[32 * j:32 * j + 32, 0:S], v_pad[:, kt, g, j, :],
                                      probsT[:, g % 2, (2 * j + kt) * S:(2 * j + kt + 1) * S],
                                      start=kt == 0, stop=kt == QT - 1, tile_position=(0, 32 * j))
                m.then_inc(av_done, 1)

            def natural(b, g):
                splits = G * b + G + 3 + g
                wait(pe, k_ready, min(splits, G * B) if known(splits) else splits)
                wait(pe, out_free, G * b + g)
                pe.wait_ge(avT_ready, G * b + g + 1)
                for qt in range(QT):
                    m = pe.transpose(misc[:, qt * P:(qt + 1) * P], avT[:, g % 2, qt * P:(qt + 1) * P], ident[:])
                m.then_inc(out_full, 1)

            def project(b, g):
                wait(pe, k_ready, G * b + g)
                wait(pe, out_free, G * (b - 1) - 2 + g)
                for k, w in enumerate((wq_stack, wk_stack)):
                    m = pe.matmul(misc[:, k * S:(k + 1) * S], w[:, g, :], xnT_all[:, bass.ds(b * S, S)], start=True, stop=True)
                m.then_inc(proj_done, 1)

            def slot(b, u, first=False, last=False):
                if u < U:
                    scores(b, u)
                if u % 2:
                    if not last and u < U:
                        project(b + 1, u // 2)
                else:
                    if u >= 6:
                        natural(b, (u - 6) // 2)
                    elif not first:
                        natural(b - 1, (u + 2) // 2)
                    if u >= 4:
                        if (u - 4) // 2 < G:
                            attend(b, (u - 4) // 2)
                    elif not first:
                        attend(b - 1, (u + 4) // 2)
                if u >= 2:
                    if u - 2 < U:
                        transposes(b, u - 2)
                elif not first:
                    transposes(b - 1, U + u - 2)

            for g in range(G):
                project(0, g)
            for u in range(U):
                slot(0, u, first=True)
            with pe.Fori(1, B - 1) as b:
                for u in range(U):
                    slot(b, u)
            for u in range(U + 5):
                slot(B - 1, u, last=True)

        @block.scalar
        def _(act):
            def exponentials(b, u):
                n = U * b + u
                act.wait_ge(max_done, n + 1)
                if not known(n) or n >= 4:
                    act.wait_ge(tr_done, 2 * n - 6)
                for j in range(4):
                    m = act.activation(probs[:, u % 4, j * S:(j + 1) * S], score[:, u % 2, j * S:(j + 1) * S], ACT.Exp,
                                       bias=nmax[:, u % 4, j:j + 1])
                m.then_inc(exp_done, 1)

            def evacuate_a(b, u):
                n, g, qt = U * b + u, u // QT, u % QT
                act.wait_ge(tr_done, 2 * n + 1)
                wait(act, av_done, G * b + g - 1)
                act.activation(probsT[:, g % 2, 0:4 * S].rearrange("p (k q) -> p k q", k=4)[:, :, qt * P:(qt + 1) * P],
                               tr_a[:].rearrange("p (k q) -> p k q", k=4), ACT.Copy).then_inc(ta_free, 1)

            def evacuate_av(b, g):
                act.wait_ge(av_done, G * b + g + 1)
                wait(act, out_full, G * b + g - 1)
                act.activation(avT[:, g % 2, :], av[:, 0:S], ACT.Copy).then_inc(avT_ready, 1)

            def high_parts(b, g):
                act.wait_ge(proj_done, G * b + g + 1)
                for k in range(2):
                    m = act.activation(high[:, k, :], misc[:, k * S:(k + 1) * S], ACT.Copy, scale=masks[:, 5 + 2 * k:6 + 2 * k])
                m.then_inc(high_ready, 1)

            def slot(b, u, first=False, last=False):
                if u % 2 and u < U and not last:
                    high_parts(b + 1, u // 2)
                if u >= 2:
                    if u - 2 < U:
                        evacuate_a(b, u - 2)
                elif not first:
                    evacuate_a(b - 1, U + u - 2)
                if u % 2 == 0:
                    if u >= 4:
                        if (u - 4) // 2 < G:
                            evacuate_av(b, (u - 4) // 2)
                    elif not first:
                        evacuate_av(b - 1, (u + 4) // 2)
                if u < U:
                    exponentials(b, u)

            for g in range(G):
                high_parts(0, g)
            for u in range(U):
                slot(0, u, first=True)
            with act.Fori(1, B - 1) as b:
                for u in range(U):
                    slot(b, u)
            for u in range(U + 5):
                slot(B - 1, u, last=True)

        @block.vector
        def _(dve):
            def maxima(b, u):
                dve.wait_ge(qk_done, U * b + u + 1)
                dve.tensor_reduce(nmax[:, u % 4, :], score[:, u % 2, :].rearrange("p (j k) -> p j k", j=4),
                                  axis=AX.X, op=ALU.max, negate=True).then_inc(max_done, 1)

            def evacuate_b(b, u):
                n, g, qt = U * b + u, u // QT, u % QT
                dve.wait_ge(tr_done, 2 * n + 2)
                wait(dve, av_done, G * b + g - 1)
                dve.tensor_copy(probsT[:, g % 2, 4 * S:8 * S].rearrange("p (k q) -> p k q", k=4)[:, :, qt * P:(qt + 1) * P],
                                tr_b[:].rearrange("p (k q) -> p k q", k=4)).then_inc(tb_free, 1)

            def split(b, g):
                n = G * b + g
                dve.wait_ge(high_ready, n + 1)
                wait(dve, qk_done, U * (b - 1) + QT * (g + 1))
                dve.scalar_tensor_tensor(out=q_parts[:, g, :], in0=misc[:, 0:S], scalar=masks[:, 4:5], in1=high[:, 0, :].bitcast(F32),
                                         op0=ALU.mult, op1=ALU.add)
                wait(dve, kd_ready, n - 1)
                dve.scalar_tensor_tensor(out=k_parts[:, g % 2, :], in0=misc[:, S:2 * S], scalar=masks[:, 6:7], in1=high[:, 1, :].bitcast(F32),
                                         op0=ALU.mult, op1=ALU.add).then_inc(k_ready, 1)

            def add_output(b, g):
                n = G * b + g
                dve.wait_ge(out_full, n + 1)
                out = misc[:, 0:S].rearrange("p (t j c) -> p t j c", t=QT, j=4)
                dve.reciprocal(sum_inv[:], out[:, :, :, D_SELF:D_SELF + 1]).then_inc(divided, 1)
                dve.wait_ge(divided, 2 * n + 1)
                dve.tensor_tensor(share[:], out[:, :, :, 0:D_SELF], sum_inv[:].to_broadcast([P, QT, 4, D_SELF]), ALU.mult).then_inc(divided, 1)
                dve.wait_ge(divided, 2 * n + 2)
                o = o_all[:, bass.ds(QT * b, QT), g * 32:(g + 1) * 32].rearrange("p t (j c) -> p t j c", c=D_SELF)
                dve.tensor_tensor(o, share[:], o, ALU.add).then_inc(out_free, 1)

            def slot(b, u, first=False, last=False):
                if u < U:
                    maxima(b, u)
                if u % 2:
                    if not last and u < U:
                        split(b + 1, u // 2)
                elif u >= 6:
                    add_output(b, (u - 6) // 2)
                elif not first:
                    add_output(b - 1, (u + 2) // 2)
                if u >= 2:
                    if u - 2 < U:
                        evacuate_b(b, u - 2)
                elif not first:
                    evacuate_b(b - 1, U + u - 2)

            for g in range(G):
                split(0, g)
            for u in range(U):
                slot(0, u, first=True)
            with dve.Fori(1, B - 1) as b:
                for u in range(U):
                    slot(b, u)
            for u in range(U + 5):
                slot(B - 1, u, last=True)

        @block.gpsimd
        def _(pool):
            def stage_values(b, g):
                wait(pool, av_done, G * (b - 1) + g + 1)
                pool.tensor_copy(v_pad[:, :, g, :, 0:D_SELF],
                                 v_all[:, bass.ds(QT * b, QT), g * 32:(g + 1) * 32].rearrange("p t (j c) -> p t j c", c=D_SELF)).then_inc(v_ready, 1)

            def spread_keys(b, g):
                pool.wait_ge(k_ready, G * b + g + 1)
                pool.tensor_tensor(k_diag[:, g, :, :],
                                   k_parts[:, g % 2:g % 2 + 1, :].to_broadcast([P, 4, S]),
                                   masks[:, 0:4].rearrange("p (h o) -> p h o", o=1).to_broadcast([P, 4, S]),
                                   ALU.mult).then_inc(kd_ready, 1)

            def batch(b):
                stage_values(b, 2)
                spread_keys(b + 1, 0)
                stage_values(b, 3)
                spread_keys(b + 1, 1)
                stage_values(b + 1, 0)
                spread_keys(b + 1, 2)
                stage_values(b + 1, 1)
                spread_keys(b + 1, 3)

            pool.memset(v_pad[:], 0.0).then_inc(cleared, 1)
            pool.wait_ge(cleared, 1)
            pool.memset(v_pad[:, :, :, :, D_SELF:D_SELF + 1], 1.0).then_inc(cleared, 1)
            for g in range(G):
                spread_keys(0, g)
            stage_values(0, 0)
            stage_values(0, 1)
            batch(0)
            with pool.Fori(1, B - 1) as b:
                batch(b)
            stage_values(B - 1, 2)
            stage_values(B - 1, 3)


def norm_stats(dve, step, x, n, stats, mv, ready):
    for t in range(n):
        m = dve.bn_stats(stats[:, t, :], x[:, t, :])
    step(m)
    for t in range(n):
        m = dve.bn_aggr(mv[:, t, :], stats[:, t, :])
    m.then_inc(ready, 1)


def latents(nc, sb, sem, v):
    x_all, o_all, kvT, ident, gb_rows, gb_cols = (v[k] for k in ("x_all", "o_all", "kvT", "ident", "gb_rows", "gb_cols"))
    stats, mv, rstd, half_neg = (v[k] for k in ("stats", "mv", "rstd", "half_neg"))
    banks = (v["misc"], v["av"])
    with ExitStack() as own:
        full = own.enter_context(nc.sbuf_tensor("full", [P, NT // 4, 512], F32))
        step_done, var_ready, rstd_ready, latent_ready, tr_done, tr_free, hi_ready = (
            sem("l_" + n) for n in ("step_done", "var_ready", "rstd_ready", "latent_ready", "tr_done", "tr_free", "hi_ready"))
        block = own.enter_context(nc.Block())

        @block.vector
        def _(dve):
            steps = [0]

            def step(m):
                steps[0] += 1
                m.then_inc(step_done, 1)
                dve.wait_ge(step_done, steps[0])

            def normalized(dst, src, k, last=None):
                dve.wait_ge(rstd_ready, 2 * k + 2)
                for t in range(NT):
                    m = dve.tensor_scalar(dst[:, t, :], src[:, t, :], mv[:, t, 0:1], rstd[:, t, :], ALU.subtract, ALU.mult)
                    if last is not None:
                        m.then_inc(last, 1)
                if last is None:
                    step(m)

            def row(k):
                return gb_rows[:, k:k + 1, :].to_broadcast([P, NT, E])

            norm_stats(dve, step, o_all, NT, stats, mv, var_ready)
            normalized(o_all, o_all, 0)
            step(dve.tensor_tensor(o_all[:], o_all[:], row(0), ALU.mult))
            step(dve.tensor_tensor(o_all[:], o_all[:], row(1), ALU.add))
            step(dve.tensor_tensor(x_all[:], x_all[:], o_all[:], ALU.add))
            norm_stats(dve, step, x_all, NT, stats, mv, var_ready)
            normalized(o_all, x_all, 1)
            norm_stats(dve, step, o_all, NT, stats, mv, var_ready)
            normalized(o_all, o_all, 2, latent_ready)
            for k in range(NT // 4):
                dve.wait_ge(hi_ready, k + 1)
                dve.tensor_tensor(kvT[:, 1, 2 * k:2 * k + 2, C:L], full[:, k, :].rearrange("p (b q) -> p b q", b=2),
                                  kvT[:, 0, 2 * k:2 * k + 2, C:L].bitcast(F32), ALU.subtract)

        @block.gpsimd
        def _(pool):
            for k in range(3):
                inverse_roots(pool, v, NT, k, var_ready, rstd_ready)

        @block.tensor
        def _(pe):
            for k in range(NT // 4):
                pe.wait_ge(latent_ready, 4 * k + 4)
                if k >= 2:
                    pe.wait_ge(tr_free, k - 1)
                for j in range(4):
                    m = pe.transpose(banks[k % 2][:, j * P:(j + 1) * P], o_all[:, 4 * k + j, :], ident[:])
                m.then_inc(tr_done, 1)

        @block.scalar
        def _(act):
            for k in range(NT // 4):
                act.wait_ge(tr_done, k + 1)
                act.activation(full[:, k, :], banks[k % 2][:], ACT.Identity,
                               scale=gb_cols[:, 2:3], bias=gb_cols[:, 3:4]).then_inc(tr_free, 1)
                act.wait_ge(tr_free, k + 1)
                act.activation(kvT[:, 0, 2 * k:2 * k + 2, C:L], full[:, k, :].rearrange("p (b q) -> p b q", b=2), ACT.Copy).then_inc(hi_ready, 1)


def inverse_roots(pool, v, n, k, var_ready, rstd_ready):
    mv, rstd, half_neg = v["mv"], v["rstd"], v["half_neg"]
    pool.wait_ge(var_ready, k + 1)
    pool.tensor_scalar(rstd[:, 0:n, :], mv[:, 0:n, 1:2], EPS, 1.0, ALU.add, ALU.mult).then_inc(rstd_ready, 1)
    pool.wait_ge(rstd_ready, 2 * k + 1)
    pool.tensor_tensor(rstd[:, 0:n, :], rstd[:, 0:n, :], half_neg[:, 0:n, :], ALU.pow).then_inc(rstd_ready, 1)


def cross_attention(nc, sb, sem, v):
    x_all, kvT, ident, mt_all, wv_all, wo_all = (v[k] for k in ("x_all", "kvT", "ident", "mt_all", "wv_all", "wo_all"))
    score, tr_a, tr_b, av, misc = (v[k] for k in ("score", "tr_a", "tr_b", "av", "misc"))
    nmax, rsum, rinv, probs, probsT, avT = (v[k] for k in ("nmax", "rsum", "rinv", "probs", "probsT", "avT"))
    IT = B * PAIRS // 2
    ITB = PAIRS // 2
    U = 4
    HI_LO = ((0, 0), (0, 1), (1, 0))
    with ExitStack() as own:
        def tmp(name, shape, dt=F32):
            return own.enter_context(nc.sbuf_tensor(name, shape, dt))
        mt = tmp("mt", [P, 2, 2, 2, E], F32R)
        kv = tmp("kv", [P, 2, L], F32R)
        aT = tmp("aT", [P, 2, 2, 2, S], F32R)
        val = tmp("val", [P, 2, KT, P])
        qk_done, max_done, exp_done, inv_done, p_ready = (sem("c_" + n) for n in ("qk_done", "max_done", "exp_done", "inv_done", "p_ready"))
        tr_done, ta_free, tb_free, av_done, avT_ready = (sem("c_" + n) for n in ("tr_done", "ta_free", "tb_free", "av_done", "avT_ready"))
        misc_full, misc_free, out_added, q_split = (sem("c_" + n) for n in ("misc_full", "misc_free", "out_added", "q_split"))
        weights_staged, tokens_staged, norm_called = (sem("c_" + n) for n in ("weights_staged", "tokens_staged", "norm_called"))
        block = own.enter_context(nc.Block())

        OUT0, Q1, V01, V23, OUT1, V45, Q2 = range(7)
        VALUES = (V01, V23, V45)
        R = 7

        def use(i, k):
            if isinstance(i, int) and i == 0:
                return 1 + (Q1, V01, V23, V45, Q2).index(k)
            return R * i + k - 1

        def use_q(i, j):
            if j:
                return use(i, Q1)
            return 0 if isinstance(i, int) and i == 0 else use(i - 1, Q2)

        def act_uses(i, k):
            return 5 * i + 1 + (Q1, V01, V23, V45, Q2).index(k)

        def batch_slice(i, part, at, n):
            return kvT[:, part, bass.ds(i // ITB, 1), at:at + n]

        @block.tensor
        def _(pe):
            def scores(i, j, u):
                p, h, qt = 2 * i + j, u // 2, u % 2
                n = U * p + u
                if u == 0:
                    pe.wait_ge(q_split, p + 1)
                wait(pe, exp_done, n - 1)
                for half in range(2):
                    for k, (a, b) in enumerate(HI_LO):
                        m = pe.matmul(score[:, u % 2, half * 512:half * 512 + HALF], aT[:, j, a, h, qt * P:(qt + 1) * P],
                                      batch_slice(i, b, half * HALF, HALF), start=k == 0, stop=k == 2)
                m.then_inc(qk_done, 1)

            def transposes(p, u):
                n = U * p + u
                pe.wait_ge(p_ready, n + 1)
                for half, bank, free in ((0, tr_a, ta_free), (1, tr_b, tb_free)):
                    wait(pe, free, n)
                    for k in range(KT // 2):
                        at = half * HALF + k * P
                        m = pe.transpose(bank[:, k * P:(k + 1) * P], probs[:, u % 4, at:at + P], ident[:])
                    m.then_inc(tr_done, 1)

            def attend(i, j):
                p = 2 * i + j
                pe.wait_ge(ta_free, U * p + U)
                pe.wait_ge(tb_free, U * p + U)
                pe.wait_ge(misc_free, act_uses(i, V45) + 1)
                wait(pe, avT_ready, p)
                for kt in range(KT):
                    for h in range(2):
                        m = pe.matmul(av[64 * h:64 * h + 64, 0:S], val[:, j, kt, 64 * h:64 * h + 64],
                                      probsT[:, j, (KT * h + kt) * S:(KT * h + kt + 1) * S],
                                      start=kt == 0, stop=kt == KT - 1, tile_position=(0, 64 * h))
                m.then_inc(av_done, 1)

            def queries(i, j, uses, outs):
                wait(pe, misc_free, uses)
                wait(pe, q_split, 2 * i + j)
                wait(pe, out_added, outs)
                pe.wait_ge(weights_staged, 2 * i + j + 1)
                for h in range(2):
                    for k, (a, b) in enumerate(HI_LO):
                        m = pe.matmul(misc[:, h * S:(h + 1) * S], mt[:, j, a, h, :], batch_slice(i, b, C, S),
                                      start=k == 0, stop=k == 2)
                m.then_inc(misc_full, 1)

            def values(i, k, first=False):
                wait(pe, misc_free, act_uses(i, VALUES[k]))
                if k == 0:
                    wait(pe, q_split, 2 * i + 2)
                    pe.wait_ge(tokens_staged, 16 * (i // ITB) + 16)
                if k == 2 and not first:
                    pe.wait_ge(out_added, 2 * i)
                for t in range(2):
                    for n, (a, b) in enumerate(HI_LO):
                        kt = 2 * k + t
                        m = pe.matmul(misc[:, t * 256:(t + 1) * 256], kv[:, a, kt * P:(kt + 1) * P],
                                      wv_all[:, b, bass.ds((i % ITB) * 256, 256)], start=n == 0, stop=n == 2)
                m.then_inc(misc_full, 1)

            def project_out(i, j):
                pe.wait_ge(avT_ready, 2 * i + j + 1)
                for qt in range(QT):
                    m = pe.matmul(misc[:, qt * P:(qt + 1) * P], avT[:, j, qt * P:(qt + 1) * P],
                                  wo_all[:, bass.ds((i % ITB) * 2 + j, 1), :], start=True, stop=True)
                m.then_inc(misc_full, 1)

            def iteration(i, first=False, last=False):
                before = i - 1
                for j in range(2):
                    p = 2 * i + j
                    none_before = first and j == 0
                    scores(i, j, 0)
                    if not none_before:
                        transposes(p - 1, 2)
                    if not first:
                        wait(pe, misc_free, act_uses(i, V45 if j else Q1))
                        wait(pe, q_split, p + 1)
                        project_out(before, j)
                    scores(i, j, 1)
                    if not none_before:
                        transposes(p - 1, 3)
                    if j:
                        values(i, 2, first)
                    else:
                        queries(i, 1, act_uses(i, Q1), 2 * i - 1)
                    scores(i, j, 2)
                    if j and not last:
                        queries(i + 1, 0, act_uses(i, Q2), 2 * i)
                    if not none_before:
                        attend(i if j else before, 1 - j)
                    transposes(p, 0)
                    if not j:
                        values(i, 0, first)
                    scores(i, j, 3)
                    transposes(p, 1)
                    if not j:
                        values(i, 1, first)

            queries(0, 0, 0, 0)
            iteration(0, first=True)
            with pe.Fori(1, IT - 1) as i:
                iteration(i)
            iteration(IT - 1, last=True)
            p = 2 * IT - 1
            transposes(p, 2)
            transposes(p, 3)
            project_out(IT - 1, 0)
            attend(IT - 1, 1)
            pe.wait_ge(out_added, p)
            project_out(IT - 1, 1)

        @block.scalar
        def _(act):
            def exponentials(p, u):
                n = U * p + u
                act.wait_ge(max_done, n + 1)
                if not isinstance(n, int) or n >= 4:
                    act.wait_ge(tr_done, 2 * n - 6)
                act.activation(probs[:, u, 0:L].rearrange("p (a k) -> p a k", a=2),
                               score[:, u % 2, :].rearrange("p (a k) -> p a k", a=2)[:, :, 0:HALF], ACT.Exp,
                               bias=nmax[:, u, 0:1], accum_out=rsum[:, u, 0:1]).then_inc(exp_done, 1)

            def evacuate_a(p, par, u):
                n, h, qt = U * p + u, u // 2, u % 2
                act.wait_ge(tr_done, 2 * n + 1)
                wait(act, av_done, p - 1)
                act.activation(probsT[:, par, KT * h * S:(KT * h + 3) * S].rearrange("p (k q) -> p k q", k=3)[:, :, qt * P:(qt + 1) * P],
                               tr_a[:, 0:HALF].rearrange("p (k q) -> p k q", k=3), ACT.Copy).then_inc(ta_free, 1)

            def evacuate_av(p, par):
                act.wait_ge(av_done, p + 1)
                wait(act, out_added, p - 1)
                act.activation(avT[:, par, :], av[:, 0:S], ACT.Copy).then_inc(avT_ready, 1)

            def evacuate_values(i, k):
                act.wait_ge(misc_full, use(i, VALUES[k]) + 1)
                wait(act, av_done, 2 * i)
                act.activation(val[:, :, 2 * k:2 * k + 2, :].rearrange("p j t c -> p t j c"),
                               misc[:].rearrange("p (t j c) -> p t j c", t=2, j=2), ACT.Copy).then_inc(misc_free, 1)

            def evacuate_queries(i, j):
                act.wait_ge(misc_full, use_q(i, j) + 1)
                wait(act, qk_done, U * (2 * i + j - 1))
                act.activation(aT[:, j, 0, :, :], misc[:].rearrange("p (h q) -> p h q", h=2), ACT.Copy).then_inc(misc_free, 1)

            def stage_weights(i, j):
                act.activation(mt[:, j].rearrange("p a h e -> p a (h e)"),
                               mt_all[:, :, bass.ds((i % ITB) * 4 + 2 * j, 2), :].rearrange("p a h e -> p a (h e)").bitcast(F32),
                               ACT.Copy).then_inc(weights_staged, 1)

            def iteration(i, first=False, last=False):
                for j in range(2):
                    p = 2 * i + j
                    none_before = first and j == 0
                    if not none_before:
                        evacuate_a(p - 1, 1 - j, 2)
                    exponentials(p, 0)
                    if not none_before:
                        evacuate_a(p - 1, 1 - j, 3)
                    exponentials(p, 1)
                    if j:
                        evacuate_values(i, 2)
                        if not last:
                            evacuate_queries(i + 1, 0)
                            stage_weights(i + 2, 0)
                    else:
                        evacuate_queries(i, 1)
                        if not last:
                            stage_weights(i + 1, 1)
                    exponentials(p, 2)
                    if not none_before:
                        evacuate_av(p - 1, 1 - j)
                    evacuate_a(p, j, 0)
                    if not j:
                        evacuate_values(i, 0)
                    evacuate_a(p, j, 1)
                    exponentials(p, 3)
                    if not j:
                        evacuate_values(i, 1)

            stage_weights(0, 0)
            stage_weights(0, 1)
            evacuate_queries(0, 0)
            stage_weights(1, 0)
            iteration(0, first=True)
            with act.Fori(1, IT - 1) as i:
                iteration(i)
            iteration(IT - 1, last=True)
            p = 2 * IT - 1
            evacuate_a(p, 1, 2)
            evacuate_a(p, 1, 3)
            evacuate_av(p, 1)

        @block.vector
        def _(dve):
            def maxima(p, u):
                dve.wait_ge(qk_done, U * p + u + 1)
                dve.tensor_reduce(nmax[:, u, 0:1], score[:, u % 2, :].rearrange("p (a k) -> p a k", a=2)[:, :, 0:HALF],
                                  axis=AX.XY, op=ALU.max, negate=True).then_inc(max_done, 1)

            def evacuate_b(p, par, u):
                n, h, qt = U * p + u, u // 2, u % 2
                dve.wait_ge(tr_done, 2 * n + 2)
                wait(dve, av_done, p - 1)
                dve.tensor_copy(probsT[:, par, (KT * h + 3) * S:(KT * h + 6) * S].rearrange("p (k q) -> p k q", k=3)[:, :, qt * P:(qt + 1) * P],
                                tr_b[:, 0:HALF].rearrange("p (k q) -> p k q", k=3)).then_inc(tb_free, 1)

            def invert(p, u):
                n = U * p + u
                dve.wait_ge(exp_done, n + 1)
                wait(dve, p_ready, n - 3)
                dve.reciprocal(rinv[:, u, 0:1], rsum[:, u, 0:1]).then_inc(inv_done, 1)

            def split_queries(i, j, evacuated):
                dve.wait_ge(misc_free, evacuated)
                dve.tensor_tensor(aT[:, j, 1, :, :], misc[:].rearrange("p (h q) -> p h q", h=2), aT[:, j, 0, :, :].bitcast(F32),
                                  ALU.subtract).then_inc(q_split, 1)

            def add_output(i, n, at):
                dve.wait_ge(misc_full, at + 1)
                wait(dve, out_added, n)
                x = x_all[:, bass.ds((i // ITB) * QT, QT), :]
                dve.tensor_tensor(x, misc[:, 0:S].rearrange("p (t e) -> p t e", t=QT), x, ALU.add).then_inc(out_added, 1)

            def iteration(i, first=False, last=False):
                for j in range(2):
                    p = 2 * i + j
                    none_before = first and j == 0
                    maxima(p, 0)
                    if not none_before:
                        invert(p - 1, 3)
                        evacuate_b(p - 1, 1 - j, 2)
                    if not first:
                        add_output(i - 1, p - 2, use(i, OUT1 if j else OUT0))
                    maxima(p, 1)
                    invert(p, 0)
                    if not none_before:
                        evacuate_b(p - 1, 1 - j, 3)
                    maxima(p, 2)
                    invert(p, 1)
                    if not j:
                        split_queries(i, 1, act_uses(i, Q1) + 1)
                    elif not last:
                        split_queries(i + 1, 0, act_uses(i, Q2) + 1)
                    invert(p, 2)
                    evacuate_b(p, j, 0)
                    maxima(p, 3)
                    evacuate_b(p, j, 1)

            split_queries(0, 0, 1)
            iteration(0, first=True)
            with dve.Fori(1, IT - 1) as i:
                iteration(i)
            iteration(IT - 1, last=True)
            p = 2 * IT - 1
            evacuate_b(p, 1, 2)
            invert(p, 3)
            evacuate_b(p, 1, 3)
            add_output(IT - 1, p - 1, use(IT - 1, V45) + 1)
            add_output(IT - 1, p, use(IT - 1, V45) + 2)

        @block.gpsimd
        def _(pool):
            def divide(p, u):
                n = U * p + u
                pool.wait_ge(inv_done, n + 1)
                pool.sem_inc(norm_called, 1)
                pool.tensor_scalar(probs[:, u, 0:L], probs[:, u, 0:L], rinv[:, u, 0:1], 1.0, ALU.mult, ALU.mult).then_inc(p_ready, 1)

            def batch(b, first=False):
                if not first:
                    pool.wait_ge(misc_full, use(ITB * b - 1, V45) + 1)
                pool.dma_start(kv[:], kvT[:, :, bass.ds(b, 1), :].rearrange("p a o l -> p a (o l)")).then_inc(tokens_staged, 16)
                for p in range(PAIRS):
                    for u in range(U):
                        divide(PAIRS * b + p, u)

            batch(0, first=True)
            with pool.Fori(1, B) as b:
                batch(b)


def experts(nc, sb, sem, v):
    x_all, o_all, xnT_all, ident = (v[k] for k in ("x_all", "o_all", "xnT_all", "ident"))
    stats, mv, rstd, half_neg = (v[k] for k in ("stats", "mv", "rstd", "half_neg"))
    misc, av, tr_a, tr_b, score = (v[k] for k in ("misc", "av", "tr_a", "tr_b", "score"))
    TT = N_TOK // 512
    with ExitStack() as own:
        def tmp(name, shape, dt=F32):
            return own.enter_context(nc.sbuf_tensor(name, shape, dt))
        wg_sb = tmp("wg_sb", [P, N_EXP])
        w1_sb = tmp("w1_sb", [P, 2, 2 * I_FF])
        w1_parts = tmp("w1_parts", [P, 2, 2, 2 * I_FF], F32R)
        xnT = tmp("xnT_parts", [P, 2, N_TOK], F32R)
        w2_sb = tmp("w2_sb", [P, 2, 2, E])
        hid = tmp("hid", [P, 2, 2, 512])
        before = tmp("before", [P, P])
        ones = tmp("ones", [P, P])
        iota_e = tmp("iota_e", [P, NT, N_EXP])
        carry_on = tmp("carry_on", [P, N_EXP, NT])
        logits = tmp("logits", [P, NT, N_EXP])
        top_v = tmp("top_v", [P, NT, 8])
        top_i = tmp("top_i", [P, NT, 8], U32)
        top_f = tmp("top_f", [P, NT, 8])
        pick = tmp("pick", [P, 2, NT, N_EXP])
        chosen = tmp("chosen", [P, NT, N_EXP])
        gate_w = tmp("gate_w", [P, 4, NT, 1])
        totals = tmp("totals", [P, N_EXP, NT])
        running = tmp("running", [P, N_EXP, NT])
        place = tmp("place", [P, NT, N_EXP])
        gates = tmp("gates", [P, NT, N_EXP])
        step_done, var_ready, rstd_ready, normed, tr_done, tr_free = (
            sem("e_" + n) for n in ("step_done", "var_ready", "rstd_ready", "normed", "tr_done", "tr_free"))
        consts, w1_hi, w1_lo, x_hi, x_lo, logits_done, chosen_ready, places_done, gap_ready, gate_exp, wg_loaded, w_loaded = (
            sem("e_" + n) for n in ("consts", "w1_hi", "w1_lo", "x_hi", "x_lo", "logits_done", "chosen_ready", "places_done", "gap_ready", "gate_exp", "wg_loaded", "w_loaded"))
        up_done, gelu_done, hid_ready, down_done, added, stored = (
            sem("e_" + n) for n in ("up_done", "gelu_done", "hid_ready", "down_done", "added", "stored"))
        block = own.enter_context(nc.Block())
        N = N_EXP * TT

        @block.sync
        def _(sp):
            sp.dma_start(wg_sb[:], v["wg"]).then_inc(wg_loaded, 16)

            def load(e, par):
                sp.dma_start(w1_sb[:, par, :], v["w1"][e]).then_inc(w_loaded, 16)
                sp.dma_start(w2_sb[:, par], v["w2"][e].rearrange("(k p) e -> p k e", p=P)).then_inc(w_loaded, 16)
                sp.wait_ge(w_loaded, 32 * e + 32)

            for e in range(N_EXP):
                wait(sp, down_done, TT * (e - 1))
                wait(sp, w1_lo, e - 1)
                load(e, e % 2)
            for t in range(0, NT, 4):
                sp.wait_ge(added, N - TT + t // 4 + 1)
                sp.dma_start(v["out"].rearrange("(t p) e -> p t e", p=P)[:, t:t + 4, :], x_all[:, t:t + 4, :]).then_inc(stored, 16)
            sp.wait_ge(stored, 16 * NT // 4)

        @block.gpsimd
        def _(pool):
            pool.memset(ones[:], 1.0).then_inc(consts, 1)
            pool.memset(before[:], 1.0).then_inc(consts, 1)
            pool.memset(carry_on[:], 1.0).then_inc(consts, 1)
            pool.iota(iota_e[:], pattern=[[0, NT], [1, N_EXP]], base=0, channel_multiplier=0,
                      allow_small_or_imprecise_dtypes=True).then_inc(consts, 1)
            pool.wait_ge(consts, 4)
            pool.affine_select(out=before[:], in_=before[:], compare_op=ALU.is_ge, fill=0.0, base=-1,
                               pattern=[[1, P]], channel_multiplier=-1).then_inc(consts, 1)
            pool.memset(carry_on[:, :, 0:1], 0.0).then_inc(consts, 1)
            inverse_roots(pool, v, NT, 0, var_ready, rstd_ready)
            for e in range(N_EXP):
                pool.wait_ge(w1_hi, e + 1)
                pool.tensor_tensor(w1_parts[:, e % 2, 1, :], w1_sb[:, e % 2, :], w1_parts[:, e % 2, 0, :].bitcast(F32),
                                   ALU.subtract).then_inc(w1_lo, 1)

        @block.vector
        def _(dve):
            steps = [0]

            def step(m):
                steps[0] += 1
                m.then_inc(step_done, 1)
                dve.wait_ge(step_done, steps[0])

            norm_stats(dve, step, x_all, NT, stats, mv, var_ready)
            dve.wait_ge(rstd_ready, 2)
            for t in range(NT):
                dve.tensor_scalar(o_all[:, t, :], x_all[:, t, :], mv[:, t, 0:1], rstd[:, t, :],
                                  ALU.subtract, ALU.mult).then_inc(normed, 1)
            for k in range(NT // 4):
                dve.wait_ge(x_hi, k + 1)
                dve.tensor_tensor(xnT[:, 1, 512 * k:512 * k + 512], xnT_all[:, 512 * k:512 * k + 512],
                                  xnT[:, 0, 512 * k:512 * k + 512].bitcast(F32), ALU.subtract).then_inc(x_lo, 1)
            dve.wait_ge(logits_done, 1)
            step(dve.tensor_copy(logits[:], misc[:, 0:NT * N_EXP].rearrange("p (t e) -> p t e", e=N_EXP)))
            for t in range(NT):
                m = dve.max(top_v[:, t, :], logits[:, t, :])
            step(m)
            for t in range(NT):
                m = dve.max_index(top_i[:, t, :], top_v[:, t, :], logits[:, t, :])
            step(m)
            step(dve.tensor_copy(top_f[:], top_i[:]))
            dve.wait_ge(consts, 6)
            for k in range(TOP):
                m = dve.tensor_tensor(pick[:, k], iota_e[:], top_f[:, :, k:k + 1].to_broadcast([P, NT, N_EXP]), ALU.is_equal)
            step(m)
            dve.tensor_tensor(chosen[:], pick[:, 0], pick[:, 1], ALU.add).then_inc(chosen_ready, 1)
            dve.tensor_tensor(gate_w[:, 0], top_v[:, :, 1:2], top_v[:, :, 0:1], ALU.subtract).then_inc(gap_ready, 1)
            dve.wait_ge(gate_exp, 1)
            step(dve.tensor_scalar(gate_w[:, 2], gate_w[:, 1], 1.0, None, ALU.add))
            step(dve.reciprocal(gate_w[:, 3], gate_w[:, 2]))
            step(dve.tensor_tensor(gate_w[:, 1], gate_w[:, 1], gate_w[:, 3], ALU.mult))
            m = dve.tensor_tensor(pick[:, 0], pick[:, 0], gate_w[:, 3].to_broadcast([P, NT, N_EXP]), ALU.mult)
            m = dve.tensor_tensor(pick[:, 1], pick[:, 1], gate_w[:, 1].to_broadcast([P, NT, N_EXP]), ALU.mult)
            step(m)
            step(dve.tensor_tensor(gates[:], pick[:, 0], pick[:, 1], ALU.add))
            dve.wait_ge(places_done, 1)
            step(dve.tensor_copy(totals[:], av[:, 0:P].rearrange("p (t e) -> p e t", e=N_EXP)))
            step(dve.tensor_tensor_scan(running[:].rearrange("p e t -> p (e t)"), carry_on[:].rearrange("p e t -> p (e t)"),
                                        totals[:].rearrange("p e t -> p (e t)"), 0.0, ALU.mult, ALU.add))
            step(dve.tensor_tensor(running[:], running[:], totals[:], ALU.subtract))
            step(dve.tensor_tensor(place[:], misc[:, 0:P].rearrange("p (t e) -> p t e", e=N_EXP),
                                   running[:].rearrange("p e t -> p t e"), ALU.add))
            step(dve.tensor_scalar(place[:], place[:], float(CAP), None, ALU.is_lt))
            step(dve.tensor_tensor(gates[:], gates[:], place[:], ALU.mult))

            def multiply(n, tt):
                for f in range(2):
                    dve.wait_ge(gelu_done, 2 * n + f + 1)
                    dve.tensor_tensor(hid[:, tt % 2, f, :], hid[:, tt % 2, f, :], score[:, f, 512:1024],
                                      ALU.mult).then_inc(hid_ready, 1)

            def accumulate(n, e, tt):
                dve.wait_ge(down_done, n + 1)
                wait(dve, added, n - TT + 1)
                for k in range(4):
                    t = 4 * tt + k
                    m = dve.scalar_tensor_tensor(out=x_all[:, t, :], in0=(tr_a, tr_b)[tt % 2][:, k * P:(k + 1) * P],
                                                 scalar=gates[:, t, bass.ds(e, 1)], in1=x_all[:, t, :],
                                                 op0=ALU.mult, op1=ALU.add)
                m.then_inc(added, 1)

            def two_experts(i, first=False):
                for par in range(2):
                    e = 2 * i + par
                    for tt in range(TT):
                        multiply(TT * e + tt, tt)
                        if tt:
                            accumulate(TT * e + tt - 1, e, tt - 1)
                        elif not (first and par == 0):
                            accumulate(TT * e - 1, e - 1, TT - 1)

            two_experts(0, first=True)
            with dve.Fori(1, N_EXP // 2) as i:
                two_experts(i)
            accumulate(N - 1, N_EXP - 1, TT - 1)

        @block.tensor
        def _(pe):
            for k in range(NT // 4):
                if k >= 2:
                    pe.wait_ge(tr_free, k - 1)
                pe.wait_ge(normed, 4 * k + 4)
                for j in range(4):
                    m = pe.transpose((tr_a, tr_b)[k % 2][:, j * P:(j + 1) * P], o_all[:, 4 * k + j, :], ident[:])
                m.then_inc(tr_done, 1)
            pe.wait_ge(wg_loaded, 16)
            for t in range(NT):
                if t % 4 == 0:
                    pe.wait_ge(tr_free, t // 4 + 1)
                m = pe.matmul(misc[:, t * N_EXP:(t + 1) * N_EXP], xnT_all[:, t * P:(t + 1) * P], wg_sb[:], start=True, stop=True)
            m.then_inc(logits_done, 1)
            pe.wait_ge(chosen_ready, 1)
            pe.wait_ge(consts, 6)
            flat = chosen[:].rearrange("p t e -> p (t e)")
            pe.matmul(misc[:, 0:P], before[:], flat, start=True, stop=True)
            pe.matmul(av[:, 0:P], ones[:], flat, start=True, stop=True).then_inc(places_done, 1)

            def up(n, par, tt):
                for f in range(2):
                    wait(pe, hid_ready, 2 * n + f - 1)
                    for half in range(2):
                        at = half * I_FF + f * P
                        for k, (a, b) in enumerate(((0, 0), (0, 1), (1, 0))):
                            m = pe.matmul(score[:, f, half * 512:(half + 1) * 512], w1_parts[:, par, a, at:at + P],
                                          xnT[:, b, tt * 512:(tt + 1) * 512], start=k == 0, stop=k == 2)
                    m.then_inc(up_done, 1)

            def down(n, par, tt):
                pe.wait_ge(hid_ready, 2 * n + 2)
                wait(pe, added, n - 1)
                for k in range(4):
                    for f in range(2):
                        m = pe.matmul((tr_a, tr_b)[tt % 2][:, k * P:(k + 1) * P], hid[:, tt % 2, f, k * P:(k + 1) * P],
                                      w2_sb[:, par, f, :], start=f == 0, stop=f == 1)
                m.then_inc(down_done, 1)

            def two_experts(i, first=False):
                for par in range(2):
                    e = 2 * i + par
                    pe.wait_ge(w_loaded, 32 * e + 32)
                    pe.wait_ge(w1_lo, e + 1)
                    for tt in range(TT):
                        up(TT * e + tt, par, tt)
                        if tt:
                            down(TT * e + tt - 1, par, tt - 1)
                        elif not (first and par == 0):
                            down(TT * e - 1, 1 - par, TT - 1)

            pe.wait_ge(x_lo, NT // 4)
            two_experts(0, first=True)
            with pe.Fori(1, N_EXP // 2) as i:
                two_experts(i)
            down(N - 1, 1, TT - 1)

        @block.scalar
        def _(act):
            def split_w1(e):
                act.wait_ge(w_loaded, 32 * e + 32)
                wait(act, down_done, TT * (e - 1))
                act.activation(w1_parts[:, e % 2, 0, :], w1_sb[:, e % 2, :], ACT.Copy).then_inc(w1_hi, 1)

            for k in range(NT // 4):
                act.wait_ge(tr_done, k + 1)
                act.activation(xnT_all[:, 512 * k:512 * k + 512], (tr_a, tr_b)[k % 2][:], ACT.Copy).then_inc(tr_free, 1)
            for k in range(NT // 4):
                act.wait_ge(tr_free, k + 1)
                act.activation(xnT[:, 0, 512 * k:512 * k + 512], xnT_all[:, 512 * k:512 * k + 512], ACT.Copy).then_inc(x_hi, 1)
            split_w1(0)
            act.wait_ge(gap_ready, 1)
            act.activation(gate_w[:, 1], gate_w[:, 0], ACT.Exp).then_inc(gate_exp, 1)

            def gelu(n, tt):
                for f in range(2):
                    act.wait_ge(up_done, 2 * n + f + 1)
                    wait(act, down_done, n - 1)
                    act.activation(hid[:, tt % 2, f, :], score[:, f, 0:512], ACT.Gelu).then_inc(gelu_done, 1)

            for e in range(N_EXP):
                for tt in range(TT):
                    gelu(TT * e + tt, tt)
                    if tt == 1 and e + 1 < N_EXP:
                        split_w1(e + 1)


_INS = {
    "x_in": lambda a: a["x"].reshape(B * S, E),
    "ctx_in": lambda a: a["ctx_1024"].reshape(B * C, E),
    "wq_s": lambda a: a["L0_attn_Wq"].T,
    "wk_s": lambda a: a["L0_attn_Wk"].T,
    "wv_s": lambda a: a["L0_attn_Wv"].T,
    "line_in": lambda a: a["L0_attn_bias_table"].T,
    "wq_c": lambda a: a["L0_xattn_Wq"].T.reshape(PAIRS, P, E).transpose(1, 0, 2),
    "wk_c": lambda a: a["L0_xattn_Wkv"][:, :H * D_CROSS].T.reshape(PAIRS, P, E).transpose(1, 0, 2),
    "wv_c": lambda a: a["L0_xattn_Wkv"][:, H * D_CROSS:],
    "wo_c": lambda a: a["L0_xattn_Wout"].reshape(PAIRS, P, E).transpose(1, 0, 2),
    "wg": lambda a: a["L0_ffn_Wg"].T,
    "w1": lambda a: a["L0_ffn_W1"],
    "w2": lambda a: a["L0_ffn_W2"],
}


def kernel(**inputs):
    import numpy as np
    import concourse.bacc as bacc
    from concourse.bass_utils import run_bass_kernel_spmd

    a = {k: np.asarray(x) for k, x in inputs.items()}
    arrays = {k: np.ascontiguousarray(lay(a)) for k, lay in _INS.items()}
    arrays["ln_rows"] = np.stack([a["L0_attn_ln_gamma"], a["L0_attn_ln_beta"]])
    arrays["ln_cols"] = np.stack([a["L0_xattn_ln_m_g"], a["L0_xattn_ln_m_b"], a["L0_xattn_ln_l_g"], a["L0_xattn_ln_l_b"]], axis=1)
    row = np.arange(P)
    low_q, low_k = row % 32 // 16, row % 16 // 8
    arrays["row_masks"] = np.stack([*(row // 32 == j for j in range(4)), low_q, 1 - 2 * low_q, low_k, 1 - 2 * low_k],
                                   axis=1).astype(np.float32)
    nc = bacc.Bacc("TRN2", target_bir_lowering=False, num_devices=1)
    aps = {k: nc.dram_tensor(k, x.shape, mybir.dt.from_np(x.dtype), kind="ExternalInput").ap() for k, x in arrays.items()}
    out = nc.dram_tensor("out", (B * S, E), F32, kind="ExternalOutput").ap()
    build(nc, out=out, **aps)
    r = run_bass_kernel_spmd(nc, [arrays], core_ids=[0])
    return r.results[0]["out"].reshape(B, S, E)
```

```python
from contextlib import ExitStack

import concourse.bass as bass
import concourse.mybir as mybir
from concourse.alu_op_type import AluOpType as ALU

F32 = mybir.dt.float32
F32R = mybir.dt.float32r
U32 = mybir.dt.uint32
ACT = mybir.ActivationFunctionType
AX = mybir.AxisListType

P = 128
B, S, E = 8, 256, 128
C = 512
H = 16
D_SELF = E // H
D_CROSS = 64
EPS = 1e-5
QT = S // P
NT = B * QT
KC = C // P
L = C + S
KT = L // P
HALF = L // 2
PAIRS = H // 2
G = H // 4
N_EXP, TOP, I_FF = 8, 2, 256
N_TOK = B * S
CAP = int(N_TOK * TOP * 1.25 / N_EXP)


def wait(engine, sem, value):
    if isinstance(value, int) and value <= 0:
        return
    engine.wait_ge(sem, value)


def build(nc, x_in, ctx_in, wq_s, wk_s, wv_s, line_in, row_masks, ln_rows, ln_cols, wq_c, wk_c, wv_c, wo_c, wg, w1, w2, out):
    es = ExitStack()
    with es:
        def sb(name, shape, dt=F32):
            return es.enter_context(nc.sbuf_tensor(name, shape, dt))

        def sem(name):
            return es.enter_context(nc.semaphore(name))

        x_all = sb("x_all", [P, NT, E])
        o_all = sb("o_all", [P, NT, E])
        xnT_all = sb("xnT_all", [P, N_TOK])
        ident = sb("ident", [P, P])
        stats = sb("stats", [P, NT + B * KC, 6])
        mv = sb("mv", [P, NT + B * KC, 2])
        rstd = sb("rstd", [P, NT + B * KC, 1])
        shift = sb("shift", [P, NT + B * KC, 1])
        half_neg = sb("half_neg", [P, NT + B * KC, 1])

        score = es.enter_context(nc.psum_tensor("score", [P, 2, 1024], F32))
        tr_a = es.enter_context(nc.psum_tensor("tr_a", [P, 512], F32))
        tr_b = es.enter_context(nc.psum_tensor("tr_b", [P, 512], F32))
        av = es.enter_context(nc.psum_tensor("av", [P, 512], F32))
        misc = es.enter_context(nc.psum_tensor("misc", [P, 512], F32))

        with ExitStack() as attentions:
            def at(name, shape, dt=F32):
                return attentions.enter_context(nc.sbuf_tensor(name, shape, dt))
            kvT = at("kvT", [P, 2, B, L], F32R)
            mt_all = at("mt_all", [P, 2, H, E], F32R)
            wv_all = at("wv_all", [P, 2, H * D_CROSS], F32R)
            wo_all = at("wo_all", [P, PAIRS, E])
            wq_stack = at("wq_stack", [P, G, P])
            wk_stack = at("wk_stack", [P, G, P])
            v_all = at("v_all", [P, NT, E])
            masks = at("masks", [P, 8])
            gb_rows = at("gb_rows", [P, 2, E])
            gb_cols = at("gb_cols", [P, 4])
            nmax = at("nmax", [P, 4, 4])
            rsum = at("rsum", [P, 4, 4])
            rinv = at("rinv", [P, 4, 4])
            probs = at("probs", [P, 4, 4 * S])
            probsT = at("probsT", [P, 2, 2 * KT * S])
            avT = at("avT", [P, 2, S])
            prepare(nc, es, sb, sem, locals())
            self_attention(nc, sb, sem, locals())
            latents(nc, sb, sem, locals())
            cross_attention(nc, sb, sem, locals())
        experts(nc, sb, sem, locals())


def prepare(nc, es, sb, sem, v):
    x_all, kvT, mt_all, ident, misc, score = (v[k] for k in ("x_all", "kvT", "mt_all", "ident", "misc", "score"))
    stats, mv, rstd, half_neg, xnT_all = (v[k] for k in ("stats", "mv", "rstd", "half_neg", "xnT_all"))
    gb_cols, gb_rows = v["gb_cols"], v["gb_rows"]
    with ExitStack() as own:
        def tmp(name, shape):
            return own.enter_context(nc.sbuf_tensor(name, shape, F32))
        ctx_sb = v["probs"][:].rearrange("p u (t e) -> p (u t) e", e=E)
        xn = v["o_all"]
        kv_full = tmp("kv_full", [P, 2, C])
        wv_full = tmp("wv_full", [P, H * D_CROSS])
        wq_c_sb = tmp("wq_c_sb", [P, PAIRS, E])
        wk_c_sb = tmp("wk_c_sb", [P, PAIRS, E])
        wq_sb = tmp("wq_sb", [P, E])
        wk_sb = tmp("wk_sb", [P, E])
        wv_sb = tmp("wv_sb", [P, E])
        mirror = tmp("mirror", [P, P])
        v_rev = tmp("v_rev", [P, QT, H, B, D_SELF])
        share_T = tmp("share_T", [P, 2, S])
        line = tmp("line", [H, 2 * S])
        bias = v["probsT"][:].rearrange("p a (h k) -> p (a h) k", k=S + P)
        line_dram = nc.dram_tensor("line_dram", (H, 2 * S), F32)
        x_loaded, ctx_loaded, wc_loaded, w_loaded = sem("x_loaded"), (sem("ctx_a_loaded"), sem("ctx_b_loaded")), sem("wc_loaded"), sem("w_loaded")
        line_loaded, line_made, line_stored, bias_loaded = sem("line_loaded"), sem("line_made"), sem("line_stored"), (sem("bias_a_loaded"), sem("bias_b_loaded"))
        consts, vec, var_ready, rstd_ready = sem("consts"), sem("p_vec"), sem("p_var_ready"), sem("p_rstd_ready")
        mt_hi, mt_lo, wv_hi, kv_hi, kv_lo = sem("mt_hi"), sem("mt_lo"), sem("wv_hi"), sem("kv_hi"), sem("kv_lo")
        x_normed, xt_done, xt_free = sem("x_normed"), sem("xt_done"), sem("xt_free")
        v_done, v_free, rev_done, rev_free, shift_done = sem("v_done"), sem("v_free"), sem("rev_done"), sem("rev_free"), sem("shift_done")
        share_done, share_free = sem("share_done"), sem("share_free")
        ctx_normed, ctx_late_normed, mt_done, tr_done, tr_free = sem("ctx_normed"), sem("ctx_late_normed"), sem("mt_done"), sem("p_tr_done"), sem("p_tr_free")
        block = own.enter_context(nc.Block())

        @block.sync
        def _(sp):
            sp.dma_start(x_all[:], v["x_in"].rearrange("(t p) e -> p t e", p=P)).then_inc(x_loaded, 16)
            sp.dma_start(line[:, 0:S - 1], v["line_in"]).then_inc(line_loaded, 16)
            for half in range(2):
                tiles = slice(half * B * KC // 2, (half + 1) * B * KC // 2)
                sp.dma_start(ctx_sb[:, tiles, :], v["ctx_in"].rearrange("(t p) e -> p t e", p=P)[:, tiles, :]).then_inc(ctx_loaded[half], 16)
            sp.wait_ge(line_made, 1)
            sp.dma_start(line_dram.ap(), line[:]).then_inc(line_stored, 16)
            sp.wait_ge(line_stored, 16)
            for half in range(2):
                window = bass.AP(line_dram, half * (H // 2) * 2 * S, [[1, P], [2 * S, H // 2], [1, S + P]])
                sp.dma_start(bias[:, half * (H // 2):(half + 1) * (H // 2), :], window).then_inc(bias_loaded[half], 16)
            for half in range(2):
                sp.wait_ge(bias_loaded[half], 16)
            sp.wait_ge(w_loaded, 16 * 8)

        @block.gpsimd
        def _(pool):
            pool.memset(ident[:], 0.0).then_inc(consts, 1)
            pool.memset(mirror[:], 0.0).then_inc(consts, 1)
            pool.memset(half_neg[:], -0.5).then_inc(consts, 1)
            pool.wait_ge(consts, 3)
            pool.affine_select(out=ident[:], in_=ident[:], compare_op=ALU.not_equal, fill=1.0,
                               base=0, pattern=[[-1, P]], channel_multiplier=1).then_inc(consts, 1)
            pool.affine_select(out=mirror[:], in_=mirror[:], compare_op=ALU.not_equal, fill=1.0,
                               base=1 - P, pattern=[[1, P]], channel_multiplier=1).then_inc(consts, 1)
            for k in range(3):
                inverse_roots(pool, v, NT * k, NT * (k + 1), k, var_ready, rstd_ready)

        @block.vector
        def _(dve):
            count = [0]

            def link(ins, hold):
                count[0] += 1
                ins.then_inc(vec, 1)
                if hold:
                    dve.wait_ge(vec, count[0])
                return ins

            dve.wait_ge(line_loaded, 16)
            dve.tensor_copy(line[:, S - 1:2 * S], line[:, S - 2:S - 1].to_broadcast([H, S + 1])).then_inc(line_made, 1)
            dve.wait_ge(x_loaded, 16)
            def statistics(k, tile):
                for t in range(NT):
                    link(dve.bn_stats(stats[:, NT * k + t, :], tile(t)), t == NT - 1)
                for t in range(NT):
                    last = dve.bn_aggr(mv[:, NT * k + t, :], stats[:, NT * k + t, :])
                    if t < NT - 1:
                        link(last, False)
                last.then_inc(var_ready, 1)

            statistics(0, lambda t: x_all[:, t, :])
            dve.wait_ge(rstd_ready, ROOTS)
            for t in range(NT):
                dve.tensor_scalar(xn[:, t, :], x_all[:, t, :], mv[:, t, 0:1], rstd[:, t, :],
                                  ALU.subtract, ALU.mult).then_inc(x_normed, 1)
            dve.wait_ge(ctx_loaded[0], 16)
            statistics(1, lambda t: ctx_sb[:, t, :])
            dve.wait_ge(w_loaded, 16 * 8)
            for dst, src, by in ((v["wq_stack"], wq_sb, E ** -0.5), (v["wk_stack"], wk_sb, 1.0)):
                dve.tensor_scalar(dst[:].rearrange("p g (j c d) -> p (g j) c d", j=4, c=4),
                                  src[:].rearrange("p (h o d) -> p h o d", o=1, d=D_SELF).to_broadcast([P, H, 4, D_SELF]),
                                  by, None, ALU.mult)
            dve.wait_ge(ctx_loaded[1], 16)
            statistics(2, lambda t: ctx_sb[:, NT + t, :])
            dve.wait_ge(rstd_ready, 2 * ROOTS)
            for t in range(NT):
                dve.tensor_scalar(ctx_sb[:, t, :], ctx_sb[:, t, :], mv[:, NT + t, 0:1], rstd[:, NT + t, :],
                                  ALU.subtract, ALU.mult).then_inc(ctx_normed, 1)
            for k in range(2):
                dve.wait_ge(mt_hi, k + 1)
                for o in range(2):
                    m = dve.scalar_tensor_tensor(out=mt_all[:, 1, 8 * k + o:8 * k + 8:2, :],
                                                 in0=score[:, k, 512 * o:512 * o + 512].rearrange("p (h e) -> p h e", e=E), scalar=D_CROSS ** -0.5,
                                                 in1=mt_all[:, 0, 8 * k + o:8 * k + 8:2, :].bitcast(F32), op0=ALU.mult, op1=ALU.subtract)
                m.then_inc(mt_lo, 1)
            dve.wait_ge(wv_hi, 1)
            dve.tensor_tensor(v["wv_all"][:, 1, :], wv_full[:], v["wv_all"][:, 0, :].bitcast(F32), ALU.subtract)

            def low_tokens(b):
                dve.wait_ge(kv_hi, b + 1)
                dve.tensor_tensor(kvT[:, 1, b, 0:C], kv_full[:, b % 2, :], kvT[:, 0, b, 0:C].bitcast(F32), ALU.subtract).then_inc(kv_lo, 1)

            for b in range(B // 2):
                low_tokens(b)
            for k in range(2 * QT):
                dve.wait_ge(shift_done, 4 * (k // 2) + 4)
                dve.tensor_copy(v["o_all"][:].rearrange("p (b t) (h d) -> p t h b d", t=QT, d=D_SELF)[:, k % 2, (k // 2) * 8:(k // 2) * 8 + 8],
                                score[:, k // 2, (k % 2) * 512:(k % 2) * 512 + 512].rearrange("p (h b d) -> p h b d", h=8, b=B))
            for b in range(B // 2, B):
                low_tokens(b)

        @block.tensor
        def _(pe):
            pe.wait_ge(wc_loaded, 32)
            for h in range(H):
                r = slice(64 * (h % 2), 64 * (h % 2) + 64)
                at = (h % 2) * 512 + (h // 2) % 4 * P
                m = pe.matmul(score[:, h // 8, at:at + P], wq_c_sb[r, h // 2, :], wk_c_sb[r, h // 2, :], start=True, stop=True)
                if h % 8 == 7:
                    m.then_inc(mt_done, 1)
            pe.wait_ge(consts, 4)
            for k in range(NT // 4):
                if k >= 2:
                    pe.wait_ge(xt_free, k - 1)
                pe.wait_ge(x_normed, 4 * k + 4)
                for j in range(4):
                    m = pe.transpose((v["tr_a"], v["tr_b"])[k % 2][:, j * P:(j + 1) * P], xn[:, 4 * k + j, :], ident[:])
                m.then_inc(xt_done, 1)
            pe.wait_ge(w_loaded, 16 * 8)
            for k in range(NT // 4):
                pe.wait_ge(xt_free, NT // 4)
                if k >= 2:
                    pe.wait_ge(v_free, k - 1)
                for j in range(4):
                    t = 4 * k + j
                    m = pe.matmul((v["tr_a"], v["tr_b"])[k % 2][:, j * P:(j + 1) * P], xnT_all[:, t * P:(t + 1) * P], wv_sb[:], start=True, stop=True)
                m.then_inc(v_done, 1)
            pe.wait_ge(consts, 5)
            for k in range(NT // 4):
                pe.wait_ge(v_free, NT // 4)
                if k >= 2:
                    pe.wait_ge(rev_free, k - 1)
                pe.matmul((v["tr_a"], v["tr_b"])[k % 2][:], mirror[:], v["v_all"][:, 4 * k:4 * k + 4, :].rearrange("p t e -> p (t e)"),
                          start=True, stop=True).then_inc(rev_done, 1)
            def transpose_context(b):
                bank = (misc, v["av"])[b % 2]
                if b >= 2:
                    pe.wait_ge(tr_free, b - 1)
                if b < B // 2:
                    pe.wait_ge(ctx_normed, KC * (b + 1))
                else:
                    pe.wait_ge(ctx_late_normed, KC * (b - B // 2 + 1))
                for k in range(KC):
                    m = pe.transpose(bank[:, k * P:(k + 1) * P], ctx_sb[:, b * KC + k, :], ident[:])
                m.then_inc(tr_done, 1)

            for b in range(B // 2):
                transpose_context(b)
            pe.wait_ge(rev_free, NT // 4)
            pe.wait_ge(mt_lo, 2)

            def transpose_bias_share(n):
                pe.wait_ge(share_free, n + 1)
                half, at = n // 4, n % 4 * P
                for qt in range(QT):
                    m = pe.transpose(score[:, half, qt * 512 + at:qt * 512 + at + P], share_T[:, n % 2, qt * P:(qt + 1) * P], ident[:])
                m.then_inc(shift_done, 1)

            for n in range(PAIRS):
                pe.wait_ge(bias_loaded[n // 4], 16)
                wait(pe, share_free, n - 1)
                bank = (v["tr_a"], v["tr_b"])[n % 2]
                for kt in range(QT):
                    for j in range(2):
                        h = 2 * n + j
                        m = pe.matmul(bank[64 * j:64 * j + 64, 0:S], v_rev[:, kt, h, :, :],
                                      bias[:, h, P * (1 - kt):P * (1 - kt) + S], start=kt == 0, stop=kt == 1, tile_position=(0, 64 * j))
                m.then_inc(share_done, 1)
                if n:
                    transpose_bias_share(n - 1)
            transpose_bias_share(PAIRS - 1)
            for b in range(B // 2, B):
                transpose_context(b)

        @block.scalar
        def _(act):
            act.dma_start(wq_c_sb[:], v["wq_c"]).then_inc(wc_loaded, 16)
            act.dma_start(wk_c_sb[:], v["wk_c"]).then_inc(wc_loaded, 16)
            act.dma_start(gb_cols[:], v["ln_cols"]).then_inc(w_loaded, 16)
            act.dma_start(gb_rows[:], v["ln_rows"].rearrange("(o k) e -> o k e", o=1).to_broadcast([P, 2, E])).then_inc(w_loaded, 16)
            act.dma_start(wq_sb[:], v["wq_s"]).then_inc(w_loaded, 16)
            act.dma_start(wk_sb[:], v["wk_s"]).then_inc(w_loaded, 16)
            act.dma_start(wv_sb[:], v["wv_s"]).then_inc(w_loaded, 16)
            act.dma_start(v["masks"][:], v["row_masks"]).then_inc(w_loaded, 16)
            act.dma_start(wv_full[:], v["wv_c"]).then_inc(w_loaded, 16)
            act.dma_start(v["wo_all"][:], v["wo_c"]).then_inc(w_loaded, 16)
            for k in range(2):
                act.wait_ge(mt_done, k + 1)
                act.activation(mt_all[:, 0, 8 * k:8 * k + 8, :].rearrange("p (h o) e -> p o h e", o=2),
                               score[:, k, :].rearrange("p (o h e) -> p o h e", o=2, e=E), ACT.Copy,
                               scale=D_CROSS ** -0.5).then_inc(mt_hi, 1)
            for k in range(NT // 4):
                act.wait_ge(xt_done, k + 1)
                act.activation(xnT_all[:, 512 * k:512 * k + 512], (v["tr_a"], v["tr_b"])[k % 2][:], ACT.Copy).then_inc(xt_free, 1)
            for k in range(NT // 4):
                act.wait_ge(v_done, k + 1)
                act.activation(v["v_all"][:, 4 * k:4 * k + 4, :], (v["tr_a"], v["tr_b"])[k % 2][:].rearrange("p (t e) -> p t e", t=4),
                               ACT.Copy).then_inc(v_free, 1)
            for k in range(NT // 4):
                act.wait_ge(rev_done, k + 1)
                for kt in range(QT):
                    m = act.activation(v_rev[:, kt, :, 2 * k:2 * k + 2, :],
                                       (v["tr_a"], v["tr_b"])[k % 2][:].rearrange("p (b t h d) -> p t h b d", b=2, t=QT, h=H)[:, kt], ACT.Copy)
                m.then_inc(rev_free, 1)
            act.wait_ge(w_loaded, 16 * 8)
            act.activation(v["wv_all"][:, 0, :], wv_full[:], ACT.Copy).then_inc(wv_hi, 1)

            def evacuate_context(b):
                bank = (misc, v["av"])[b % 2]
                act.wait_ge(tr_done, b + 1)
                if b >= 2:
                    act.wait_ge(kv_lo, b - 1)
                act.activation(kv_full[:, b % 2, :], bank[:], ACT.Identity, scale=gb_cols[:, 0:1],
                               bias=gb_cols[:, 1:2]).then_inc(tr_free, 1)
                act.wait_ge(tr_free, b + 1)
                act.activation(kvT[:, 0, b, 0:C], kv_full[:, b % 2, :], ACT.Copy).then_inc(kv_hi, 1)

            for b in range(B // 2):
                evacuate_context(b)
            act.wait_ge(rstd_ready, 3 * ROOTS)
            for t in range(NT):
                if t % 2 == 0:
                    n = t // 2
                    act.wait_ge(share_done, n + 1)
                    wait(act, shift_done, n - 1)
                    act.activation(share_T[:, n % 2, :], (v["tr_a"], v["tr_b"])[n % 2][:, 0:S], ACT.Copy).then_inc(share_free, 1)
                act.activation(ctx_sb[:, NT + t, :], ctx_sb[:, NT + t, :], ACT.Identity, scale=rstd[:, 2 * NT + t, :],
                               bias=v["shift"][:, 2 * NT + t, :]).then_inc(ctx_late_normed, 1)
            for b in range(B // 2, B):
                evacuate_context(b)


def self_attention(nc, sb, sem, v):
    xnT_all, o_all, v_all, ident, masks = (v[k] for k in ("xnT_all", "o_all", "v_all", "ident", "masks"))
    wq_stack, wk_stack = v["wq_stack"], v["wk_stack"]
    score, tr_a, tr_b, av, misc = (v[k] for k in ("score", "tr_a", "tr_b", "av", "misc"))
    nmax, probs, probsT, avT = (v[k] for k in ("nmax", "probs", "probsT", "avT"))
    U = G * QT
    with ExitStack() as own:
        def tmp(name, shape, dt=F32):
            return own.enter_context(nc.sbuf_tensor(name, shape, dt))
        high = tmp("high", [P, 2, S], F32R)
        q_parts = tmp("q_parts", [P, G, S], F32R)
        k_parts = tmp("k_parts", [P, 2, S])
        k_diag = tmp("k_diag", [P, G, 4, S], F32R)
        v_pad = tmp("v_pad", [P, QT, G, 4, 32])
        sum_inv = tmp("sum_inv", [P, QT, 4, 1])
        share = tmp("share", [P, 2, QT, 4, D_SELF])
        qk_done, max_done, exp_done, high_ready, k_ready, kd_ready = (sem("s_" + n) for n in ("qk_done", "max_done", "exp_done", "high_ready", "k_ready", "kd_ready"))
        tr_done, ta_free, tb_free, av_done, avT_ready, v_ready = (sem("s_" + n) for n in ("tr_done", "ta_free", "tb_free", "av_done", "avT_ready", "v_ready"))
        proj_done, out_full, out_free, divided, added, cleared = (sem("s_" + n) for n in ("proj_done", "out_full", "out_free", "divided", "added", "cleared"))
        block = own.enter_context(nc.Block())

        first_banks = (tr_a, tr_b, av, misc)

        def known(x):
            return isinstance(x, int)

        @block.tensor
        def _(pe):
            def scores(b, u):
                g, qt, n = u // QT, u % QT, U * b + u
                if qt == 0:
                    pe.wait_ge(kd_ready, G * b + g + 1)
                wait(pe, exp_done, n - 1)
                for j in range(2):
                    m = pe.matmul(score[:, u % 2, j * 512:(j + 1) * 512], q_parts[:, g, qt * P:(qt + 1) * P],
                                  k_diag[:, g, 2 * j:2 * j + 2, :], start=True, stop=True)
                m.then_inc(qk_done, 1)

            def transposes(b, u):
                n = U * b + u
                pe.wait_ge(exp_done, n + 1)
                for half, bank, free in ((0, tr_a, ta_free), (1, tr_b, tb_free)):
                    wait(pe, free, n)
                    for k in range(4):
                        at = half * 512 + k * P
                        m = pe.transpose(bank[:, k * P:(k + 1) * P], probs[:, u % 4, at:at + P], ident[:])
                    m.then_inc(tr_done, 1)

            def attend(b, g):
                n = G * b + g
                pe.wait_ge(ta_free, QT * n + QT)
                pe.wait_ge(tb_free, QT * n + QT)
                wait(pe, avT_ready, n)
                pe.wait_ge(v_ready, n + 1)
                for kt in range(QT):
                    for j in range(4):
                        m = pe.matmul(av[32 * j:32 * j + 32, 0:S], v_pad[:, kt, g, j, :],
                                      probsT[:, g % 2, (2 * j + kt) * S:(2 * j + kt + 1) * S],
                                      start=kt == 0, stop=kt == QT - 1, tile_position=(0, 32 * j))
                m.then_inc(av_done, 1)

            def natural(b, g):
                splits = G * b + G + 3 + g
                wait(pe, k_ready, min(splits, G * B) if known(splits) else splits)
                wait(pe, out_free, G * b + g)
                pe.wait_ge(avT_ready, G * b + g + 1)
                for qt in range(QT):
                    m = pe.transpose(misc[:, qt * P:(qt + 1) * P], avT[:, g % 2, qt * P:(qt + 1) * P], ident[:])
                m.then_inc(out_full, 1)

            def project(b, g):
                first = known(b) and b == 0
                if not first:
                    wait(pe, k_ready, G * b + g)
                    wait(pe, out_free, G * (b - 1) - 2 + g)
                bank = first_banks[g] if first else misc
                for k, w in enumerate((wq_stack, wk_stack)):
                    m = pe.matmul(bank[:, k * S:(k + 1) * S], w[:, g, :], xnT_all[:, bass.ds(b * S, S)], start=True, stop=True)
                m.then_inc(proj_done, 1)

            def slot(b, u, first=False, last=False):
                if u < U:
                    scores(b, u)
                if u % 2 == 0:
                    if u >= 4:
                        if (u - 4) // 2 < G:
                            attend(b, (u - 4) // 2)
                    elif not first:
                        attend(b - 1, (u + 4) // 2)
                if u >= 2:
                    if u - 2 < U:
                        transposes(b, u - 2)
                elif not first:
                    transposes(b - 1, U + u - 2)
                if u % 2:
                    if not last and u < U:
                        project(b + 1, u // 2)
                elif u >= 6:
                    natural(b, (u - 6) // 2)
                elif not first:
                    natural(b - 1, (u + 2) // 2)

            for g in range(G):
                project(0, g)
            for u in range(U):
                slot(0, u, first=True)
            with pe.Fori(1, B - 1) as b:
                for u in range(U):
                    slot(b, u)
            for u in range(U + 5):
                slot(B - 1, u, last=True)

        @block.scalar
        def _(act):
            def exponentials(b, u):
                n = U * b + u
                act.wait_ge(max_done, n + 1)
                if not known(n) or n >= 4:
                    act.wait_ge(tr_done, 2 * n - 6)
                for j in range(4):
                    m = act.activation(probs[:, u % 4, j * S:(j + 1) * S], score[:, u % 2, j * S:(j + 1) * S], ACT.Exp,
                                       bias=nmax[:, u % 4, j:j + 1])
                m.then_inc(exp_done, 1)

            def evacuate_a(b, u):
                n, g, qt = U * b + u, u // QT, u % QT
                act.wait_ge(tr_done, 2 * n + 1)
                wait(act, av_done, G * b + g - 1)
                act.activation(probsT[:, g % 2, 0:4 * S].rearrange("p (k q) -> p k q", k=4)[:, :, qt * P:(qt + 1) * P],
                               tr_a[:].rearrange("p (k q) -> p k q", k=4), ACT.Copy).then_inc(ta_free, 1)

            def evacuate_av(b, g):
                act.wait_ge(av_done, G * b + g + 1)
                wait(act, out_full, G * b + g - 1)
                act.activation(avT[:, g % 2, :], av[:, 0:S], ACT.Copy).then_inc(avT_ready, 1)

            def high_parts(b, g):
                act.wait_ge(proj_done, G * b + g + 1)
                first = known(b) and b == 0
                if first:
                    wait(act, k_ready, g)
                bank = first_banks[g] if first else misc
                for k in range(2):
                    m = act.activation(high[:, k, :], bank[:, k * S:(k + 1) * S], ACT.Copy, scale=masks[:, 5 + 2 * k:6 + 2 * k])
                m.then_inc(high_ready, 1)

            def slot(b, u, first=False, last=False):
                if u == 0 and not first:
                    high_parts(b, G - 1)
                elif u in (2, 4, 6) and not last:
                    high_parts(b + 1, u // 2 - 1)
                if u >= 2:
                    if u - 2 < U:
                        evacuate_a(b, u - 2)
                elif not first:
                    evacuate_a(b - 1, U + u - 2)
                if u % 2 == 0:
                    if u >= 4:
                        if (u - 4) // 2 < G:
                            evacuate_av(b, (u - 4) // 2)
                    elif not first:
                        evacuate_av(b - 1, (u + 4) // 2)
                if u < U:
                    exponentials(b, u)

            for g in range(G):
                high_parts(0, g)
            for u in range(U):
                slot(0, u, first=True)
            with act.Fori(1, B - 1) as b:
                for u in range(U):
                    slot(b, u)
            for u in range(U + 5):
                slot(B - 1, u, last=True)

        @block.vector
        def _(dve):
            def maxima(b, u):
                dve.wait_ge(qk_done, U * b + u + 1)
                dve.tensor_reduce(nmax[:, u % 4, :], score[:, u % 2, :].rearrange("p (j k) -> p j k", j=4),
                                  axis=AX.X, op=ALU.max, negate=True).then_inc(max_done, 1)

            def evacuate_b(b, u):
                n, g, qt = U * b + u, u // QT, u % QT
                dve.wait_ge(tr_done, 2 * n + 2)
                wait(dve, av_done, G * b + g - 1)
                dve.tensor_copy(probsT[:, g % 2, 4 * S:8 * S].rearrange("p (k q) -> p k q", k=4)[:, :, qt * P:(qt + 1) * P],
                                tr_b[:].rearrange("p (k q) -> p k q", k=4)).then_inc(tb_free, 1)

            def split(b, g):
                n = G * b + g
                dve.wait_ge(high_ready, n + 1)
                wait(dve, qk_done, U * (b - 1) + QT * (g + 1))
                bank = first_banks[g] if known(b) and b == 0 else misc
                dve.scalar_tensor_tensor(out=q_parts[:, g, :], in0=bank[:, 0:S], scalar=masks[:, 4:5], in1=high[:, 0, :].bitcast(F32),
                                         op0=ALU.mult, op1=ALU.add)
                wait(dve, kd_ready, n - 1)
                dve.scalar_tensor_tensor(out=k_parts[:, g % 2, :], in0=bank[:, S:2 * S], scalar=masks[:, 6:7], in1=high[:, 1, :].bitcast(F32),
                                         op0=ALU.mult, op1=ALU.add).then_inc(k_ready, 1)

            def divide_output(b, g):
                n = G * b + g
                dve.wait_ge(out_full, n + 1)
                out = misc[:, 0:S].rearrange("p (t j c) -> p t j c", t=QT, j=4)
                dve.reciprocal(sum_inv[:], out[:, :, :, D_SELF:D_SELF + 1]).then_inc(divided, 1)
                dve.wait_ge(divided, n + 1)
                wait(dve, added, n - 1)
                dve.tensor_tensor(share[:, g % 2], out[:, :, :, 0:D_SELF], sum_inv[:].to_broadcast([P, QT, 4, D_SELF]), ALU.mult).then_inc(out_free, 1)

            def slot(b, u, first=False, last=False):
                if u < U:
                    maxima(b, u)
                if u == 0 and not first:
                    split(b, G - 1)
                elif u in (2, 4, 6) and not last:
                    split(b + 1, u // 2 - 1)
                if u >= 2:
                    if u - 2 < U:
                        evacuate_b(b, u - 2)
                elif not first:
                    evacuate_b(b - 1, U + u - 2)
                if u % 2 == 0 and u >= 6:
                    divide_output(b, (u - 6) // 2)
                elif u % 2 == 0 and not first:
                    divide_output(b - 1, (u + 2) // 2)

            for g in range(G):
                split(0, g)
            for u in range(U):
                slot(0, u, first=True)
            with dve.Fori(1, B - 1) as b:
                for u in range(U):
                    slot(b, u)
            for u in range(U + 5):
                slot(B - 1, u, last=True)

        @block.gpsimd
        def _(pool):
            def stage_values(b, g):
                wait(pool, av_done, G * (b - 1) + g + 1)
                pool.tensor_copy(v_pad[:, :, g, :, 0:D_SELF],
                                 v_all[:, bass.ds(QT * b, QT), g * 32:(g + 1) * 32].rearrange("p t (j c) -> p t j c", c=D_SELF)).then_inc(v_ready, 1)

            def spread_keys(b, g):
                pool.wait_ge(k_ready, G * b + g + 1)
                pool.tensor_tensor(k_diag[:, g, :, :],
                                   k_parts[:, g % 2:g % 2 + 1, :].to_broadcast([P, 4, S]),
                                   masks[:, 0:4].rearrange("p (h o) -> p h o", o=1).to_broadcast([P, 4, S]),
                                   ALU.mult).then_inc(kd_ready, 1)

            def add_output(b, g):
                pool.wait_ge(out_free, G * b + g + 1)
                o = o_all[:, bass.ds(QT * b, QT), g * 32:(g + 1) * 32].rearrange("p t (j c) -> p t j c", c=D_SELF)
                pool.tensor_tensor(o, share[:, g % 2], o, ALU.add).then_inc(added, 1)

            def batch(b, first=False):
                if not first:
                    spread_keys(b, 3)
                stage_values(b, 2)
                if not first:
                    add_output(b - 1, 1)
                spread_keys(b + 1, 0)
                stage_values(b, 3)
                if not first:
                    add_output(b - 1, 2)
                spread_keys(b + 1, 1)
                stage_values(b + 1, 0)
                if not first:
                    add_output(b - 1, 3)
                spread_keys(b + 1, 2)
                stage_values(b + 1, 1)
                add_output(b, 0)

            pool.memset(v_pad[:], 0.0).then_inc(cleared, 1)
            pool.wait_ge(cleared, 1)
            pool.memset(v_pad[:, :, :, :, D_SELF:D_SELF + 1], 1.0).then_inc(cleared, 1)
            for g in range(G):
                spread_keys(0, g)
            stage_values(0, 0)
            stage_values(0, 1)
            batch(0, first=True)
            with pool.Fori(1, B - 1) as b:
                batch(b)
            spread_keys(B - 1, 3)
            stage_values(B - 1, 2)
            add_output(B - 2, 1)
            stage_values(B - 1, 3)
            add_output(B - 2, 2)
            add_output(B - 2, 3)
            for g in range(G):
                add_output(B - 1, g)


def norm_stats(dve, step, x, tiles, stats, mv, ready):
    for t in tiles:
        m = dve.bn_stats(stats[:, t, :], x[:, t, :])
    step(m)
    for t in tiles:
        m = dve.bn_aggr(mv[:, t, :], stats[:, t, :])
    m.then_inc(ready, 1)


def latents(nc, sb, sem, v):
    x_all, o_all, kvT, ident, gb_rows, gb_cols = (v[k] for k in ("x_all", "o_all", "kvT", "ident", "gb_rows", "gb_cols"))
    stats, mv, rstd, shift = (v[k] for k in ("stats", "mv", "rstd", "shift"))
    banks = (v["misc"], v["av"])
    HT = NT // 2
    halves = [range(HT * k, HT * (k + 1)) for k in range(2)]
    with ExitStack() as own:
        full = own.enter_context(nc.sbuf_tensor("full", [P, NT // 4, 512], F32))
        step_done, var_ready, rstd_ready, out_normed, latent_ready, tr_done, tr_free, hi_ready = (
            sem("l_" + n) for n in ("step_done", "var_ready", "rstd_ready", "out_normed", "latent_ready", "tr_done", "tr_free", "hi_ready"))
        block = own.enter_context(nc.Block())

        @block.vector
        def _(dve):
            steps = [0]

            def step(m):
                steps[0] += 1
                m.then_inc(step_done, 1)
                dve.wait_ge(step_done, steps[0])

            def row(k):
                return gb_rows[:, k:k + 1, :].to_broadcast([P, HT, E])

            for half in halves:
                norm_stats(dve, step, o_all, half, stats, mv, var_ready)
            for k, half in enumerate(halves):
                o, x = (y[:, HT * k:HT * (k + 1), :] for y in (o_all, x_all))
                dve.wait_ge(out_normed, k + 1)
                step(dve.tensor_tensor(o, o, row(0), ALU.mult))
                step(dve.tensor_tensor(o, o, row(1), ALU.add))
                step(dve.tensor_tensor(x, x, o, ALU.add))
                norm_stats(dve, step, x_all, half, stats, mv, var_ready)
            for k in range(NT // 4):
                dve.wait_ge(hi_ready, k + 1)
                dve.tensor_tensor(kvT[:, 1, 2 * k:2 * k + 2, C:L], full[:, k, :].rearrange("p (b q) -> p b q", b=2),
                                  kvT[:, 0, 2 * k:2 * k + 2, C:L].bitcast(F32), ALU.subtract)

        @block.gpsimd
        def _(pool):
            for k in range(4):
                lo = HT * (k % 2)
                inverse_roots(pool, v, lo, lo + HT, k, var_ready, rstd_ready, twice=k >= 2)

        @block.tensor
        def _(pe):
            for k in range(NT // 4):
                pe.wait_ge(latent_ready, 4 * k + 4)
                if k >= 2:
                    pe.wait_ge(tr_free, k - 1)
                for j in range(4):
                    m = pe.transpose(banks[k % 2][:, j * P:(j + 1) * P], o_all[:, 4 * k + j, :], ident[:])
                m.then_inc(tr_done, 1)

        @block.scalar
        def _(act):
            def normalized(dst, src, half):
                for t in half:
                    m = act.activation(dst[:, t, :], src[:, t, :], ACT.Identity, scale=rstd[:, t, :], bias=shift[:, t, :])
                    if src is x_all:
                        m.then_inc(latent_ready, 1)
                return m

            for k, half in enumerate(halves):
                act.wait_ge(rstd_ready, ROOTS * (k + 1))
                normalized(o_all, o_all, half).then_inc(out_normed, 1)
            for k, half in enumerate(halves):
                act.wait_ge(rstd_ready, ROOTS * (k + 3))
                normalized(o_all, x_all, half)
                for j in range(2 * k, 2 * k + 2):
                    act.wait_ge(tr_done, j + 1)
                    act.activation(full[:, j, :], banks[j % 2][:], ACT.Identity,
                                   scale=gb_cols[:, 2:3], bias=gb_cols[:, 3:4]).then_inc(tr_free, 1)
                    act.wait_ge(tr_free, j + 1)
                    act.activation(kvT[:, 0, 2 * j:2 * j + 2, C:L], full[:, j, :].rearrange("p (b q) -> p b q", b=2), ACT.Copy).then_inc(hi_ready, 1)


ROOTS = 4


def inverse_roots(pool, v, lo, hi, k, var_ready, rstd_ready, twice=False):
    mv, rstd, shift, half_neg = (v[x][:, lo:hi, :] for x in ("mv", "rstd", "shift", "half_neg"))
    pool.wait_ge(var_ready, k + 1)
    by, plus = (1.0 + EPS, EPS * EPS) if twice else (1.0, EPS)
    pool.tensor_scalar(rstd, mv[:, :, 1:2], by, plus, ALU.mult, ALU.add).then_inc(rstd_ready, 1)
    pool.tensor_scalar(shift, mv[:, :, 0:1], -1.0, 1.0, ALU.mult, ALU.mult).then_inc(rstd_ready, 1)
    pool.wait_ge(rstd_ready, ROOTS * k + 2)
    pool.tensor_tensor(rstd, rstd, half_neg, ALU.pow).then_inc(rstd_ready, 1)
    pool.wait_ge(rstd_ready, ROOTS * k + 3)
    pool.tensor_tensor(shift, shift, rstd, ALU.mult).then_inc(rstd_ready, 1)


def cross_attention(nc, sb, sem, v):
    x_all, kvT, ident, mt_all, wv_all, wo_all = (v[k] for k in ("x_all", "kvT", "ident", "mt_all", "wv_all", "wo_all"))
    score, tr_a, tr_b, av, misc = (v[k] for k in ("score", "tr_a", "tr_b", "av", "misc"))
    nmax, rsum, rinv, probs, probsT, avT = (v[k] for k in ("nmax", "rsum", "rinv", "probs", "probsT", "avT"))
    IT = B * PAIRS // 2
    ITB = PAIRS // 2
    U = 4
    HI_LO = ((0, 0), (0, 1), (1, 0))
    with ExitStack() as own:
        def tmp(name, shape, dt=F32):
            return own.enter_context(nc.sbuf_tensor(name, shape, dt))
        mt = tmp("mt", [P, 2, 2, 2, E], F32R)
        kv = tmp("kv", [P, 2, L], F32R)
        aT = tmp("aT", [P, 2, 2, 2, S], F32R)
        val = tmp("val", [P, 2, KT, P])
        qk_done, max_done, exp_done, inv_done, p_ready = (sem("c_" + n) for n in ("qk_done", "max_done", "exp_done", "inv_done", "p_ready"))
        tr_done, ta_free, tb_free, av_done, avT_ready = (sem("c_" + n) for n in ("tr_done", "ta_free", "tb_free", "av_done", "avT_ready"))
        misc_full, misc_free, out_added, q_split = (sem("c_" + n) for n in ("misc_full", "misc_free", "out_added", "q_split"))
        weights_staged, tokens_staged, norm_called = (sem("c_" + n) for n in ("weights_staged", "tokens_staged", "norm_called"))
        block = own.enter_context(nc.Block())

        OUT0, Q1, V01, V23, OUT1, V45, Q2 = range(7)
        VALUES = (V01, V23, V45)
        R = 7

        def use(i, k):
            if isinstance(i, int) and i == 0:
                return 1 + (Q1, V01, V23, V45, Q2).index(k)
            return R * i + k - 1

        def use_q(i, j):
            if j:
                return use(i, Q1)
            return 0 if isinstance(i, int) and i == 0 else use(i - 1, Q2)

        def act_uses(i, k):
            return 5 * i + 1 + (Q1, V01, V23, V45, Q2).index(k)

        def batch_slice(i, part, at, n):
            return kvT[:, part, bass.ds(i // ITB, 1), at:at + n]

        @block.tensor
        def _(pe):
            def scores(i, j, u):
                p, h, qt = 2 * i + j, u // 2, u % 2
                n = U * p + u
                if u == 0:
                    pe.wait_ge(q_split, p + 1)
                wait(pe, exp_done, n - 1)
                for half in range(2):
                    for k, (a, b) in enumerate(HI_LO):
                        m = pe.matmul(score[:, u % 2, half * 512:half * 512 + HALF], aT[:, j, a, h, qt * P:(qt + 1) * P],
                                      batch_slice(i, b, half * HALF, HALF), start=k == 0, stop=k == 2)
                m.then_inc(qk_done, 1)

            def transposes(p, u):
                n = U * p + u
                pe.wait_ge(p_ready, n + 1)
                for half, bank, free in ((0, tr_a, ta_free), (1, tr_b, tb_free)):
                    wait(pe, free, n)
                    for k in range(KT // 2):
                        at = half * HALF + k * P
                        m = pe.transpose(bank[:, k * P:(k + 1) * P], probs[:, u % 4, at:at + P], ident[:])
                    m.then_inc(tr_done, 1)

            def attend(i, j):
                p = 2 * i + j
                pe.wait_ge(ta_free, U * p + U)
                pe.wait_ge(tb_free, U * p + U)
                pe.wait_ge(misc_free, act_uses(i, V45) + 1)
                wait(pe, avT_ready, p)
                for kt in range(KT):
                    for h in range(2):
                        m = pe.matmul(av[64 * h:64 * h + 64, 0:S], val[:, j, kt, 64 * h:64 * h + 64],
                                      probsT[:, j, (KT * h + kt) * S:(KT * h + kt + 1) * S],
                                      start=kt == 0, stop=kt == KT - 1, tile_position=(0, 64 * h))
                m.then_inc(av_done, 1)

            def queries(i, j, uses, outs):
                wait(pe, misc_free, uses)
                wait(pe, q_split, 2 * i + j)
                wait(pe, out_added, outs)
                pe.wait_ge(weights_staged, 2 * i + j + 1)
                for h in range(2):
                    for k, (a, b) in enumerate(HI_LO):
                        m = pe.matmul(misc[:, h * S:(h + 1) * S], mt[:, j, a, h, :], batch_slice(i, b, C, S),
                                      start=k == 0, stop=k == 2)
                m.then_inc(misc_full, 1)

            def values(i, k, first=False):
                wait(pe, misc_free, act_uses(i, VALUES[k]))
                if k == 0:
                    wait(pe, q_split, 2 * i + 2)
                    pe.wait_ge(tokens_staged, 16 * (i // ITB) + 16)
                if k == 2 and not first:
                    pe.wait_ge(out_added, 2 * i)
                for t in range(2):
                    for n, (a, b) in enumerate(HI_LO):
                        kt = 2 * k + t
                        m = pe.matmul(misc[:, t * 256:(t + 1) * 256], kv[:, a, kt * P:(kt + 1) * P],
                                      wv_all[:, b, bass.ds((i % ITB) * 256, 256)], start=n == 0, stop=n == 2)
                m.then_inc(misc_full, 1)

            def project_out(i, j):
                pe.wait_ge(avT_ready, 2 * i + j + 1)
                for qt in range(QT):
                    m = pe.matmul(misc[:, qt * P:(qt + 1) * P], avT[:, j, qt * P:(qt + 1) * P],
                                  wo_all[:, bass.ds((i % ITB) * 2 + j, 1), :], start=True, stop=True)
                m.then_inc(misc_full, 1)

            def iteration(i, first=False, last=False):
                before = i - 1
                for j in range(2):
                    p = 2 * i + j
                    none_before = first and j == 0
                    scores(i, j, 0)
                    if not none_before:
                        transposes(p - 1, 2)
                    if not first:
                        wait(pe, misc_free, act_uses(i, V45 if j else Q1))
                        wait(pe, q_split, p + 1)
                        project_out(before, j)
                    scores(i, j, 1)
                    if j:
                        values(i, 2, first)
                    if not none_before:
                        transposes(p - 1, 3)
                    if not j:
                        queries(i, 1, act_uses(i, Q1), 2 * i - 1)
                    scores(i, j, 2)
                    if j and not last:
                        queries(i + 1, 0, act_uses(i, Q2), 2 * i)
                    if not none_before:
                        attend(i if j else before, 1 - j)
                    transposes(p, 0)
                    if not j:
                        values(i, 0, first)
                    scores(i, j, 3)
                    transposes(p, 1)
                    if not j:
                        values(i, 1, first)

            queries(0, 0, 0, 0)
            iteration(0, first=True)
            with pe.Fori(1, IT - 1) as i:
                iteration(i)
            iteration(IT - 1, last=True)
            p = 2 * IT - 1
            transposes(p, 2)
            transposes(p, 3)
            project_out(IT - 1, 0)
            attend(IT - 1, 1)
            pe.wait_ge(out_added, p)
            project_out(IT - 1, 1)

        @block.scalar
        def _(act):
            def exponentials(p, u):
                n = U * p + u
                act.wait_ge(max_done, n + 1)
                if not isinstance(n, int) or n >= 4:
                    act.wait_ge(tr_done, 2 * n - 6)
                act.activation(probs[:, u, 0:L].rearrange("p (a k) -> p a k", a=2),
                               score[:, u % 2, :].rearrange("p (a k) -> p a k", a=2)[:, :, 0:HALF], ACT.Exp,
                               bias=nmax[:, u, 0:1], accum_out=rsum[:, u, 0:1]).then_inc(exp_done, 1)

            def evacuate_a(p, par, u):
                n, h, qt = U * p + u, u // 2, u % 2
                act.wait_ge(tr_done, 2 * n + 1)
                wait(act, av_done, p - 1)
                act.activation(probsT[:, par, KT * h * S:(KT * h + 3) * S].rearrange("p (k q) -> p k q", k=3)[:, :, qt * P:(qt + 1) * P],
                               tr_a[:, 0:HALF].rearrange("p (k q) -> p k q", k=3), ACT.Copy).then_inc(ta_free, 1)

            def evacuate_av(p, par):
                act.wait_ge(av_done, p + 1)
                wait(act, out_added, p - 1)
                act.activation(avT[:, par, :], av[:, 0:S], ACT.Copy).then_inc(avT_ready, 1)

            def evacuate_values(i, k):
                act.wait_ge(misc_full, use(i, VALUES[k]) + 1)
                wait(act, av_done, 2 * i)
                act.activation(val[:, :, 2 * k:2 * k + 2, :].rearrange("p j t c -> p t j c"),
                               misc[:].rearrange("p (t j c) -> p t j c", t=2, j=2), ACT.Copy).then_inc(misc_free, 1)

            def evacuate_queries(i, j):
                act.wait_ge(misc_full, use_q(i, j) + 1)
                wait(act, qk_done, U * (2 * i + j - 1))
                act.activation(aT[:, j, 0, :, :], misc[:].rearrange("p (h q) -> p h q", h=2), ACT.Copy).then_inc(misc_free, 1)

            def stage_weights(i, j):
                act.activation(mt[:, j].rearrange("p a h e -> p a (h e)"),
                               mt_all[:, :, bass.ds((i % ITB) * 4 + 2 * j, 2), :].rearrange("p a h e -> p a (h e)").bitcast(F32),
                               ACT.Copy).then_inc(weights_staged, 1)

            def iteration(i, first=False, last=False):
                for j in range(2):
                    p = 2 * i + j
                    none_before = first and j == 0
                    if not none_before:
                        evacuate_a(p - 1, 1 - j, 2)
                    exponentials(p, 0)
                    if j:
                        evacuate_values(i, 2)
                    if not none_before:
                        evacuate_a(p - 1, 1 - j, 3)
                    exponentials(p, 1)
                    if j:
                        if not last:
                            evacuate_queries(i + 1, 0)
                            stage_weights(i + 2, 0)
                    else:
                        evacuate_queries(i, 1)
                        if not last:
                            stage_weights(i + 1, 1)
                    exponentials(p, 2)
                    if not none_before:
                        evacuate_av(p - 1, 1 - j)
                    evacuate_a(p, j, 0)
                    if not j:
                        evacuate_values(i, 0)
                    evacuate_a(p, j, 1)
                    exponentials(p, 3)
                    if not j:
                        evacuate_values(i, 1)

            stage_weights(0, 0)
            stage_weights(0, 1)
            evacuate_queries(0, 0)
            stage_weights(1, 0)
            iteration(0, first=True)
            with act.Fori(1, IT - 1) as i:
                iteration(i)
            iteration(IT - 1, last=True)
            p = 2 * IT - 1
            evacuate_a(p, 1, 2)
            evacuate_a(p, 1, 3)
            evacuate_av(p, 1)

        @block.vector
        def _(dve):
            def maxima(p, u):
                dve.wait_ge(qk_done, U * p + u + 1)
                dve.tensor_reduce(nmax[:, u, 0:1], score[:, u % 2, :].rearrange("p (a k) -> p a k", a=2)[:, :, 0:HALF],
                                  axis=AX.XY, op=ALU.max, negate=True).then_inc(max_done, 1)

            def evacuate_b(p, par, u):
                n, h, qt = U * p + u, u // 2, u % 2
                dve.wait_ge(tr_done, 2 * n + 2)
                wait(dve, av_done, p - 1)
                dve.tensor_copy(probsT[:, par, (KT * h + 3) * S:(KT * h + 6) * S].rearrange("p (k q) -> p k q", k=3)[:, :, qt * P:(qt + 1) * P],
                                tr_b[:, 0:HALF].rearrange("p (k q) -> p k q", k=3)).then_inc(tb_free, 1)

            def invert(p, u):
                n = U * p + u
                dve.wait_ge(exp_done, n + 1)
                wait(dve, p_ready, n - 3)
                dve.reciprocal(rinv[:, u, 0:1], rsum[:, u, 0:1]).then_inc(inv_done, 1)

            def split_queries(i, j, evacuated):
                dve.wait_ge(misc_free, evacuated)
                dve.tensor_tensor(aT[:, j, 1, :, :], misc[:].rearrange("p (h q) -> p h q", h=2), aT[:, j, 0, :, :].bitcast(F32),
                                  ALU.subtract).then_inc(q_split, 1)

            def add_output(i, n, at):
                dve.wait_ge(misc_full, at + 1)
                wait(dve, out_added, n)
                x = x_all[:, bass.ds((i // ITB) * QT, QT), :]
                dve.tensor_tensor(x, misc[:, 0:S].rearrange("p (t e) -> p t e", t=QT), x, ALU.add).then_inc(out_added, 1)

            def iteration(i, first=False, last=False):
                for j in range(2):
                    p = 2 * i + j
                    none_before = first and j == 0
                    maxima(p, 0)
                    if not none_before:
                        invert(p - 1, 3)
                        evacuate_b(p - 1, 1 - j, 2)
                    if not first:
                        add_output(i - 1, p - 2, use(i, OUT1 if j else OUT0))
                    maxima(p, 1)
                    invert(p, 0)
                    if not none_before:
                        evacuate_b(p - 1, 1 - j, 3)
                    maxima(p, 2)
                    invert(p, 1)
                    if not j:
                        split_queries(i, 1, act_uses(i, Q1) + 1)
                    elif not last:
                        split_queries(i + 1, 0, act_uses(i, Q2) + 1)
                    invert(p, 2)
                    evacuate_b(p, j, 0)
                    maxima(p, 3)
                    evacuate_b(p, j, 1)

            split_queries(0, 0, 1)
            iteration(0, first=True)
            with dve.Fori(1, IT - 1) as i:
                iteration(i)
            iteration(IT - 1, last=True)
            p = 2 * IT - 1
            evacuate_b(p, 1, 2)
            invert(p, 3)
            evacuate_b(p, 1, 3)
            add_output(IT - 1, p - 1, use(IT - 1, V45) + 1)
            add_output(IT - 1, p, use(IT - 1, V45) + 2)

        @block.gpsimd
        def _(pool):
            def divide(p, u):
                n = U * p + u
                pool.wait_ge(inv_done, n + 1)
                pool.sem_inc(norm_called, 1)
                pool.tensor_scalar(probs[:, u, 0:L], probs[:, u, 0:L], rinv[:, u, 0:1], 1.0, ALU.mult, ALU.mult).then_inc(p_ready, 1)

            def batch(b, first=False):
                if not first:
                    pool.wait_ge(misc_full, use(ITB * b - 1, V45) + 1)
                pool.dma_start(kv[:], kvT[:, :, bass.ds(b, 1), :].rearrange("p a o l -> p a (o l)")).then_inc(tokens_staged, 16)
                for p in range(PAIRS):
                    for u in range(U):
                        divide(PAIRS * b + p, u)

            batch(0, first=True)
            with pool.Fori(1, B) as b:
                batch(b)


def experts(nc, sb, sem, v):
    x_all, o_all, xnT_all, ident = (v[k] for k in ("x_all", "o_all", "xnT_all", "ident"))
    stats, mv, rstd, half_neg = (v[k] for k in ("stats", "mv", "rstd", "half_neg"))
    misc, av, tr_a, tr_b, score = (v[k] for k in ("misc", "av", "tr_a", "tr_b", "score"))
    TT = N_TOK // 512
    with ExitStack() as own:
        def tmp(name, shape, dt=F32):
            return own.enter_context(nc.sbuf_tensor(name, shape, dt))
        wg_sb = tmp("wg_sb", [P, N_EXP])
        w1_sb = tmp("w1_sb", [P, 2, 2 * I_FF])
        w1_parts = tmp("w1_parts", [P, 2, 2, 2 * I_FF], F32R)
        xnT = tmp("xnT_parts", [P, 2, N_TOK], F32R)
        w2_sb = tmp("w2_sb", [P, 2, 2, E])
        hid = tmp("hid", [P, 2, 2, 512])
        before = tmp("before", [P, P])
        ones = tmp("ones", [P, P])
        iota_e = tmp("iota_e", [P, NT, N_EXP])
        carry_on = tmp("carry_on", [P, N_EXP, NT])
        logits = tmp("logits", [P, NT, N_EXP])
        top_v = tmp("top_v", [P, NT, 8])
        top_i = tmp("top_i", [P, NT, 8], U32)
        top_f = tmp("top_f", [P, NT, 8])
        pick = tmp("pick", [P, 2, NT, N_EXP])
        chosen = tmp("chosen", [P, NT, N_EXP])
        gate_w = tmp("gate_w", [P, 4, NT, 1])
        totals = tmp("totals", [P, N_EXP, NT])
        running = tmp("running", [P, N_EXP, NT])
        place = tmp("place", [P, NT, N_EXP])
        gates = tmp("gates", [P, NT, N_EXP])
        step_done, var_ready, rstd_ready, normed, tr_done, tr_free = (
            sem("e_" + n) for n in ("step_done", "var_ready", "rstd_ready", "normed", "tr_done", "tr_free"))
        consts, w1_hi, w1_lo, x_hi, x_lo, logits_done, chosen_ready, places_done, gap_ready, gate_exp, wg_loaded, w_loaded = (
            sem("e_" + n) for n in ("consts", "w1_hi", "w1_lo", "x_hi", "x_lo", "logits_done", "chosen_ready", "places_done", "gap_ready", "gate_exp", "wg_loaded", "w_loaded"))
        up_done, gelu_done, hid_ready, down_done, added, stored = (
            sem("e_" + n) for n in ("up_done", "gelu_done", "hid_ready", "down_done", "added", "stored"))
        block = own.enter_context(nc.Block())
        N = N_EXP * TT

        @block.sync
        def _(sp):
            sp.dma_start(wg_sb[:], v["wg"]).then_inc(wg_loaded, 16)

            def load(e, par):
                sp.dma_start(w1_sb[:, par, :], v["w1"][e]).then_inc(w_loaded, 16)
                sp.dma_start(w2_sb[:, par], v["w2"][e].rearrange("(k p) e -> p k e", p=P)).then_inc(w_loaded, 16)
                sp.wait_ge(w_loaded, 32 * e + 32)

            for e in range(N_EXP):
                wait(sp, down_done, TT * (e - 1))
                wait(sp, w1_lo, e - 1)
                load(e, e % 2)
            for t in range(0, NT, 4):
                sp.wait_ge(added, N - TT + t // 4 + 1)
                sp.dma_start(v["out"].rearrange("(t p) e -> p t e", p=P)[:, t:t + 4, :], x_all[:, t:t + 4, :]).then_inc(stored, 16)
            sp.wait_ge(stored, 16 * NT // 4)

        @block.gpsimd
        def _(pool):
            pool.memset(ones[:], 1.0).then_inc(consts, 1)
            pool.memset(before[:], 1.0).then_inc(consts, 1)
            pool.memset(carry_on[:], 1.0).then_inc(consts, 1)
            pool.iota(iota_e[:], pattern=[[0, NT], [1, N_EXP]], base=0, channel_multiplier=0,
                      allow_small_or_imprecise_dtypes=True).then_inc(consts, 1)
            pool.wait_ge(consts, 4)
            pool.affine_select(out=before[:], in_=before[:], compare_op=ALU.is_ge, fill=0.0, base=-1,
                               pattern=[[1, P]], channel_multiplier=-1).then_inc(consts, 1)
            pool.memset(carry_on[:, :, 0:1], 0.0).then_inc(consts, 1)
            inverse_roots(pool, v, 0, NT, 0, var_ready, rstd_ready)
            for e in range(N_EXP):
                pool.wait_ge(w1_hi, e + 1)
                pool.tensor_tensor(w1_parts[:, e % 2, 1, :], w1_sb[:, e % 2, :], w1_parts[:, e % 2, 0, :].bitcast(F32),
                                   ALU.subtract).then_inc(w1_lo, 1)

        @block.vector
        def _(dve):
            steps = [0]

            def step(m):
                steps[0] += 1
                m.then_inc(step_done, 1)
                dve.wait_ge(step_done, steps[0])

            norm_stats(dve, step, x_all, range(NT), stats, mv, var_ready)
            dve.wait_ge(rstd_ready, ROOTS)
            for t in range(NT):
                dve.tensor_scalar(o_all[:, t, :], x_all[:, t, :], mv[:, t, 0:1], rstd[:, t, :],
                                  ALU.subtract, ALU.mult).then_inc(normed, 1)
            for k in range(NT // 4):
                dve.wait_ge(x_hi, k + 1)
                dve.tensor_tensor(xnT[:, 1, 512 * k:512 * k + 512], xnT_all[:, 512 * k:512 * k + 512],
                                  xnT[:, 0, 512 * k:512 * k + 512].bitcast(F32), ALU.subtract).then_inc(x_lo, 1)
            dve.wait_ge(logits_done, 1)
            step(dve.tensor_copy(logits[:], misc[:, 0:NT * N_EXP].rearrange("p (t e) -> p t e", e=N_EXP)))
            for t in range(NT):
                m = dve.max(top_v[:, t, :], logits[:, t, :])
            step(m)
            for t in range(NT):
                m = dve.max_index(top_i[:, t, :], top_v[:, t, :], logits[:, t, :])
            step(m)
            step(dve.tensor_copy(top_f[:], top_i[:]))
            dve.wait_ge(consts, 6)
            for k in range(TOP):
                m = dve.tensor_tensor(pick[:, k], iota_e[:], top_f[:, :, k:k + 1].to_broadcast([P, NT, N_EXP]), ALU.is_equal)
            step(m)
            dve.tensor_tensor(chosen[:], pick[:, 0], pick[:, 1], ALU.add).then_inc(chosen_ready, 1)
            dve.tensor_tensor(gate_w[:, 0], top_v[:, :, 1:2], top_v[:, :, 0:1], ALU.subtract).then_inc(gap_ready, 1)
            dve.wait_ge(gate_exp, 1)
            step(dve.tensor_scalar(gate_w[:, 2], gate_w[:, 1], 1.0, None, ALU.add))
            step(dve.reciprocal(gate_w[:, 3], gate_w[:, 2]))
            step(dve.tensor_tensor(gate_w[:, 1], gate_w[:, 1], gate_w[:, 3], ALU.mult))
            m = dve.tensor_tensor(pick[:, 0], pick[:, 0], gate_w[:, 3].to_broadcast([P, NT, N_EXP]), ALU.mult)
            m = dve.tensor_tensor(pick[:, 1], pick[:, 1], gate_w[:, 1].to_broadcast([P, NT, N_EXP]), ALU.mult)
            step(m)
            step(dve.tensor_tensor(gates[:], pick[:, 0], pick[:, 1], ALU.add))
            dve.wait_ge(places_done, 1)
            step(dve.tensor_copy(totals[:], av[:, 0:P].rearrange("p (t e) -> p e t", e=N_EXP)))
            step(dve.tensor_tensor_scan(running[:].rearrange("p e t -> p (e t)"), carry_on[:].rearrange("p e t -> p (e t)"),
                                        totals[:].rearrange("p e t -> p (e t)"), 0.0, ALU.mult, ALU.add))
            step(dve.tensor_tensor(running[:], running[:], totals[:], ALU.subtract))
            step(dve.tensor_tensor(place[:], misc[:, 0:P].rearrange("p (t e) -> p t e", e=N_EXP),
                                   running[:].rearrange("p e t -> p t e"), ALU.add))
            step(dve.tensor_scalar(place[:], place[:], float(CAP), None, ALU.is_lt))
            step(dve.tensor_tensor(gates[:], gates[:], place[:], ALU.mult))

            def multiply(n, tt):
                for f in range(2):
                    dve.wait_ge(gelu_done, 2 * n + f + 1)
                    dve.tensor_tensor(hid[:, tt % 2, f, :], hid[:, tt % 2, f, :], score[:, f, 512:1024],
                                      ALU.mult).then_inc(hid_ready, 1)

            def accumulate(n, e, tt):
                dve.wait_ge(down_done, n + 1)
                wait(dve, added, n - TT + 1)
                for k in range(4):
                    t = 4 * tt + k
                    m = dve.scalar_tensor_tensor(out=x_all[:, t, :], in0=(tr_a, tr_b)[tt % 2][:, k * P:(k + 1) * P],
                                                 scalar=gates[:, t, bass.ds(e, 1)], in1=x_all[:, t, :],
                                                 op0=ALU.mult, op1=ALU.add)
                m.then_inc(added, 1)

            def two_experts(i, first=False):
                for par in range(2):
                    e = 2 * i + par
                    for tt in range(TT):
                        multiply(TT * e + tt, tt)
                        if tt:
                            accumulate(TT * e + tt - 1, e, tt - 1)
                        elif not (first and par == 0):
                            accumulate(TT * e - 1, e - 1, TT - 1)

            two_experts(0, first=True)
            with dve.Fori(1, N_EXP // 2) as i:
                two_experts(i)
            accumulate(N - 1, N_EXP - 1, TT - 1)

        @block.tensor
        def _(pe):
            for k in range(NT // 4):
                if k >= 2:
                    pe.wait_ge(tr_free, k - 1)
                pe.wait_ge(normed, 4 * k + 4)
                for j in range(4):
                    m = pe.transpose((tr_a, tr_b)[k % 2][:, j * P:(j + 1) * P], o_all[:, 4 * k + j, :], ident[:])
                m.then_inc(tr_done, 1)
            pe.wait_ge(wg_loaded, 16)
            for t in range(NT):
                if t % 4 == 0:
                    pe.wait_ge(tr_free, t // 4 + 1)
                m = pe.matmul(misc[:, t * N_EXP:(t + 1) * N_EXP], xnT_all[:, t * P:(t + 1) * P], wg_sb[:], start=True, stop=True)
            m.then_inc(logits_done, 1)
            pe.wait_ge(chosen_ready, 1)
            pe.wait_ge(consts, 6)
            flat = chosen[:].rearrange("p t e -> p (t e)")
            pe.matmul(misc[:, 0:P], before[:], flat, start=True, stop=True)
            pe.matmul(av[:, 0:P], ones[:], flat, start=True, stop=True).then_inc(places_done, 1)

            def up(n, par, tt):
                for f in range(2):
                    wait(pe, hid_ready, 2 * n + f - 1)
                    for half in range(2):
                        at = half * I_FF + f * P
                        for k, (a, b) in enumerate(((0, 0), (0, 1), (1, 0))):
                            m = pe.matmul(score[:, f, half * 512:(half + 1) * 512], w1_parts[:, par, a, at:at + P],
                                          xnT[:, b, tt * 512:(tt + 1) * 512], start=k == 0, stop=k == 2)
                    m.then_inc(up_done, 1)

            def down(n, par, tt):
                pe.wait_ge(hid_ready, 2 * n + 2)
                wait(pe, added, n - 1)
                for k in range(4):
                    for f in range(2):
                        m = pe.matmul((tr_a, tr_b)[tt % 2][:, k * P:(k + 1) * P], hid[:, tt % 2, f, k * P:(k + 1) * P],
                                      w2_sb[:, par, f, :], start=f == 0, stop=f == 1)
                m.then_inc(down_done, 1)

            def two_experts(i, first=False):
                for par in range(2):
                    e = 2 * i + par
                    pe.wait_ge(w_loaded, 32 * e + 32)
                    pe.wait_ge(w1_lo, e + 1)
                    for tt in range(TT):
                        up(TT * e + tt, par, tt)
                        if tt:
                            down(TT * e + tt - 1, par, tt - 1)
                        elif not (first and par == 0):
                            down(TT * e - 1, 1 - par, TT - 1)

            pe.wait_ge(x_lo, NT // 4)
            two_experts(0, first=True)
            with pe.Fori(1, N_EXP // 2) as i:
                two_experts(i)
            down(N - 1, 1, TT - 1)

        @block.scalar
        def _(act):
            def split_w1(e):
                act.wait_ge(w_loaded, 32 * e + 32)
                wait(act, down_done, TT * (e - 1))
                act.activation(w1_parts[:, e % 2, 0, :], w1_sb[:, e % 2, :], ACT.Copy).then_inc(w1_hi, 1)

            for k in range(NT // 4):
                act.wait_ge(tr_done, k + 1)
                act.activation(xnT_all[:, 512 * k:512 * k + 512], (tr_a, tr_b)[k % 2][:], ACT.Copy).then_inc(tr_free, 1)
            for k in range(NT // 4):
                act.wait_ge(tr_free, k + 1)
                act.activation(xnT[:, 0, 512 * k:512 * k + 512], xnT_all[:, 512 * k:512 * k + 512], ACT.Copy).then_inc(x_hi, 1)
            split_w1(0)
            act.wait_ge(gap_ready, 1)
            act.activation(gate_w[:, 1], gate_w[:, 0], ACT.Exp).then_inc(gate_exp, 1)

            def gelu(n, tt):
                for f in range(2):
                    act.wait_ge(up_done, 2 * n + f + 1)
                    wait(act, down_done, n - 1)
                    act.activation(hid[:, tt % 2, f, :], score[:, f, 0:512], ACT.Gelu).then_inc(gelu_done, 1)

            for e in range(N_EXP):
                for tt in range(TT):
                    gelu(TT * e + tt, tt)
                    if tt == 1 and e + 1 < N_EXP:
                        split_w1(e + 1)


_INS = {
    "x_in": lambda a: a["x"].reshape(B * S, E),
    "ctx_in": lambda a: a["ctx_1024"].reshape(B * C, E),
    "wq_s": lambda a: a["L0_attn_Wq"].T,
    "wk_s": lambda a: a["L0_attn_Wk"].T,
    "wv_s": lambda a: a["L0_attn_Wv"].T,
    "line_in": lambda a: a["L0_attn_bias_table"].T,
    "wq_c": lambda a: a["L0_xattn_Wq"].T.reshape(PAIRS, P, E).transpose(1, 0, 2),
    "wk_c": lambda a: a["L0_xattn_Wkv"][:, :H * D_CROSS].T.reshape(PAIRS, P, E).transpose(1, 0, 2),
    "wv_c": lambda a: a["L0_xattn_Wkv"][:, H * D_CROSS:],
    "wo_c": lambda a: a["L0_xattn_Wout"].reshape(PAIRS, P, E).transpose(1, 0, 2),
    "wg": lambda a: a["L0_ffn_Wg"].T,
    "w1": lambda a: a["L0_ffn_W1"],
    "w2": lambda a: a["L0_ffn_W2"],
}


def kernel(**inputs):
    import numpy as np
    import concourse.bacc as bacc
    from concourse.bass_utils import run_bass_kernel_spmd

    a = {k: np.asarray(x) for k, x in inputs.items()}
    arrays = {k: np.ascontiguousarray(lay(a)) for k, lay in _INS.items()}
    arrays["ln_rows"] = np.stack([a["L0_attn_ln_gamma"], a["L0_attn_ln_beta"]])
    arrays["ln_cols"] = np.stack([a["L0_xattn_ln_m_g"], a["L0_xattn_ln_m_b"], a["L0_xattn_ln_l_g"], a["L0_xattn_ln_l_b"]], axis=1)
    row = np.arange(P)
    low_q, low_k = row % 32 // 16, row % 16 // 8
    arrays["row_masks"] = np.stack([*(row // 32 == j for j in range(4)), low_q, 1 - 2 * low_q, low_k, 1 - 2 * low_k],
                                   axis=1).astype(np.float32)
    nc = bacc.Bacc("TRN2", target_bir_lowering=False, num_devices=1)
    aps = {k: nc.dram_tensor(k, x.shape, mybir.dt.from_np(x.dtype), kind="ExternalInput").ap() for k, x in arrays.items()}
    out = nc.dram_tensor("out", (B * S, E), F32, kind="ExternalOutput").ap()
    build(nc, out=out, **aps)
    r = run_bass_kernel_spmd(nc, [arrays], core_ids=[0])
    return r.results[0]["out"].reshape(B, S, E)
```
